# Optimizing a Trainium2 kernel written in Bass

```python
import numpy as np
import jax
import jax.numpy as jnp

def _softmax(x, axis=-1):
    return jax.nn.softmax(x, axis=axis)

def _gelu(x):
    return jax.nn.gelu(x, approximate=True)

def _silu(x):
    return jax.nn.silu(x)

def _sigmoid(x):
    return jax.nn.sigmoid(x)

def _layernorm(x, axis=-1, eps=1e-05):
    m = jnp.mean(x, axis=axis, keepdims=True)
    v = jnp.var(x, axis=axis, keepdims=True)
    return (x - m) / jnp.sqrt(v + eps)

def _scatter_add(tgt, idx, src, axis=0):
    return tgt.at[idx].add(src)

def _segment_sum(src, seg, n):
    return jax.ops.segment_sum(src, seg, n)
kernel_name = 'mk_hybrid_d2_jaxref_r8_120c12'

def setup_inputs(seed: int=0):
    np.random.seed(seed)
    _w = jnp.asarray

    def _L0_attn_a_setup():
        import jax, jax.numpy as jnp
        import numpy as np
        H = 128
        NH = 16
        L = 4
        B = 4
        N = 256
        EPS_LN = 1e-12

        def gelu(x):
            return jax.nn.gelu(x, approximate=False)

        def layernorm(x, g, b):
            m = jnp.mean(x, axis=-1, keepdims=True)
            v = jnp.mean((x - m) ** 2, axis=-1, keepdims=True)
            return (x - m) / jnp.sqrt(v + EPS_LN) * g + b

        def conv1d_grouped(x, w, b, groups):
            y = jax.lax.conv_general_dilated(x, w, window_strides=(1,), padding=[(2, 2)], dimension_numbers=('NCH', 'OIH', 'NCH'), feature_group_count=groups)
            return y + b[None, :, None]

        def rope(x):
            b, n, c = x.shape
            half = c // 2
            inv = 1.0 / 10000.0 ** (jnp.arange(0, c, 2, dtype=jnp.float32) / c)
            freqs = jnp.arange(n, dtype=jnp.float32)[:, None] * inv[None, :]
            freqs = jnp.repeat(freqs, 2, axis=-1)
            cos, sin = (jnp.cos(freqs), jnp.sin(freqs))
            xp = x.reshape(b, n, half, 2)
            xr = jnp.stack([-xp[..., 1], xp[..., 0]], axis=-1).reshape(b, n, c)
            return x * cos + xr * sin

        def linear_attention(x, Wq, bq, Wk, bk, Wv, bv, g, bb):
            b, n, c = x.shape
            hd = c // NH
            q = gelu(x @ Wq + bq) + 0.21
            k = gelu(x @ Wk + bk) + 0.21
            v = x @ Wv + bv
            q_r = rope(q)
            k_r = rope(k)
            to_h = lambda t: t.reshape(b, n, NH, hd).transpose(0, 2, 1, 3)
            q, k, v, q_r, k_r = map(to_h, (q, k, v, q_r, k_r))
            kmean = jnp.mean(k, axis=2, keepdims=True)
            z = 1.0 / (jnp.einsum('bhnd,bhmd->bhnm', q, kmean) + 1e-06)
            kv = jnp.einsum('bhnd,bhne->bhde', k_r, v) / n
            out = jnp.einsum('bhnd,bhde->bhne', q_r, kv) * z
            out = out.transpose(0, 2, 1, 3).reshape(b, n, c)
            return layernorm(out + x, g, bb)
        key = jax.random.key(seed)
        ks = jax.random.split(key, 10)
        s = 0.02
        r = lambda k, sh: jax.random.normal(k, sh, dtype=jnp.float32) * s
        d = {}
        d['x'] = jax.random.normal(ks[0], (B, N, H), dtype=jnp.float32)
        d['conv1_w'] = r(ks[1], (4 * H, 1, 5))
        d['conv1_b'] = jnp.zeros((4 * H,), jnp.float32)
        d['conv2_w'] = r(ks[2], (H, 4, 5))
        d['conv2_b'] = jnp.zeros((H,), jnp.float32)
        d['ln0_g'] = jnp.ones((H,), jnp.float32)
        d['ln0_b'] = jnp.zeros((H,), jnp.float32)
        d['Wq'] = r(ks[3], (L, H, H))
        d['bq'] = jnp.zeros((L, H), jnp.float32)
        d['Wk'] = r(ks[4], (L, H, H))
        d['bk'] = jnp.zeros((L, H), jnp.float32)
        d['Wv'] = r(ks[5], (L, H, H))
        d['bv'] = jnp.zeros((L, H), jnp.float32)
        d['lnA_g'] = jnp.ones((L, H), jnp.float32)
        d['lnA_b'] = jnp.zeros((L, H), jnp.float32)
        d['W1'] = r(ks[6], (H, 4 * H))
        d['b1'] = jnp.zeros((4 * H,), jnp.float32)
        d['W2'] = r(ks[7], (4 * H, H))
        d['b2'] = jnp.zeros((H,), jnp.float32)
        d['ln2_g'] = jnp.ones((H,), jnp.float32)
        d['ln2_b'] = jnp.zeros((H,), jnp.float32)
        return d
    _L0_attn_a_in = _L0_attn_a_setup()

    def _L0_attn_b_setup():
        import jax, jax.numpy as jnp
        import numpy as np
        H = 16
        RMS_EPS = 1.1920928955078125e-07
        NORM_EPS = 1e-12

        def _rms_norm(t):
            ms = jnp.mean(t * t, axis=-1, keepdims=True)
            return t * jax.lax.rsqrt(ms + RMS_EPS)
        key = jax.random.key(seed)
        k1, k2, k3 = jax.random.split(key, 3)
        B, N, C = (2, 256, 128)
        x = jax.random.normal(k1, (B, N, C), dtype=jnp.float32)
        w_qkv = jax.random.normal(k2, (3 * C, C), dtype=jnp.float32) * C ** (-0.5)
        w_proj = jax.random.normal(k3, (C, C), dtype=jnp.float32) * C ** (-0.5)
        return {'x': x, 'w_qkv': w_qkv, 'w_proj': w_proj}
    _L0_attn_b_in = _L0_attn_b_setup()

    def _L0_ffn_setup():
        import jax, jax.numpy as jnp
        import numpy as np
        EMBED_DIM = 128
        NUM_EXPERTS = 8
        B, S = (2, 256)
        key = jax.random.key(seed)
        ks = jax.random.split(key, 5)
        scale = 1.0 / np.sqrt(EMBED_DIM)
        x = jax.random.normal(ks[0], (B, S, EMBED_DIM), dtype=jnp.float32)
        router_w = jax.random.normal(ks[1], (NUM_EXPERTS, EMBED_DIM), dtype=jnp.float32) * scale
        router_b = jnp.zeros((NUM_EXPERTS,), dtype=jnp.float32)
        expert_w = jax.random.normal(ks[2], (NUM_EXPERTS, EMBED_DIM, EMBED_DIM), dtype=jnp.float32) * scale
        expert_b = jnp.zeros((NUM_EXPERTS, EMBED_DIM), dtype=jnp.float32)
        return {'x': x, 'router_w': router_w, 'router_b': router_b, 'expert_w': expert_w, 'expert_b': expert_b}
    _L0_ffn_in = _L0_ffn_setup()

    def _L1_attn_a_setup():
        import jax, jax.numpy as jnp
        import numpy as np
        EMBED_DIM = 128
        NUM_HEADS = 16
        key = jax.random.key(seed)
        k_x, k_wqkv, k_bqkv, k_wo, k_bo = jax.random.split(key, 5)
        C = EMBED_DIM
        s = 1.0 / np.sqrt(C)
        return {'x': jax.random.normal(k_x, (64, 32, C), dtype=jnp.float32), 'Wqkv': jax.random.uniform(k_wqkv, (C, 3 * C), jnp.float32, -s, s), 'bqkv': jax.random.uniform(k_bqkv, (3 * C,), jnp.float32, -s, s), 'Wo': jax.random.uniform(k_wo, (C, C), jnp.float32, -s, s), 'bo': jax.random.uniform(k_bo, (C,), jnp.float32, -s, s)}
    _L1_attn_a_in = _L1_attn_a_setup()

    def _L1_attn_b_setup():
        import jax, jax.numpy as jnp
        import numpy as np
        D_MODEL = 128
        N_HEADS = 16
        D_HEAD = D_MODEL // N_HEADS

        def _rmsnorm(x, w):
            xf = x.astype(jnp.float32)
            rms = jnp.mean(xf * xf, axis=-1, keepdims=True)
            return (xf / jnp.sqrt(rms + 1e-06) * w.astype(jnp.float32)).astype(x.dtype)
        key = jax.random.key(seed)
        ks = jax.random.split(key, 7)
        x = jax.random.normal(ks[0], (1, 512, D_MODEL), dtype=jnp.float32)
        Wqkv = jax.random.normal(ks[1], (3 * D_MODEL, D_MODEL), dtype=jnp.float32) * (1.0 / np.sqrt(D_MODEL))
        bqkv = jax.random.normal(ks[2], (3 * D_MODEL,), dtype=jnp.float32) * 0.01
        Wo = jax.random.normal(ks[3], (D_MODEL, D_MODEL), dtype=jnp.float32) * (1.0 / np.sqrt(D_MODEL))
        bo = jax.random.normal(ks[4], (D_MODEL,), dtype=jnp.float32) * 0.01
        wq = jnp.ones((D_HEAD,), dtype=jnp.float32)
        wk = jnp.ones((D_HEAD,), dtype=jnp.float32)
        return {'x': x, 'Wqkv': Wqkv, 'bqkv': bqkv, 'Wo': Wo, 'bo': bo, 'wq': wq, 'wk': wk}
    _L1_attn_b_in = _L1_attn_b_setup()

    def _L1_ffn_setup():
        import jax, jax.numpy as jnp
        import numpy as np
        B, S, H, F, E, K = (4, 512, 128, 512, 8, 2)
        LN_EPS = 1e-05
        key = jax.random.key(seed)
        kx, kr, k1, k2 = jax.random.split(key, 4)
        x = jax.random.normal(kx, (B, S, H), dtype=jnp.float32)
        gamma = jnp.ones((H,), jnp.float32)
        beta = jnp.zeros((H,), jnp.float32)
        Wr = jax.random.normal(kr, (H, E), jnp.float32) * 0.02
        br = jnp.zeros((E,), jnp.float32)
        W1 = jax.random.normal(k1, (E, H, F), jnp.float32) * (1.0 / np.sqrt(H))
        b1 = jnp.zeros((E, F), jnp.float32)
        W2 = jax.random.normal(k2, (E, F, H), jnp.float32) * (1.0 / np.sqrt(F))
        b2 = jnp.zeros((E, H), jnp.float32)
        return {'x': x, 'gamma': gamma, 'beta': beta, 'Wr': Wr, 'br': br, 'W1': W1, 'b1': b1, 'W2': W2, 'b2': b2}
    _L1_ffn_in = _L1_ffn_setup()
    _d = {'L0_attn_a_x': _L0_attn_a_in['x'], 'L0_attn_a_conv1_w': _L0_attn_a_in['conv1_w'], 'L0_attn_a_conv1_b': _L0_attn_a_in['conv1_b'], 'L0_attn_a_conv2_w': _L0_attn_a_in['conv2_w'], 'L0_attn_a_conv2_b': _L0_attn_a_in['conv2_b'], 'L0_attn_a_ln0_g': _L0_attn_a_in['ln0_g'], 'L0_attn_a_ln0_b': _L0_attn_a_in['ln0_b'], 'L0_attn_a_Wq': _L0_attn_a_in['Wq'], 'L0_attn_a_bq': _L0_attn_a_in['bq'], 'L0_attn_a_Wk': _L0_attn_a_in['Wk'], 'L0_attn_a_bk': _L0_attn_a_in['bk'], 'L0_attn_a_Wv': _L0_attn_a_in['Wv'], 'L0_attn_a_bv': _L0_attn_a_in['bv'], 'L0_attn_a_lnA_g': _L0_attn_a_in['lnA_g'], 'L0_attn_a_lnA_b': _L0_attn_a_in['lnA_b'], 'L0_attn_a_W1': _L0_attn_a_in['W1'], 'L0_attn_a_b1': _L0_attn_a_in['b1'], 'L0_attn_a_W2': _L0_attn_a_in['W2'], 'L0_attn_a_b2': _L0_attn_a_in['b2'], 'L0_attn_a_ln2_g': _L0_attn_a_in['ln2_g'], 'L0_attn_a_ln2_b': _L0_attn_a_in['ln2_b'], 'L0_attn_b_w_qkv': _L0_attn_b_in['w_qkv'], 'L0_attn_b_w_proj': _L0_attn_b_in['w_proj'], 'L0_ffn_router_w': _L0_ffn_in['router_w'], 'L0_ffn_router_b': _L0_ffn_in['router_b'], 'L0_ffn_expert_w': _L0_ffn_in['expert_w'], 'L0_ffn_expert_b': _L0_ffn_in['expert_b'], 'L1_attn_a_Wqkv': _L1_attn_a_in['Wqkv'], 'L1_attn_a_bqkv': _L1_attn_a_in['bqkv'], 'L1_attn_a_Wo': _L1_attn_a_in['Wo'], 'L1_attn_a_bo': _L1_attn_a_in['bo'], 'L1_attn_b_Wqkv': _L1_attn_b_in['Wqkv'], 'L1_attn_b_bqkv': _L1_attn_b_in['bqkv'], 'L1_attn_b_Wo': _L1_attn_b_in['Wo'], 'L1_attn_b_bo': _L1_attn_b_in['bo'], 'L1_attn_b_wq': _L1_attn_b_in['wq'], 'L1_attn_b_wk': _L1_attn_b_in['wk'], 'L1_ffn_gamma': _L1_ffn_in['gamma'], 'L1_ffn_beta': _L1_ffn_in['beta'], 'L1_ffn_Wr': _L1_ffn_in['Wr'], 'L1_ffn_br': _L1_ffn_in['br'], 'L1_ffn_W1': _L1_ffn_in['W1'], 'L1_ffn_b1': _L1_ffn_in['b1'], 'L1_ffn_W2': _L1_ffn_in['W2'], 'L1_ffn_b2': _L1_ffn_in['b2']}
    _x0 = _d['L0_attn_a_x']
    _d['L0_attn_a_x'] = jax.random.normal(jax.random.fold_in(jax.random.key(seed), 1), (16, 256, 128), dtype=_x0.dtype)
    del _x0
    return _d

def reference(L0_attn_a_x, L0_attn_a_conv1_w, L0_attn_a_conv1_b, L0_attn_a_conv2_w, L0_attn_a_conv2_b, L0_attn_a_ln0_g, L0_attn_a_ln0_b, L0_attn_a_Wq, L0_attn_a_bq, L0_attn_a_Wk, L0_attn_a_bk, L0_attn_a_Wv, L0_attn_a_bv, L0_attn_a_lnA_g, L0_attn_a_lnA_b, L0_attn_a_W1, L0_attn_a_b1, L0_attn_a_W2, L0_attn_a_b2, L0_attn_a_ln2_g, L0_attn_a_ln2_b, L0_attn_b_w_qkv, L0_attn_b_w_proj, L0_ffn_router_w, L0_ffn_router_b, L0_ffn_expert_w, L0_ffn_expert_b, L1_attn_a_Wqkv, L1_attn_a_bqkv, L1_attn_a_Wo, L1_attn_a_bo, L1_attn_b_Wqkv, L1_attn_b_bqkv, L1_attn_b_Wo, L1_attn_b_bo, L1_attn_b_wq, L1_attn_b_wk, L1_ffn_gamma, L1_ffn_beta, L1_ffn_Wr, L1_ffn_br, L1_ffn_W1, L1_ffn_b1, L1_ffn_W2, L1_ffn_b2):

    def _L0_attn_a_ref(x, conv1_w, conv1_b, conv2_w, conv2_b, ln0_g, ln0_b, Wq, bq, Wk, bk, Wv, bv, lnA_g, lnA_b, W1, b1, W2, b2, ln2_g, ln2_b):
        import jax, jax.numpy as jnp
        import numpy as np
        H = 128
        NH = 16
        L = 4
        B = 4
        N = 256
        EPS_LN = 1e-12

        def gelu(x):
            return jax.nn.gelu(x, approximate=False)

        def layernorm(x, g, b):
            m = jnp.mean(x, axis=-1, keepdims=True)
            v = jnp.mean((x - m) ** 2, axis=-1, keepdims=True)
            return (x - m) / jnp.sqrt(v + EPS_LN) * g + b

        def conv1d_grouped(x, w, b, groups):
            y = jax.lax.conv_general_dilated(x, w, window_strides=(1,), padding=[(2, 2)], dimension_numbers=('NCH', 'OIH', 'NCH'), feature_group_count=groups)
            return y + b[None, :, None]

        def rope(x):
            b, n, c = x.shape
            half = c // 2
            inv = 1.0 / 10000.0 ** (jnp.arange(0, c, 2, dtype=jnp.float32) / c)
            freqs = jnp.arange(n, dtype=jnp.float32)[:, None] * inv[None, :]
            freqs = jnp.repeat(freqs, 2, axis=-1)
            cos, sin = (jnp.cos(freqs), jnp.sin(freqs))
            xp = x.reshape(b, n, half, 2)
            xr = jnp.stack([-xp[..., 1], xp[..., 0]], axis=-1).reshape(b, n, c)
            return x * cos + xr * sin

        def linear_attention(x, Wq, bq, Wk, bk, Wv, bv, g, bb):
            b, n, c = x.shape
            hd = c // NH
            q = gelu(x @ Wq + bq) + 0.21
            k = gelu(x @ Wk + bk) + 0.21
            v = x @ Wv + bv
            q_r = rope(q)
            k_r = rope(k)
            to_h = lambda t: t.reshape(b, n, NH, hd).transpose(0, 2, 1, 3)
            q, k, v, q_r, k_r = map(to_h, (q, k, v, q_r, k_r))
            kmean = jnp.mean(k, axis=2, keepdims=True)
            z = 1.0 / (jnp.einsum('bhnd,bhmd->bhnm', q, kmean) + 1e-06)
            kv = jnp.einsum('bhnd,bhne->bhde', k_r, v) / n
            out = jnp.einsum('bhnd,bhde->bhne', q_r, kv) * z
            out = out.transpose(0, 2, 1, 3).reshape(b, n, c)
            return layernorm(out + x, g, bb)
        b, n, c = x.shape
        h = x.transpose(0, 2, 1)
        h = conv1d_grouped(h, conv1_w, conv1_b, c)
        h = gelu(h)
        h = conv1d_grouped(h, conv2_w, conv2_b, c)
        h = h.transpose(0, 2, 1)
        h = layernorm(h + x, ln0_g, ln0_b)
        for i in range(Wq.shape[0]):
            h = linear_attention(h, Wq[i], bq[i], Wk[i], bk[i], Wv[i], bv[i], lnA_g[i], lnA_b[i])
        f = gelu(h @ W1 + b1) @ W2 + b2
        return layernorm(f + h, ln2_g, ln2_b)

    def _L0_attn_b_ref(x, w_qkv, w_proj):
        import jax, jax.numpy as jnp
        import numpy as np
        H = 16
        RMS_EPS = 1.1920928955078125e-07
        NORM_EPS = 1e-12

        def _rms_norm(t):
            ms = jnp.mean(t * t, axis=-1, keepdims=True)
            return t * jax.lax.rsqrt(ms + RMS_EPS)
        B, N, C = x.shape
        D = C // H
        scale = D ** (-0.5)
        qkv = x @ w_qkv.T
        qkv = qkv.reshape(B, N, 3, H, D)
        q = qkv[:, :, 0].transpose(0, 2, 1, 3)
        k = qkv[:, :, 1].transpose(0, 2, 1, 3)
        v = qkv[:, :, 2].transpose(0, 2, 1, 3)
        q = _rms_norm(q)
        k = _rms_norm(k)
        attn = jnp.einsum('bhnd,bhmd->bhnm', q, k) * scale
        attn = jax.nn.softmax(attn, axis=-1)
        y = jnp.einsum('bhnm,bhmd->bhnd', attn, v)
        vnorm = jnp.linalg.norm(v, axis=-1, keepdims=True)
        Vn = v / jnp.maximum(vnorm, NORM_EPS)
        y = y - jnp.sum(y * Vn, axis=-1, keepdims=True) * Vn
        out = y.transpose(0, 2, 1, 3).reshape(B, N, C)
        return out @ w_proj.T

    def _L0_ffn_ref(x, router_w, router_b, expert_w, expert_b):
        import jax, jax.numpy as jnp
        import numpy as np
        EMBED_DIM = 128
        NUM_EXPERTS = 8
        B, S = (2, 256)
        Bb, Ss, D = x.shape
        xt = x.reshape(-1, D)
        logits = xt @ router_w.T + router_b
        probs = jax.nn.softmax(logits, axis=-1)
        idx = jnp.argmax(logits, axis=-1)
        w = jnp.take_along_axis(probs, idx[:, None], axis=1)[:, 0]
        y_all = jnp.einsum('td,efd->tef', xt, expert_w) + expert_b
        y = jnp.take_along_axis(y_all, idx[:, None, None], axis=1)[:, 0]
        out = (y * w[:, None]).reshape(Bb, Ss, D)
        return out

    def _L1_attn_a_ref(x, Wqkv, bqkv, Wo, bo):
        import jax, jax.numpy as jnp
        import numpy as np
        EMBED_DIM = 128
        NUM_HEADS = 16
        B, T, C = x.shape
        H = NUM_HEADS
        D = C // H
        qkv = x @ Wqkv + bqkv
        q, k, v = jnp.split(qkv, 3, axis=-1)
        q = q.reshape(B, T, H, D).transpose(0, 2, 1, 3)
        k = k.reshape(B, T, H, D).transpose(0, 2, 1, 3)
        v = v.reshape(B, T, H, D).transpose(0, 2, 1, 3)
        scale = D ** (-0.5)
        scores = jnp.einsum('bhtd,bhsd->bhts', q, k) * scale
        causal = jnp.tril(jnp.ones((T, T), dtype=bool))
        scores = jnp.where(causal[None, None], scores, -jnp.inf)
        weights = jax.nn.softmax(scores, axis=-1)
        y = jnp.einsum('bhts,bhsd->bhtd', weights, v)
        y = y.transpose(0, 2, 1, 3).reshape(B, T, C)
        return y @ Wo + bo

    def _L1_attn_b_ref(x, Wqkv, bqkv, Wo, bo, wq, wk):
        import jax, jax.numpy as jnp
        import numpy as np
        D_MODEL = 128
        N_HEADS = 16
        D_HEAD = D_MODEL // N_HEADS

        def _rmsnorm(x, w):
            xf = x.astype(jnp.float32)
            rms = jnp.mean(xf * xf, axis=-1, keepdims=True)
            return (xf / jnp.sqrt(rms + 1e-06) * w.astype(jnp.float32)).astype(x.dtype)
        b, s, d = x.shape
        qkv = x @ Wqkv.T + bqkv
        q, k, v = jnp.split(qkv, 3, axis=-1)
        q = q.reshape(b, s, N_HEADS, D_HEAD)
        k = k.reshape(b, s, N_HEADS, D_HEAD)
        v = v.reshape(b, s, N_HEADS, D_HEAD)
        q = _rmsnorm(q, wq)
        k = _rmsnorm(k, wk)
        qf = q.astype(jnp.float32)
        kf = k.astype(jnp.float32)
        vf = v.astype(jnp.float32)
        attn = jnp.einsum('bqhd,bkhd->bhqk', qf, kf)
        attn = jax.nn.softmax(attn, axis=-1)
        z = jnp.einsum('bhqk,bkhd->bqhd', attn, vf).astype(x.dtype)
        z = z.reshape(b, s, d)
        return z @ Wo.T + bo

    def _L1_ffn_ref(x, gamma, beta, Wr, br, W1, b1, W2, b2):
        import jax, jax.numpy as jnp
        import numpy as np
        B, S, H, F, E, K = (4, 512, 128, 512, 8, 2)
        LN_EPS = 1e-05
        residual = x
        mu = jnp.mean(x, axis=-1, keepdims=True)
        var = jnp.var(x, axis=-1, keepdims=True)
        xn = (x - mu) * jax.lax.rsqrt(var + LN_EPS) * gamma + beta
        probs = jax.nn.softmax(xn @ Wr + br, axis=-1)
        scores, idx = jax.lax.top_k(probs, K)

        def expert_fn(w):
            W1_e, b1_e, W2_e, b2_e = w
            return jax.nn.relu(xn @ W1_e + b1_e) @ W2_e + b2_e
        full = jax.lax.map(expert_fn, (W1, b1, W2, b2))
        full = jnp.moveaxis(full, 0, 2)
        c = jnp.einsum('ef,efh->eh', jax.nn.relu(b1), W2) + b2
        c_total = c.sum(axis=0)
        sel_full = jnp.take_along_axis(full, idx[..., None], axis=2)
        c_sel = c[idx]
        output = jnp.sum(scores[..., None] * (sel_full - c_sel + c_total), axis=2)
        return residual + output
    x = L0_attn_a_x
    x = x + _L0_attn_a_ref(_layernorm(x, axis=-1), L0_attn_a_conv1_w, L0_attn_a_conv1_b, L0_attn_a_conv2_w, L0_attn_a_conv2_b, L0_attn_a_ln0_g, L0_attn_a_ln0_b, L0_attn_a_Wq, L0_attn_a_bq, L0_attn_a_Wk, L0_attn_a_bk, L0_attn_a_Wv, L0_attn_a_bv, L0_attn_a_lnA_g, L0_attn_a_lnA_b, L0_attn_a_W1, L0_attn_a_b1, L0_attn_a_W2, L0_attn_a_b2, L0_attn_a_ln2_g, L0_attn_a_ln2_b)
    x = x + _L0_ffn_ref(_layernorm(x, axis=-1), L0_ffn_router_w, L0_ffn_router_b, L0_ffn_expert_w, L0_ffn_expert_b)
    x = x + _L0_attn_b_ref(_layernorm(x, axis=-1), L0_attn_b_w_qkv, L0_attn_b_w_proj)
    x = x + _L0_ffn_ref(_layernorm(x, axis=-1), L0_ffn_router_w, L0_ffn_router_b, L0_ffn_expert_w, L0_ffn_expert_b)
    x = x + _L1_attn_a_ref(_layernorm(x, axis=-1), L1_attn_a_Wqkv, L1_attn_a_bqkv, L1_attn_a_Wo, L1_attn_a_bo)
    x = x + _L1_ffn_ref(_layernorm(x, axis=-1), L1_ffn_gamma, L1_ffn_beta, L1_ffn_Wr, L1_ffn_br, L1_ffn_W1, L1_ffn_b1, L1_ffn_W2, L1_ffn_b2)
    x = x + _L1_attn_b_ref(_layernorm(x, axis=-1), L1_attn_b_Wqkv, L1_attn_b_bqkv, L1_attn_b_Wo, L1_attn_b_bo, L1_attn_b_wq, L1_attn_b_wk)
    x = x + _L1_ffn_ref(_layernorm(x, axis=-1), L1_ffn_gamma, L1_ffn_beta, L1_ffn_Wr, L1_ffn_br, L1_ffn_W1, L1_ffn_b1, L1_ffn_W2, L1_ffn_b2)
    return x

_drawn_inputs = setup_inputs


def setup_inputs(seed=0):
    import zlib

    import numpy as np

    out = dict(_drawn_inputs(seed))
    spreads = {'L0_attn_a_conv1_b': (0.0, 0.683),
     'L0_attn_a_conv2_b': (0.0, 0.1),
     'L0_attn_a_ln0_g': (1.0, 0.2),
     'L0_attn_a_ln0_b': (0.0, 0.1),
     'L0_attn_a_bq': (0.0, 0.8),
     'L0_attn_a_bk': (0.0, 0.661),
     'L0_attn_a_bv': (0.0, 0.1),
     'L0_attn_a_lnA_g': (1.0, 0.2),
     'L0_attn_a_lnA_b': (0.0, 0.1),
     'L0_attn_a_b1': (0.0, 0.1),
     'L0_attn_a_b2': (0.0, 0.1),
     'L0_attn_a_ln2_g': (1.0, 0.2),
     'L0_attn_a_ln2_b': (0.0, 0.1),
     'L0_ffn_router_b': (0.0, 0.1),
     'L0_ffn_expert_b': (0.0, 0.1),
     'L1_attn_b_wq': (1.0, 0.6),
     'L1_attn_b_wk': (1.0, 0.2),
     'L1_ffn_gamma': (1.0, 0.2),
     'L1_ffn_beta': (0.0, 0.414),
     'L1_ffn_br': (0.0, 0.1),
     'L1_ffn_b1': (0.0, 0.1),
     'L1_ffn_b2': (0.0, 0.1)}
    factors = {'L0_attn_a_conv1_w': 8.0,
     'L0_attn_a_conv2_w': 7.616,
     'L0_attn_a_Wq': 3.953,
     'L0_attn_a_Wk': 3.972,
     'L1_attn_a_bqkv': 3.247,
     'L1_attn_b_bqkv': 8.0,
     'L1_attn_b_bo': 8.0}
    for name, (base, spread) in spreads.items():
        noise = np.random.default_rng([zlib.crc32(name.encode()), seed]).standard_normal(out[name].shape)
        drawn = base * np.exp(spread * noise) if base else spread * noise
        out[name] = jnp.asarray(drawn.astype(out[name].dtype))
    for name, factor in factors.items():
        out[name] = (out[name] * factor).astype(out[name].dtype)
    return out
```

```python
from contextlib import ExitStack

import numpy as np

import concourse.bass as bass
from concourse import mybir

F32 = mybir.dt.float32
BF16 = mybir.dt.bfloat16
ALU = mybir.AluOpType
ACT = mybir.ActivationFunctionType
AX = mybir.AxisListType

P = 128
B = 16
N = 256
NT = N // P
C = 128
NH = 16
HD = C // NH
L = 4
TAPS = 5
PAD = TAPS // 2
MULT = 4
FF = 512
FJ = FF // P
E = 8
GELU_SHIFT = 0.21
LN_EPS = 1e-5
LN_EPS_A = 1e-12




def semaphores(nc, ctx, prefix, names):
    sems = {n: nc.alloc_semaphore(f"{prefix}_{n}") for n in names.split()}

    def clear():
        nc.clear_and_free_semaphores(list(sems.values()))
        nc.all_engine_barrier()

    ctx.callback(clear)
    return sems


def finished(eng, sem, n):
    if isinstance(n, int) and n < 0:
        return
    eng.wait_ge(sem, n + 1)


def held(eng, sem, n, tick):
    if isinstance(n, int) and n < 0:
        return
    finished(eng, sem, n)
    eng.sem_inc(tick, 1)


def turn(nc, out, in_, ident):
    return nc.tensor.matmul(out, lhsT=in_, rhs=ident, start=True, stop=True, is_transpose=True)


def spread(ap, n):
    return ap.unsqueeze(len(ap.shape)).broadcast_to([*ap.shape, n])


def column(t, l):
    return t[:, :].rearrange("p (l o) -> p l o", o=1)[:, l, :]


def conv_phase(nc, g):
    U = 2
    with ExitStack() as ctx:
        s = semaphores(nc, ctx, "cv", "x w later tick diag1 zero stats mv vareps rstd r rt rT c1 gl tap yt stats2 mv2 "
                                      "vareps2 rstd2 un unt h")

        def sb(name, shape, dt=F32):
            return ctx.enter_context(nc.sbuf_tensor("cv_" + name, shape, dt))

        st = sb("st", [P, U, NT, 6])
        mv = sb("mv", [P, U, NT, 2])
        ve = sb("ve", [P, U, NT])
        rstd = sb("rstd", [P, U, NT])
        r = sb("r", [P, U, NT, C])
        rT = sb("rT", [P, U, N + 2 * PAD])
        gl = sb("gl", [P, U, MULT, N + 2 * PAD])
        y = sb("y", [P, U, N])
        diag = sb("diag", [P, MULT * TAPS, C])
        half = sb("half", [P, NT])
        eps = sb("eps", [P, 2, NT])
        X, HT, ident, PS = g["X"], g["HT"], g["ident"], g["PS"]
        block = ctx.enter_context(nc.Block())
        bank_t = [PS[:, 3 * u, :] for u in range(U)]
        bank_c = [PS[:, 3 * u + 1:3 * u + 3, :].rearrange("p b (j n) -> p (b j) n", n=N) for u in range(U)]
        steps = B // U

        @block.sync
        def _(sp):
            for dst, src in g["first_loads"]:
                sp.dma_start(dst, src).then_inc(s["w"], 16)
            xd = g["x_dram"].rearrange("b (h p) c -> p b h c", p=P)
            for q in range(4):
                sp.dma_start(X[:, 4 * q:4 * q + 4], xd[:, 4 * q:4 * q + 4]).then_inc(s["x"], 16)
            for dst, src in g["loads"]:
                sp.dma_start(dst, src).then_inc(s["later"], 16)
            sp.wait_ge(s["later"], 16 * len(g["loads"]))

        @block.gpsimd
        def _(pool):
            pool.memset(half[:, :], -0.5).then_inc(s["zero"], 1)
            pool.memset(eps[:, 0, :], LN_EPS).then_inc(s["zero"], 1)
            pool.memset(eps[:, 1, :], LN_EPS_A).then_inc(s["zero"], 1)
            pool.memset(rT[:, :, :], 0.0).then_inc(s["zero"], 1)
            pool.memset(gl[:, :, :, :], 0.0).then_inc(s["zero"], 1)
            pool.wait_ge(s["zero"], 5)
            with pool.Fori(0, steps) as i:
                for a, b, c, m in (("mv", "vareps", "rstd", 0), ("mv2", "vareps2", "rstd2", 1)):
                    for u in range(U):
                        finished(pool, s[a], i * U + u)
                        pool.tensor_tensor(ve[:, u, :], mv[:, u, :, 1], eps[:, m, :], ALU.add).then_inc(s[b], 1)
                    for u in range(U):
                        finished(pool, s[b], i * U + u)
                        pool.tensor_tensor(rstd[:, u, :], ve[:, u, :], half[:, :], ALU.pow).then_inc(s[c], 1)

        @block.vector
        def _(v):
            v.wait_ge(s["w"], 16 * len(g["first_loads"]))
            for t in range(MULT * TAPS):
                d = v.tensor_scalar(diag[:, t, :], ident[:, :], g["conv1_w"][:, t:t + 1], None, ALU.mult)
            d.then_inc(s["diag1"], 1)
            v.wait_ge(s["x"], 64)
            v.wait_ge(s["zero"], 5)

            def norm(i, src, names, dst):
                stats, mvs, rs, done = names
                for u in range(U):
                    for h in range(NT):
                        last = v.bn_stats(st[:, u, h, :], src(u, h))
                    last.then_inc(s[stats], 1)
                for u in range(U):
                    held(v, s[stats], i * U + u, s["tick"])
                    for h in range(NT):
                        last = v.bn_aggr(mv[:, u, h, :], st[:, u, h, :])
                    last.then_inc(s[mvs], 1)
                for u in range(U):
                    finished(v, s[rs], i * U + u)
                    for h in range(NT):
                        last = v.tensor_scalar(r[:, u, h, :], src(u, h), mv[:, u, h, 0:1], rstd[:, u, h:h + 1],
                                               ALU.subtract, ALU.mult)
                    last.then_inc(s[done], 1)

            xv = X[:, :, :, :].rearrange("p (i u) h c -> p i u h c", u=U)
            with v.Fori(0, steps) as i:
                for u in range(U):
                    v.wait_ge(s["h"], i * U + u + 1)
                norm(i, lambda u, h: xv[:, i, u, h, :], ("stats", "mv", "rstd", "r"), r)
                first = True
                taps = MULT * TAPS
                for t in range(taps + 1):
                    for u in range(U):
                        if t:
                            v.wait_ge(s["tap"], i * (U * (taps + 1)) + (t - 1) * U + u + 1)
                        else:
                            finished(v, s["gl"], i * U + u)
                        if t < taps:
                            src = gl[:, u, t // TAPS, t % TAPS:t % TAPS + N]
                            w = g["conv2_w"][:, t:t + 1]
                        if t == 0:
                            op = v.tensor_scalar(y[:, u, :], src, w, g["conv2_b"][:, 0:1], ALU.mult, ALU.add)
                        elif t < taps:
                            op = v.scalar_tensor_tensor(out=y[:, u, :], in0=src, scalar=w, in1=y[:, u, :],
                                                        op0=ALU.mult, op1=ALU.add)
                        else:
                            op = v.tensor_tensor(y[:, u, :], y[:, u, :], rT[:, u, PAD:PAD + N], ALU.add)
                        op.then_inc(s["tap"], 1)
                for u in range(U):
                    finished(v, s["yt"], i * U + u)
                norm(i, lambda u, h: bank_t[u][:, h * C:(h + 1) * C], ("stats2", "mv2", "rstd2", "un"), r)

        @block.tensor
        def _(pe):
            pe.wait_ge(s["w"], 16 * len(g["first_loads"]))
            pe.wait_ge(s["diag1"], 1)
            taps = MULT * TAPS
            with pe.Fori(0, steps) as i:
                for u in range(U):
                    finished(pe, s["r"], i * U + u)
                    for h in range(NT):
                        last = turn(nc, bank_t[u][:, h * P:(h + 1) * P], r[:, u, h, :], ident[:, :])
                    last.then_inc(s["rt"], 1)
                for u in range(U):
                    finished(pe, s["rT"], i * U + u)
                    for j in range(MULT):
                        for k in range(TAPS):
                            last = pe.matmul(bank_c[u][:, j, :], lhsT=diag[:, j * TAPS + k, :],
                                             rhs=rT[:, u, k:k + N], start=(k == 0), stop=(k == TAPS - 1))
                    last.then_inc(s["c1"], 1)
                for u in range(U):
                    pe.wait_ge(s["tap"], i * (U * (taps + 1)) + taps * U + u + 1)
                    for h in range(NT):
                        last = turn(nc, bank_t[u][:, h * P:(h + 1) * P], y[:, u, h * P:(h + 1) * P], ident[:, :])
                    last.then_inc(s["yt"], 1)
                for u in range(U):
                    finished(pe, s["un"], i * U + u)
                    for h in range(NT):
                        last = turn(nc, bank_t[u][:, h * P:(h + 1) * P], r[:, u, h, :], ident[:, :])
                    last.then_inc(s["unt"], 1)

        @block.scalar
        def _(act):
            act.preload_act_table_set("gelu_and_others")
            act.sem_inc(s["h"], U)
            act.wait_ge(s["w"], 16 * len(g["first_loads"]))
            act.wait_ge(s["zero"], 5)
            hv = HT[:, :, :].rearrange("p (i u) n -> p i u n", u=U)
            with act.Fori(0, steps) as i:
                for u in range(U):
                    finished(act, s["rt"], i * U + u)
                    act.activation(rT[:, u, PAD:PAD + N], bank_t[u][:, 0:N], ACT.Copy).then_inc(s["rT"], 1)
                for u in range(U):
                    finished(act, s["c1"], i * U + u)
                    for j in range(MULT):
                        last = act.activation(gl[:, u, j, PAD:PAD + N], bank_c[u][:, j, :], ACT.Gelu,
                                              bias=g["conv1_b"][:, j:j + 1])
                    last.then_inc(s["gl"], 1)
                for u in range(U):
                    finished(act, s["unt"], i * U + u)
                    act.activation(hv[:, i, u, :], bank_t[u][:, 0:N], ACT.Identity, bias=g["ln0_b"][:, 0:1],
                                   scale=g["ln0_g"][:, 0:1]).then_inc(s["h"], 1)


def linear_phase(nc, g):
    U = 4
    steps = B // U
    with ExitStack() as ctx:
        s = semaphores(nc, ctx, "la", "zero tick atick wq h0 proj kv q qs k kc ks kr ksum kvm kmean km kvbd den kv2 kv2s dens "
                                      "z qz qc qsn out y yt stats mv vareps rstd un unt h saved")

        def sb(name, shape, dt=F32):
            return ctx.enter_context(nc.sbuf_tensor("la_" + name, shape, dt))

        half = sb("half", [P, NT])
        eps = sb("eps", [P, NT])
        ones = sb("ones", [P, 1])
        shift = sb("shift", [P, N])
        wq = sb("wq", [P, C])
        h = sb("h", [P, U, N])
        q = sb("q", [P, U, N])
        kv = sb("kv", [P, U, NT, 2 * C])
        k = sb("k", [P, U, NT, C])
        kc = sb("kc", [P, U, NT, C])
        ks = sb("ks", [P, U, NT, C])
        kmean = sb("kmean", [P, U, 1])
        km = sb("km", [P, U, C])
        kvbd = sb("kvbd", [P, U, C])
        kv2 = sb("kv2", [P, U, C])
        z = sb("z", [P, U, N])
        qc = sb("qc", [P, U, N])
        qs = sb("qs", [P, U, N])
        st = sb("st", [P, U, NT, 6])
        mv = sb("mv", [P, U, NT, 2])
        ve = sb("ve", [P, U, NT])
        rstd = sb("rstd", [P, U, NT])
        HT, ident, PS = g["HT"], g["ident"], g["PS"]
        hv = HT[:, :, :].rearrange("p (i u) n -> p i u n", u=U)
        A = [PS[:, 2 * u, :] for u in range(U)]
        D = [PS[:, 2 * u + 1, :] for u in range(U)]
        block = ctx.enter_context(nc.Block())

        def rounds(eng, body):
            with eng.Fori(0, steps) as i:
                with eng.Fori(0, L) as l:
                    body(i, l, i * L + l)

        @block.sync
        def _(sp):
            pass

        @block.gpsimd
        def _(pool):
            pool.memset(half[:, :], -0.5).then_inc(s["zero"], 1)
            pool.memset(eps[:, :], LN_EPS_A).then_inc(s["zero"], 1)
            pool.memset(ones[:, :], 1.0).then_inc(s["zero"], 1)
            pool.wait_ge(s["zero"], 4)

            def body(i, l, n):
                pool.wait_ge(s["proj"], n * U + 1)
                pool.tensor_copy(wq[:, :], g["Wq"][:, l, :]).then_inc(s["wq"], 1)
                for u in range(U):
                    finished(pool, s["q"], n * U + u)
                    pool.tensor_tensor(q[:, u, :], q[:, u, :], shift[:, :], ALU.add).then_inc(s["qs"], 1)
                for u in range(U):
                    finished(pool, s["ks"], n * U + u)
                    pool.tensor_tensor(kc[:, u], kc[:, u], ks[:, u], ALU.add).then_inc(s["kr"], 1)
                for u in range(U):
                    finished(pool, s["qz"], n * U + u)
                    pool.tensor_tensor(qs[:, u, :], z[:, u, :], g["sinF"][:, :], ALU.mult).then_inc(s["qsn"], 1)
                for u in range(U):
                    finished(pool, s["mv"], n * U + u)
                    pool.tensor_tensor(ve[:, u, :], mv[:, u, :, 1], eps[:, :], ALU.add).then_inc(s["vareps"], 1)
                for u in range(U):
                    finished(pool, s["vareps"], n * U + u)
                    pool.tensor_tensor(rstd[:, u, :], ve[:, u, :], half[:, :], ALU.pow).then_inc(s["rstd"], 1)

            pool.sem_inc(s["proj"], 1)
            rounds(pool, body)

        @block.vector
        def _(v):
            v.memset(shift[:, :], GELU_SHIFT).then_inc(s["zero"], 1)
            v.wait_ge(s["zero"], 4)

            def body(i, l, n):
                bias = g["bkv"][:, l, :].unsqueeze(1).broadcast_to([P, NT, 2 * C])
                for u in range(U):
                    finished(v, s["proj"], n * U + u + 1)
                    v.tensor_tensor(kv[:, u], A[u].rearrange("p (h c) -> p h c", h=NT), bias,
                                    ALU.add).then_inc(s["kv"], 1)
                for u in range(U):
                    finished(v, s["k"], n * U + u)
                    v.scalar_tensor_tensor(out=kc[:, u], in0=k[:, u], scalar=GELU_SHIFT, in1=g["cosT"][:, :, :],
                                           op0=ALU.add, op1=ALU.mult)
                    for par in range(2):
                        a = [t.rearrange("p h (c t) -> p h c t", t=2) for t in (ks[:, u], k[:, u], g["sinT"][:, :, :])]
                        last = v.scalar_tensor_tensor(out=a[0][:, :, :, par], in0=a[1][:, :, :, 1 - par],
                                                      scalar=GELU_SHIFT, in1=a[2][:, :, :, par],
                                                      op0=ALU.add, op1=ALU.mult)
                    last.then_inc(s["ks"], 1)
                for u in range(U):
                    finished(v, s["ksum"], n * U + u)
                    v.tensor_scalar(kmean[:, u, :], D[u][:, N:N + 1], 1.0 / N, GELU_SHIFT, ALU.mult,
                                    ALU.add).then_inc(s["kmean"], 1)
                for u in range(U):
                    finished(v, s["kmean"], n * U + u)
                    v.tensor_scalar(km[:, u, :], g["head_mask"][:, :], kmean[:, u, :], None, ALU.mult).then_inc(s["km"], 1)
                    finished(v, s["kvm"], n * U + u)
                    v.scalar_tensor_tensor(out=kvbd[:, u, :], in0=A[u][:, 0:C], scalar=1.0 / N, in1=g["head_mask"][:, :],
                                           op0=ALU.mult, op1=ALU.mult).then_inc(s["kvbd"], 1)
                for u in range(U):
                    finished(v, s["dens"], n * U + u)
                    v.reciprocal(z[:, u, :], z[:, u, :]).then_inc(s["z"], 1)
                for u in range(U):
                    finished(v, s["z"], n * U + u)
                    finished(v, s["qs"], n * U + u)
                    v.tensor_tensor(z[:, u, :], q[:, u, :], z[:, u, :], ALU.mult).then_inc(s["qz"], 1)
                for u in range(U):
                    finished(v, s["qz"], n * U + u)
                    v.tensor_tensor(qc[:, u, :], z[:, u, :], g["cosF"][:, :], ALU.mult).then_inc(s["qc"], 1)
                for u in range(U):
                    finished(v, s["out"], n * U + u)
                    v.tensor_tensor(q[:, u, :], A[u][:, 0:N], h[:, u, :], ALU.add).then_inc(s["y"], 1)
                for u in range(U):
                    finished(v, s["yt"], n * U + u)
                    for t in range(NT):
                        last = v.bn_stats(st[:, u, t, :], D[u][:, t * C:(t + 1) * C])
                    last.then_inc(s["stats"], 1)
                for u in range(U):
                    held(v, s["stats"], n * U + u, s["tick"])
                    for t in range(NT):
                        last = v.bn_aggr(mv[:, u, t, :], st[:, u, t, :])
                    last.then_inc(s["mv"], 1)
                for u in range(U):
                    finished(v, s["rstd"], n * U + u)
                    for t in range(NT):
                        last = v.tensor_scalar(k[:, u, t, :], D[u][:, t * C:(t + 1) * C], mv[:, u, t, 0:1],
                                               rstd[:, u, t:t + 1], ALU.subtract, ALU.mult)
                    last.then_inc(s["un"], 1)

            rounds(v, body)

        @block.tensor
        def _(pe):
            pe.wait_ge(s["zero"], 4)

            def body(i, l, n):
                finished(pe, s["wq"], n)
                for u in range(U):
                    finished(pe, s["h"], n * U + u)
                    finished(pe, s["h0"], i * U + u)
                    pe.matmul(D[u][:, 0:N], lhsT=wq[:, :], rhs=h[:, u, :], start=True, stop=True)
                    for t in range(NT):
                        last = pe.matmul(A[u][:, t * 2 * C:(t + 1) * 2 * C], lhsT=h[:, u, t * P:(t + 1) * P],
                                         rhs=g["Wkv"][:, l, :], start=True, stop=True)
                    last.then_inc(s["proj"], 1)
                for u in range(U):
                    finished(pe, s["k"], n * U + u)
                    finished(pe, s["q"], n * U + u)
                    for t in range(NT):
                        last = pe.matmul(D[u][:, N:N + 1], lhsT=k[:, u, t, :], rhs=ones[:, :],
                                         start=(t == 0), stop=(t == NT - 1))
                    last.then_inc(s["ksum"], 1)
                for u in range(U):
                    finished(pe, s["kr"], n * U + u)
                    for t in range(NT):
                        last = pe.matmul(A[u][:, 0:C], lhsT=kc[:, u, t, :], rhs=kv[:, u, t, C:2 * C],
                                         start=(t == 0), stop=(t == NT - 1))
                    last.then_inc(s["kvm"], 1)
                for u in range(U):
                    finished(pe, s["km"], n * U + u)
                    finished(pe, s["qs"], n * U + u)
                    pe.matmul(D[u][:, 0:N], lhsT=km[:, u, :], rhs=q[:, u, :], start=True, stop=True)\
                      .then_inc(s["den"], 1)
                    finished(pe, s["kvbd"], n * U + u)
                    pe.matmul(A[u][:, C:2 * C], lhsT=g["pair_turn"][:, :], rhs=kvbd[:, u, :], start=True, stop=True)\
                      .then_inc(s["kv2"], 1)
                for u in range(U):
                    finished(pe, s["qc"], n * U + u)
                    finished(pe, s["kv2s"], n * U + u)
                    pe.matmul(A[u][:, 0:N], lhsT=kvbd[:, u, :], rhs=qc[:, u, :], start=True, stop=False)
                    finished(pe, s["qsn"], n * U + u)
                    pe.matmul(A[u][:, 0:N], lhsT=kv2[:, u, :], rhs=qs[:, u, :], start=False, stop=True)\
                      .then_inc(s["out"], 1)
                for u in range(U):
                    finished(pe, s["y"], n * U + u)
                    for t in range(NT):
                        last = turn(nc, D[u][:, t * P:(t + 1) * P], q[:, u, t * P:(t + 1) * P], ident[:, :])
                    last.then_inc(s["yt"], 1)
                for u in range(U):
                    finished(pe, s["un"], n * U + u)
                    for t in range(NT):
                        last = turn(nc, A[u][:, t * P:(t + 1) * P], k[:, u, t, :], ident[:, :])
                    last.then_inc(s["unt"], 1)

            rounds(pe, body)

        @block.scalar
        def _(act):
            act.preload_act_table_set("gelu_and_others")
            act.sem_inc(s["h"], U)
            act.sem_inc(s["saved"], U)
            with act.Fori(0, steps) as i:
                for u in range(U):
                    act.wait_ge(s["saved"], i * U + u + 1)
                    act.activation(h[:, u, :], hv[:, i, u, :], ACT.Copy).then_inc(s["h0"], 1)
                with act.Fori(0, L) as l:
                    n = i * L + l
                    for u in range(U):
                        held(act, s["proj"], n * U + u + 1, s["atick"])
                        act.activation(q[:, u, :], D[u][:, 0:N], ACT.Gelu, bias=column(g["bq"], l)).then_inc(s["q"], 1)
                    for u in range(U):
                        finished(act, s["kv"], n * U + u)
                        act.activation(k[:, u], kv[:, u, :, 0:C], ACT.Gelu).then_inc(s["k"], 1)
                    for u in range(U):
                        finished(act, s["den"], n * U + u)
                        act.activation(z[:, u, :], D[u][:, 0:N], ACT.Copy, bias=1e-6).then_inc(s["dens"], 1)
                        finished(act, s["kv2"], n * U + u)
                        act.activation(kv2[:, u, :], A[u][:, C:2 * C], ACT.Copy).then_inc(s["kv2s"], 1)
                    for u in range(U):
                        held(act, s["unt"], n * U + u, s["atick"])
                        act.activation(h[:, u, :], A[u][:, 0:N], ACT.Identity, bias=column(g["lnA_b"], l),
                                       scale=column(g["lnA_g"], l)).then_inc(s["h"], 1)
                for u in range(U):
                    held(act, s["h"], (i + 1) * (L * U) + u, s["atick"])
                    act.activation(hv[:, i, u, :], h[:, u, :], ACT.Copy).then_inc(s["saved"], 1)


def ffn_phase(nc, g):
    U = 2
    steps = B // U
    with ExitStack() as ctx:
        s = semaphores(nc, ctx, "ff", "zero tick h0 up gl down y yt stats mv vareps rstd un ug ub x")

        def sb(name, shape, dt=F32):
            return ctx.enter_context(nc.sbuf_tensor("ff_" + name, shape, dt))

        half = sb("half", [P, NT])
        eps = sb("eps", [P, NT])
        h = sb("h", [P, U, N])
        gl = sb("gl", [P, U, FJ, N])
        y = sb("y", [P, U, N])
        un = sb("un", [P, U, NT, C])
        st = sb("st", [P, U, NT, 6])
        mv = sb("mv", [P, U, NT, 2])
        ve = sb("ve", [P, U, NT])
        rstd = sb("rstd", [P, U, NT])
        X, HT, ident, PS = g["X"], g["HT"], g["ident"], g["PS"]
        hv = HT[:, :, :].rearrange("p (i u) n -> p i u n", u=U)
        xv = X[:, :, :, :].rearrange("p (i u) h c -> p i u h c", u=U)
        up = [PS[:, 4 * u:4 * u + 2, :].rearrange("p b (j n) -> p (b j) n", n=N) for u in range(U)]
        D = [PS[:, 4 * u + 2, :] for u in range(U)]
        T = [PS[:, 4 * u + 3, :] for u in range(U)]
        gain = g["ln2_g"][:, :].unsqueeze(1).broadcast_to([P, NT, C])
        shift = g["ln2_b"][:, :].unsqueeze(1).broadcast_to([P, NT, C])
        block = ctx.enter_context(nc.Block())

        @block.gpsimd
        def _(pool):
            pool.memset(half[:, :], -0.5).then_inc(s["zero"], 1)
            pool.memset(eps[:, :], LN_EPS_A).then_inc(s["zero"], 1)
            pool.wait_ge(s["zero"], 2)
            with pool.Fori(0, steps) as i:
                for u in range(U):
                    finished(pool, s["mv"], i * U + u)
                    pool.tensor_tensor(ve[:, u, :], mv[:, u, :, 1], eps[:, :], ALU.add).then_inc(s["vareps"], 1)
                for u in range(U):
                    finished(pool, s["vareps"], i * U + u)
                    pool.tensor_tensor(rstd[:, u, :], ve[:, u, :], half[:, :], ALU.pow).then_inc(s["rstd"], 1)
                for u in range(U):
                    finished(pool, s["un"], i * U + u)
                    pool.tensor_tensor(un[:, u], un[:, u], gain, ALU.mult).then_inc(s["ug"], 1)
                for u in range(U):
                    finished(pool, s["ug"], i * U + u)
                    pool.tensor_tensor(un[:, u], un[:, u], shift, ALU.add).then_inc(s["ub"], 1)

        @block.vector
        def _(v):
            v.sem_inc(s["x"], U)
            with v.Fori(0, steps) as i:
                for u in range(U):
                    finished(v, s["down"], i * U + u)
                    v.scalar_tensor_tensor(out=y[:, u, :], in0=D[u][:, 0:N], scalar=g["b2"][:, 0:1], in1=h[:, u, :],
                                           op0=ALU.add, op1=ALU.add).then_inc(s["y"], 1)
                for u in range(U):
                    finished(v, s["yt"], i * U + u)
                    for t in range(NT):
                        last = v.bn_stats(st[:, u, t, :], T[u][:, t * C:(t + 1) * C])
                    last.then_inc(s["stats"], 1)
                for u in range(U):
                    held(v, s["stats"], i * U + u, s["tick"])
                    for t in range(NT):
                        last = v.bn_aggr(mv[:, u, t, :], st[:, u, t, :])
                    last.then_inc(s["mv"], 1)
                for u in range(U):
                    finished(v, s["rstd"], i * U + u)
                    for t in range(NT):
                        last = v.tensor_scalar(un[:, u, t, :], T[u][:, t * C:(t + 1) * C], mv[:, u, t, 0:1],
                                               rstd[:, u, t:t + 1], ALU.subtract, ALU.mult)
                    last.then_inc(s["un"], 1)
                for u in range(U):
                    finished(v, s["ub"], i * U + u)
                    v.tensor_tensor(xv[:, i, u], xv[:, i, u], un[:, u], ALU.add).then_inc(s["x"], 1)

        @block.tensor
        def _(pe):
            with pe.Fori(0, steps) as i:
                for u in range(U):
                    finished(pe, s["h0"], i * U + u)
                    for j in range(FJ):
                        last = pe.matmul(up[u][:, j, :], lhsT=g["W1"][:, j * P:(j + 1) * P], rhs=h[:, u, :],
                                         start=True, stop=True)
                    last.then_inc(s["up"], 1)
                for u in range(U):
                    finished(pe, s["gl"], i * U + u)
                    for j in range(FJ):
                        last = pe.matmul(D[u][:, 0:N], lhsT=g["W2"][:, j, :], rhs=gl[:, u, j, :],
                                         start=(j == 0), stop=(j == FJ - 1))
                    last.then_inc(s["down"], 1)
                for u in range(U):
                    finished(pe, s["y"], i * U + u)
                    for t in range(NT):
                        last = turn(nc, T[u][:, t * P:(t + 1) * P], y[:, u, t * P:(t + 1) * P], ident[:, :])
                    last.then_inc(s["yt"], 1)

        @block.scalar
        def _(act):
            act.preload_act_table_set("gelu_and_others")
            with act.Fori(0, steps) as i:
                for u in range(U):
                    act.wait_ge(s["x"], i * U + u + 1)
                    act.activation(h[:, u, :], hv[:, i, u, :], ACT.Copy).then_inc(s["h0"], 1)
                for u in range(U):
                    finished(act, s["up"], i * U + u)
                    for j in range(FJ):
                        last = act.activation(gl[:, u, j, :], up[u][:, j, :], ACT.Gelu, bias=g["b1"][:, j:j + 1])
                    last.then_inc(s["gl"], 1)


def moe0_phase(nc, g, name):
    U = 2
    steps = B // U
    with ExitStack() as ctx:
        s = semaphores(nc, ctx, name, "zero tick stats mv vareps rstd r rt rT lg lgb mx d eq rank best hot sum ex w ws wst "
                                      "wsT bias acc all x")

        def sb(nm, shape, dt=F32):
            return ctx.enter_context(nc.sbuf_tensor(name + nm, shape, dt))

        half = sb("half", [P, NT])
        eps = sb("eps", [P, NT])
        st = sb("st", [P, U, NT, 6])
        mv = sb("mv", [P, U, NT, 2])
        ve = sb("ve", [P, U, NT])
        rstd = sb("rstd", [P, U, NT])
        r = sb("r", [P, U, NT, C])
        rT = sb("rT", [P, U, N])
        lg = sb("lg", [P, U, NT, E])
        mx = sb("mx", [P, U, NT])
        dd = sb("dd", [P, U, NT, E])
        hot = sb("hot", [P, U, NT, E])
        w = sb("w", [P, U, NT])
        wsT = sb("wsT", [E, U, N])
        X, ident, PS = g["X"], g["ident"], g["PS"]
        xv = X[:, :, :, :].rearrange("p (i u) h c -> p i u h c", u=U)
        T = [PS[:, 4 * u, :] for u in range(U)]
        R = [PS[:, 4 * u + 1, :] for u in range(U)]
        Y = [PS[:, 4 * u + 2:4 * u + 4, :] for u in range(U)]
        first = g["first"][:, :].unsqueeze(1).broadcast_to([P, NT, E])
        block = ctx.enter_context(nc.Block())

        @block.gpsimd
        def _(pool):
            pool.memset(half[:, :], -0.5).then_inc(s["zero"], 1)
            pool.memset(eps[:, :], LN_EPS).then_inc(s["zero"], 1)
            pool.wait_ge(s["zero"], 2)
            with pool.Fori(0, steps) as i:
                for u in range(U):
                    finished(pool, s["mv"], i * U + u)
                    pool.tensor_tensor(ve[:, u, :], mv[:, u, :, 1], eps[:, :], ALU.add).then_inc(s["vareps"], 1)
                for u in range(U):
                    finished(pool, s["vareps"], i * U + u)
                    pool.tensor_tensor(rstd[:, u, :], ve[:, u, :], half[:, :], ALU.pow).then_inc(s["rstd"], 1)

        @block.vector
        def _(v):
            v.sem_inc(s["x"], U * NT)
            with v.Fori(0, steps) as i:
                def each(before, after, op, hold=False):
                    for u in range(U):
                        if hold:
                            held(v, s[before], i * U + u, s["tick"])
                        elif before:
                            finished(v, s[before], i * U + u)
                        op(u).then_inc(s[after], 1)

                def both(op):
                    def go(u):
                        for h in range(NT):
                            last = op(u, h)
                        return last
                    return go

                each(None, "stats", both(lambda u, h: v.bn_stats(st[:, u, h, :], xv[:, i, u, h, :])))
                each("stats", "mv", both(lambda u, h: v.bn_aggr(mv[:, u, h, :], st[:, u, h, :])), hold=True)
                each("rstd", "r", both(lambda u, h: v.tensor_scalar(
                    r[:, u, h, :], xv[:, i, u, h, :], mv[:, u, h, 0:1], rstd[:, u, h:h + 1], ALU.subtract, ALU.mult)))
                bias = g["rb0"][:, :].unsqueeze(1).broadcast_to([P, NT, E])
                each("lg", "lgb", lambda u: v.tensor_tensor(
                    lg[:, u], R[u][:, 0:NT * E].rearrange("p (h e) -> p h e", e=E), bias, ALU.add))
                each("lgb", "mx", lambda u: v.tensor_reduce(mx[:, u, :], lg[:, u], AX.X, ALU.max))
                each("mx", "d", lambda u: v.tensor_tensor(dd[:, u], lg[:, u], spread(mx[:, u, :], E), ALU.subtract))
                each("d", "eq", lambda u: v.tensor_tensor(hot[:, u], lg[:, u], spread(mx[:, u, :], E), ALU.is_equal))
                each("eq", "rank", lambda u: v.tensor_tensor(hot[:, u], hot[:, u], first, ALU.mult))
                each("rank", "best", lambda u: v.tensor_reduce(mx[:, u, :], hot[:, u], AX.X, ALU.max))
                each("best", "hot", lambda u: v.tensor_tensor(hot[:, u], hot[:, u], spread(mx[:, u, :], E),
                                                              ALU.is_equal))
                each("ex", "sum", lambda u: v.tensor_reduce(w[:, u, :], dd[:, u], AX.X, ALU.add))
                each("sum", "w", lambda u: v.reciprocal(w[:, u, :], w[:, u, :]))
                for u in range(U):
                    finished(v, s["hot"], i * U + u)
                    finished(v, s["w"], i * U + u)
                    v.tensor_tensor(hot[:, u], hot[:, u], spread(w[:, u, :], E), ALU.mult).then_inc(s["ws"], 1)
                for u in range(U):
                    finished(v, s["bias"], i * U + u)
                    v.tensor_tensor(xv[:, i, u], xv[:, i, u],
                                    R[u][:, 256:512].rearrange("p (h c) -> p h c", h=NT), ALU.add).then_inc(s["acc"], 1)
                for h in range(NT):
                    for e in range(E):
                        for u in range(U):
                            if e == 0:
                                finished(v, s["all"], (i * NT + h) * U + u)
                            v.wait_ge(s["acc"], i * (U + NT * E * U) + U + (h * E + e - 1) * U + u + 1 if (h or e)
                                      else i * (U + NT * E * U) + u + 1)
                            op = v.scalar_tensor_tensor(
                                out=xv[:, i, u, h, :], in0=Y[u][:, e // 4, (e % 4) * C:(e % 4 + 1) * C],
                                scalar=hot[:, u, h, e:e + 1], in1=xv[:, i, u, h, :], op0=ALU.mult, op1=ALU.add)
                            op.then_inc(s["acc"], 1)
                    for u in range(U):
                        v.wait_ge(s["acc"], i * (U + NT * E * U) + U + (h * E + E - 1) * U + u + 1)
                        v.sem_inc(s["x"], 1)

        @block.tensor
        def _(pe):
            with pe.Fori(0, steps) as i:
                for u in range(U):
                    finished(pe, s["r"], i * U + u)
                    for h in range(NT):
                        last = turn(nc, T[u][:, h * P:(h + 1) * P], r[:, u, h, :], ident[:, :])
                    last.then_inc(s["rt"], 1)
                for u in range(U):
                    finished(pe, s["rT"], i * U + u)
                    for h in range(NT):
                        last = pe.matmul(R[u][:, h * E:(h + 1) * E], lhsT=rT[:, u, h * P:(h + 1) * P],
                                         rhs=g["rw0"][:, :], start=True, stop=True)
                    last.then_inc(s["lg"], 1)
                for h in range(NT):
                    for u in range(U):
                        pe.wait_ge(s["x"], (i * NT + h) * U + u + U + 1)
                        for b in range(2):
                            last = pe.matmul(Y[u][:, b, :], lhsT=rT[:, u, h * P:(h + 1) * P],
                                             rhs=g["ew0"][:, 4 * b:4 * b + 4, :], start=True, stop=True)
                        last.then_inc(s["all"], 1)
                    if h == 0:
                        for u in range(U):
                            finished(pe, s["ws"], i * U + u)
                            for t in range(NT):
                                last = turn(nc, T[u][0:E, t * P:(t + 1) * P], hot[:, u, t, :], ident[:, :])
                            last.then_inc(s["wst"], 1)
                        for u in range(U):
                            finished(pe, s["wsT"], i * U + u)
                            for t in range(NT):
                                last = pe.matmul(R[u][:, 256 + t * C:256 + (t + 1) * C],
                                                 lhsT=wsT[:, u, t * P:(t + 1) * P], rhs=g["eb0"][:, :],
                                                 start=True, stop=True)
                            last.then_inc(s["bias"], 1)

        @block.scalar
        def _(act):
            with act.Fori(0, steps) as i:
                for u in range(U):
                    finished(act, s["rt"], i * U + u)
                    act.activation(rT[:, u, :], T[u][:, 0:N], ACT.Copy).then_inc(s["rT"], 1)
                for u in range(U):
                    finished(act, s["d"], i * U + u)
                    act.activation(dd[:, u], dd[:, u], ACT.Exp).then_inc(s["ex"], 1)
                for u in range(U):
                    finished(act, s["wst"], i * U + u)
                    act.activation(wsT[:, u, :], T[u][0:E, 0:N], ACT.Copy).then_inc(s["wsT"], 1)


def attention_phase(nc, g, name, scale=1.0, norm_eps=None, weights=False, bias=False, causal=False, keep_max=False,
                    deflate=False):
    G = 4
    S = NH // G
    RW = 32
    RING = 8
    NEG = -3e38
    AT = {"unit": 0, "wn": 1, "hi": 1, "lo": 2, "oT1": 3, "turns": 3, "stats": 3, "aggr": 4, "lanes": 4, "minus1": 5,
          "mt1": 6, "r": 6, "ot": 8, "y": 9, "dot": 10, "yd": 11, "xb": 6, "va": 12 if deflate else 8, "rt": 10, "qkv": 11, "oT0": 11, "raw": 12, "yt": 13,
          "minus0": 13, "sq": 13, "ss": 14, "root": 14, "proj": 14, "x": 15, "mt0": 15}
    LAG = 3
    TLAG = 6
    HN = NH // 2
    SA = 2 if keep_max else 1

    n_prob = NT * N - (P if causal else 0)
    with ExitStack() as ctx:
        s = semaphores(nc, ctx, name, "zero zeroq tick ptick stats mv vareps rstd r rt rT qkv0 qkv1 raw sq ss sse ln root nw rn unit wn hi lo "
                                      " qt kt kT qm qmv mt0 mt1 mT0 mT1 nwa nwb nwc top mx nhi0 nhi1 nlo0 nlo1 sc exp tri pv oT0 oT1 ot den y va t1 t2 t3 yd yt yT "
                                      "proj xb x")

        def sb(nm, shape, dt=F32):
            return ctx.enter_context(nc.sbuf_tensor(name + nm, shape, dt))

        half = sb("half", [P, NT])
        eps = sb("eps", [P, NT])
        st = sb("st", [P, NT, 6])
        mv = sb("mv", [P, NT, 2])
        ve = sb("ve", [P, NT])
        rstd = sb("rstd", [P, NT])
        r = sb("r", [P, NT, C])
        rT = sb("rT", [P, N])
        identb = sb("identb", [P, P], BF16)
        qk = sb("qk", [P, NT, 2 * C])
        sq = sb("sq", [P, NT, 2 * C])
        ss = sb("ss", [P, NT, 2 * NH])
        rn = sb("rn", [P, NT, 2 * NH])
        ln = sb("ln", [P, NT, 2 * NH])
        nw = sb("nw", [P, NT, 2 * NH])
        parts = sb("parts", [P, NT, 2, NH, RW], BF16)
        qm = sb("qm", [P, 2, G, S, N], BF16)
        kT = sb("kT", [P, 2, G, N], BF16)
        va = sb("va", [P, 2, NT, NH, RW])
        mx = sb("mx", [P, NT, NH])
        minus = sb("minus", [P, NT, NH, 2], BF16)
        mT = sb("mT", [2 * HN, 2, N], BF16)
        sel = sb("sel", [2 * HN, HN, P], BF16)
        prob = sb("prob", [P, RING, NT * N])
        oT = sb("oT", [P, G, N])
        den = sb("den", [P, NT, NH])
        y = sb("y", [P, NT, C])
        t = sb("t", [P, NT, C])
        dot = sb("dot", [P, NT, NH])
        vv = sb("vv", [P, NT, NH])
        yT = sb("yT", [P, N])
        vs = sb("vs", [P, 2, NT, C])
        junk = sb("junk", [P, 2 * NT, N])
        X, ident, PS = g["X"], g["ident"], g["PS"]
        wqkv, wo = g[name + "_wqkv"], g[name + "_wo"]
        SB = [PS[:, i, :] for i in range(2 if keep_max else 4)]
        NSB = len(SB)
        MB = [PS[:, 2, :], PS[:, 3, :]]
        OB = PS[:, 4:6, :].rearrange("p b (g n) -> p (b g) n", n=N)
        M0, M1 = PS[:, 6, :], PS[:, 7, :]
        block = ctx.enter_context(nc.Block())

        def heads(ap):
            return ap.rearrange("p t (n d) -> p t n d", d=HD)

        def next1(b):
            return not isinstance(b, int) or b + 1 < B

        def next2(b):
            return not isinstance(b, int) or b + 2 < B

        def every_step(eng, step):
            step(0, 0)
            with eng.Fori(0, B // 2 - 2) as i:
                step(2 * i + 1, 1)
                step(2 * i + 2, 0)
            for b in range(B - 3, B):
                step(b, b % 2)

        def behind(b):
            return not isinstance(b, int) or b > 0

        @block.gpsimd
        def _(pool):
            pool.memset(half[:, :], -0.5).then_inc(s["zero"], 1)
            pool.memset(eps[:, :], LN_EPS).then_inc(s["zero"], 1)
            pool.memset(parts[:, :, :, :, :], 0.0).then_inc(s["zero"], 1)
            pool.memset(va[:, :, :, :, :], 0.0).then_inc(s["zero"], 1)
            pool.wait_ge(s["zero"], 4)
            pool.memset(va[:, :, :, :, HD:HD + 1], 1.0).then_inc(s["zero"], 1)
            pool.wait_ge(s["zero"], 5)

            def prepare_rstd(b):
                finished(pool, s["mv"], b)
                pool.tensor_tensor(ve[:, :], mv[:, :, 1], eps[:, :], ALU.add).then_inc(s["vareps"], 1)
                finished(pool, s["vareps"], b)
                pool.tensor_tensor(rstd[:, :], ve[:, :], half[:, :], ALU.pow).then_inc(s["rstd"], 1)

            def place_v(b, u):
                held(pool, s["raw"], b, s["ptick"])
                held(pool, s["pv"], (b - 1) * NH - 1, s["ptick"])
                if deflate:
                    held(pool, s["yd"], b - 2, s["ptick"])
                pool.tensor_copy(va[:, u, :, :, 0:HD], heads(vs[:, u])).then_inc(s["va"], 1)

            def select(b, h):
                held(pool, s["exp"], b * NH + h, s["ptick"])
                a = prob[:, h % RING, :]
                for at in (0, N):
                    part = a[:, at:at + P]
                    last = pool.affine_select(out=part, in_=part, compare_op=ALU.is_ge, fill=0.0, base=0,
                                              pattern=[[1, P]], channel_multiplier=-1)
                last.then_inc(s["tri"], 1)

            def step(b, u):
                for h in range(NH):
                    if causal:
                        select(b, h)
                    if h == AT["aggr"] and next2(b):
                        prepare_rstd(b + 2)
                    if h == AT["xb"] and bias:
                        finished(pool, s["r"], b)
                        nx = X[:, b]
                        pool.tensor_tensor(nx, nx, g[name + "_bo"][:, :].unsqueeze(1).broadcast_to([P, NT, C]),
                                           ALU.add).then_inc(s["xb"], 1)
                    if h == AT["va"] and next1(b):
                        place_v(b + 1, 1 - u)

            prepare_rstd(0)
            prepare_rstd(1)
            place_v(0, 0)
            every_step(pool, step)

        @block.vector
        def _(v):
            v.memset(qm[:, :, :, :, :], 0.0).then_inc(s["zeroq"], 1)
            v.wait_ge(s["zero"], 5)
            v.tensor_copy(identb[:, :], ident[:, :]).then_inc(s["zero"], 1)
            if keep_max:
                pairs = ident[0:2 * HN, 0:2 * HN].rearrange("p (n k) -> p n k", k=2)
                v.tensor_tensor(sel[:, :, :], pairs[:, :, 0:1].broadcast_to([2 * HN, HN, P]),
                                pairs[:, :, 1:2].broadcast_to([2 * HN, HN, P]), ALU.add).then_inc(s["zero"], 1)

            def take_lane(b, u, lane):
                if lane == SA:
                    finished(v, s["zeroq"], 0)
                    finished(v, s["qt"], b)
                    finished(v, s["qm"], b * SA + SA - 1)
                rows = slice(RW * lane, RW * (lane + 1))
                v.tensor_copy(qm[rows, u, :, lane, :], M0[rows, :].bitcast(BF16).rearrange("p (g n) -> p g n", n=N))\
                 .then_inc(s["qmv"], 1)

            def prepare_stats(b):
                for h in range(NT):
                    last = v.bn_stats(st[:, h, :], X[:, b, h, :])
                last.then_inc(s["stats"], 1)

            def prepare_aggr(b):
                held(v, s["stats"], b, s["tick"])
                for h in range(NT):
                    last = v.bn_aggr(mv[:, h, :], st[:, h, :])
                last.then_inc(s["mv"], 1)

            def prepare_r(b):
                held(v, s["rstd"], b, s["tick"])
                for h in range(NT):
                    last = v.tensor_scalar(r[:, h, :], X[:, b, h, :], mv[:, h, 0:1], rstd[:, h:h + 1],
                                           ALU.subtract, ALU.mult)
                last.then_inc(s["r"], 1)

            def prepare_raw(b, u):
                finished(v, s["va"], b - 2)
                for h in range(NT):
                    src = (M1, M0)[h][:, 0:3 * C]
                    finished(v, s["qkv0" if h == 0 else "qkv1"], b)
                    outs = ((qk[:, h, :].rearrange("p (n d) -> p n d", d=HD), 0, 2 * C),
                            (vs[:, u, h, :].rearrange("p (n d) -> p n d", d=HD), 2 * C, 3 * C))
                    for dst, lo, hi in outs:
                        part = src[:, lo:hi].rearrange("p (n d) -> p n d", d=HD)
                        if bias:
                            last = v.tensor_tensor(dst, part, g[name + "_bqkv"][:, lo:hi].rearrange(
                                "p (n d) -> p n d", d=HD), ALU.add)
                        else:
                            last = v.tensor_copy(dst, part)
                    last.then_inc(s["raw"], 1) if h else None

            def prepare_sq(b):
                finished(v, s["raw"], b)
                v.tensor_tensor(sq[:, :, :], qk[:, :, :], qk[:, :, :], ALU.mult).then_inc(s["sq"], 1)

            def prepare_ss(b):
                finished(v, s["sq"], b)
                v.tensor_reduce(ss[:, :, :], heads(sq[:, :, :]), AX.X, ALU.add).then_inc(s["ss"], 1)
                finished(v, s["ss"], b)
                v.tensor_scalar(ss[:, :, :], ss[:, :, :], 1.0 / HD, norm_eps, ALU.mult, ALU.add).then_inc(s["sse"], 1)

            def prepare_unit(b):
                finished(v, s["root"], b)
                v.tensor_tensor(nw[:, :, :], rn[:, :, :], rn[:, :, :], ALU.mult).then_inc(s["nwa"], 1)
                finished(v, s["nwa"], b)
                v.tensor_tensor(nw[:, :, :], nw[:, :, :], ss[:, :, :], ALU.mult).then_inc(s["nwb"], 1)
                finished(v, s["nwb"], b)
                v.tensor_scalar(nw[:, :, :], nw[:, :, :], -0.5, 1.5, ALU.mult, ALU.add).then_inc(s["nwc"], 1)
                finished(v, s["nwc"], b)
                v.tensor_tensor(rn[:, :, :], rn[:, :, :], nw[:, :, :], ALU.mult).then_inc(s["rn"], 1)
                finished(v, s["rn"], b)
                v.tensor_tensor(heads(qk[:, :, :]), heads(qk[:, :, :]), spread(rn[:, :, :], HD),
                                ALU.mult).then_inc(s["unit"], 1)

            def prepare_wn(b):
                finished(v, s["unit"], b)
                v.tensor_tensor(qk[:, :, :], qk[:, :, :], g[name + "_wn"][:, :].unsqueeze(1).broadcast_to(
                    [P, NT, 2 * C]), ALU.mult).then_inc(s["wn"], 1)

            def halves(w):
                return heads(qk[:, :, w * C:(w + 1) * C])

            def prepare_hi(b):
                finished(v, s["wn" if weights else "unit" if norm_eps is not None else "raw"], b)
                finished(v, s["qt"], b - 1)
                for w in range(2):
                    rows = parts[:, :, w, :, :].rearrange("p t n (k d) -> p t n k d", d=HD)
                    for t in range(NT):
                        last = v.tensor_copy(rows[:, t, :, 0:2 + w:1 + w],
                                             halves(w)[:, t].unsqueeze(2).broadcast_to([P, NH, 2, HD]))
                last.then_inc(s["hi"], 1)

            def prepare_lo(b):
                finished(v, s["hi"], b)
                for w, at in ((0, 2 * HD), (1, HD)):
                    last = v.tensor_tensor(parts[:, :, w, :, at:at + HD], halves(w), parts[:, :, w, :, 0:HD],
                                           ALU.subtract)
                last.then_inc(s["lo"], 1)

            def prepare_max(b, h):
                if not causal:
                    finished(v, s["top"], b * NH + h)
                if causal:
                    held(v, s["top"], b * NH + h, s["tick"])
                    for t in range(NT):
                        last = v.tensor_tensor_reduce(
                            out=junk[:, h % 2 * NT + t, 0:(t + 1) * P], in0=MB[h % 2][:, t * N:t * N + (t + 1) * P],
                            in1=g["tri"][:, t, 0:(t + 1) * P], scale=1.0, scalar=NEG, op0=ALU.add, op1=ALU.max,
                            accum_out=mx[:, t, h:h + 1])
                else:
                    last = v.tensor_reduce(mx[:, :, h], MB[h % 2].rearrange("p (t n) -> p t n", n=N), AX.X, ALU.max)
                last.then_inc(s["mx"], 1)

            def prepare_minus(b, half):
                part = slice(half * HN, (half + 1) * HN)
                finished(v, s["mx"], b * NH + half * HN + HN - 1)
                finished(v, s[("mt0", "mt1")[half]], b - 1)
                v.tensor_scalar(minus[:, :, part, 0], mx[:, :, part], -1.0, None, ALU.mult)\
                 .then_inc(s[("nhi0", "nhi1")[half]], 1)
                finished(v, s[("nhi0", "nhi1")[half]], b)
                v.scalar_tensor_tensor(out=minus[:, :, part, 1], in0=mx[:, :, part], scalar=-1.0,
                                       in1=minus[:, :, part, 0], op0=ALU.mult, op1=ALU.subtract)\
                 .then_inc(s[("nlo0", "nlo1")[half]], 1)

            def complete_y(b):
                finished(v, s["ot"], b)
                cols = [(M0, M1)[h][:, :].rearrange("p (n r) -> p n r", r=RW) for h in range(NT)]
                for h in range(NT):
                    last = v.reciprocal(den[:, h, :], cols[h][:, :, HD])
                last.then_inc(s["den"], 1)
                finished(v, s["den"], b)
                for h in range(NT):
                    last = v.tensor_tensor(y[:, h, :].rearrange("p (n d) -> p n d", d=HD), cols[h][:, :, 0:HD],
                                           spread(den[:, h, :], HD), ALU.mult)
                last.then_inc(s["y"], 1)

            def complete_dot(b, u):
                vh = va[:, u, :, :, 0:HD]
                yh, th = heads(y[:, :, :]), heads(t[:, :, :])
                v.tensor_tensor(th, vh, vh, ALU.mult).then_inc(s["t1"], 1)
                v.wait_ge(s["t1"], b * 4 + 1)
                v.tensor_reduce(vv[:, :, :], th, AX.X, ALU.add).then_inc(s["t1"], 1)
                v.wait_ge(s["t1"], b * 4 + 2)
                finished(v, s["y"], b)
                v.tensor_tensor(th, yh, vh, ALU.mult).then_inc(s["t2"], 1)
                v.tensor_scalar(vv[:, :, :], vv[:, :, :], 1e-24, None, ALU.max).then_inc(s["t1"], 1)
                v.wait_ge(s["t1"], b * 4 + 3)
                v.reciprocal(vv[:, :, :], vv[:, :, :]).then_inc(s["t1"], 1)
                finished(v, s["t2"], b)
                v.tensor_reduce(dot[:, :, :], th, AX.X, ALU.add).then_inc(s["t3"], 1)
                v.wait_ge(s["t1"], b * 4 + 4)
                v.wait_ge(s["t3"], b * 3 + 1)
                v.tensor_tensor(dot[:, :, :], dot[:, :, :], vv[:, :, :], ALU.mult).then_inc(s["t3"], 1)

            def complete_yd(b, u):
                vh = va[:, u, :, :, 0:HD]
                yh, th = heads(y[:, :, :]), heads(t[:, :, :])
                v.wait_ge(s["t3"], b * 3 + 2)
                v.tensor_tensor(th, vh, spread(dot[:, :, :], HD), ALU.mult).then_inc(s["t3"], 1)
                v.wait_ge(s["t3"], b * 3 + 3)
                v.tensor_tensor(yh, yh, th, ALU.subtract).then_inc(s["yd"], 1)

            def complete_x(b):
                finished(v, s["proj"], b)
                if bias:
                    finished(v, s["xb"], b)
                v.tensor_tensor(X[:, b], X[:, b], M1[:, 0:N].rearrange("p (t c) -> p t c", t=NT),
                                ALU.add).then_inc(s["x"], 1)

            def step(b, u):
                for h in range(NH):
                    if keep_max and h < TLAG:
                        prepare_max(b, NH - TLAG + h)
                    if keep_max and h >= TLAG and next1(b):
                        prepare_max(b + 1, h - TLAG)
                    if next1(b):
                        if h == AT["unit"] and norm_eps is not None:
                            prepare_unit(b + 1)
                        if h == AT["wn"] and weights:
                            prepare_wn(b + 1)
                        if h == AT["hi"]:
                            prepare_hi(b + 1)
                        if h == AT["lo"]:
                            prepare_lo(b + 1)
                        if AT["lanes"] + SA <= h < AT["lanes"] + S:
                            take_lane(b + 1, 1 - u, h - AT["lanes"])
                    if next2(b):
                        if h == AT["stats"]:
                            prepare_stats(b + 2)
                        if h == AT["aggr"]:
                            prepare_aggr(b + 2)
                        if h == AT["r"]:
                            prepare_r(b + 2)
                        if h == AT["raw"]:
                            prepare_raw(b + 2, u)
                        if h == AT["sq"] and norm_eps is not None:
                            prepare_sq(b + 2)
                        if h == AT["ss"] and norm_eps is not None:
                            prepare_ss(b + 2)
                    if keep_max and h == AT["minus1"]:
                        prepare_minus(b, 1)
                    if keep_max and h == AT["minus0"] and next1(b):
                        prepare_minus(b + 1, 0)
                    if behind(b):
                        if h == AT["y"]:
                            complete_y(b - 1)
                        if h == AT["dot"] and deflate:
                            complete_dot(b - 1, 1 - u)
                        if h == AT["yd"] and deflate:
                            complete_yd(b - 1, 1 - u)
                        if h == AT["x"]:
                            complete_x(b - 1)

            for b in range(2):
                prepare_stats(b)
                prepare_aggr(b)
                prepare_r(b)
                prepare_raw(b, b)
                if norm_eps is not None:
                    prepare_sq(b)
                    prepare_ss(b)
                if b == 0:
                    if norm_eps is not None:
                        prepare_unit(0)
                    if weights:
                        prepare_wn(0)
                    prepare_hi(0)
                    prepare_lo(0)
                    for lane in range(SA, S):
                        take_lane(0, 0, lane)
                    if keep_max:
                        for h in range(NH - TLAG):
                            prepare_max(0, h)
                        prepare_minus(0, 0)
            every_step(v, step)
            complete_y(B - 1)
            if deflate:
                complete_dot(B - 1, 1)
                complete_yd(B - 1, 1)
            complete_x(B - 1)

        @block.tensor
        def _(pe):
            pe.wait_ge(s["zero"], 7 if keep_max else 6)

            def turned(dst, what):
                for gg in range(G):
                    for h in range(NT):
                        last = turn(nc, dst.bitcast(BF16)[:, gg * N + h * P:gg * N + (h + 1) * P],
                                    parts[:, h, what, S * gg:S * gg + S, :], identb[:, :])
                return last

            def lanes_taken(b):
                finished(pe, s["qm"], b * SA + SA - 1)
                if SA < S:
                    finished(pe, s["qmv"], (b + 1) * (S - SA) - 1)

            def prepare_rt(b):
                finished(pe, s["r"], b)
                if isinstance(b, int) and b <= 2:
                    lanes_taken(b - 1)
                    finished(pe, s["kT"], b - 1)
                    if keep_max:
                        finished(pe, s["mT0"], min(b - 1, 0))
                        finished(pe, s["mT1"], b - 2)
                else:
                    finished(pe, s["y"], b - 3)
                for h in range(NT):
                    last = turn(nc, M0[:, h * P:(h + 1) * P], r[:, h, :], ident[:, :])
                last.then_inc(s["rt"], 1)

            def prepare_qkv(b):
                finished(pe, s["rT"], b)
                for h in range(NT):
                    pe.matmul((M1, M0)[h][:, 0:3 * C], lhsT=rT[:, h * P:(h + 1) * P], rhs=wqkv[:, :],
                              start=True, stop=True).then_inc(s["qkv0" if h == 0 else "qkv1"], 1)

            def prepare_turns(b):
                finished(pe, s["lo"], b)
                finished(pe, s["x"], b - 3)
                if keep_max:
                    finished(pe, s["mT0"], b - 1)
                turned(M1, 1).then_inc(s["kt"], 1)
                turned(M0, 0).then_inc(s["qt"], 1)

            def prepare_top(b, u, h):
                gg = h // S
                if h == 0:
                    finished(pe, s["kT"], b)
                if h < SA:
                    finished(pe, s["qm"], b * SA + h)
                elif h < S:
                    finished(pe, s["qmv"], b * (S - SA) + h - SA)
                if not (isinstance(b, int) and b == 0 and h < 2):
                    finished(pe, s["mx"], b * NH + h - 2)
                for t in range(NT):
                    keys = (t + 1) * P if causal else N
                    last = pe.matmul(MB[h % 2][:, t * N:t * N + keys],
                                     lhsT=qm[:, u, gg, h % S, t * P:(t + 1) * P],
                                     rhs=kT[:, u, gg, 0:keys], start=True, stop=True)
                last.then_inc(s["top"], 1)

            def prepare_mt(b, half):
                finished(pe, s[("nlo0", "nlo1")[half]], b)
                if half == 1:
                    finished(pe, s["kT"], b + 1 if next1(b) else b)
                    if not next1(b):
                        finished(pe, s["x"], b - 2)
                elif isinstance(b, int) and b <= 1:
                    lanes_taken(0)
                    if b == 1:
                        finished(pe, s["raw"], 2)
                for t in range(NT):
                    last = turn(nc, (M0, M1)[half].bitcast(BF16)[0:2 * HN, t * P:(t + 1) * P],
                                minus[:, t, half * HN:(half + 1) * HN, :], identb[:, :])
                last.then_inc(s[("mt0", "mt1")[half]], 1)

            def scores(b, u, h):
                gg = h // S
                if h == 0:
                    pe.wait_ge(s["zeroq"], 1)
                    finished(pe, s["kT"], b)
                if h < SA:
                    finished(pe, s["qm"], b * SA + h)
                elif h < S:
                    finished(pe, s["qmv"], b * (S - SA) + h - SA)
                if not (isinstance(b, int) and b == 0 and h < NSB):
                    finished(pe, s["exp"], b * NH + h - NSB)
                if keep_max and h % HN == 0:
                    finished(pe, s[("mT0", "mT1")[h // HN]], b)
                for t in range(NT):
                    lo = t * P if causal else 0
                    at = N if t else 0
                    last = pe.matmul(SB[h % NSB][:, at:at + N - lo], lhsT=kT[:, u, gg, t * P:(t + 1) * P],
                                     rhs=qm[:, u, gg, h % S, lo:N], start=True, stop=not keep_max)
                    if keep_max:
                        last = pe.matmul(SB[h % NSB][:, at:at + N - lo], lhsT=sel[:, h % HN, :],
                                         rhs=mT[:, h // HN, lo:N], start=False, stop=True)
                last.then_inc(s["sc"], 1)

            def products(b, u, h):
                gg, lane = h // S, RW * (h % S)
                if h == 0:
                    finished(pe, s["oT0"], b - 1)
                    finished(pe, s["va"], b)
                if h == NH // 2:
                    finished(pe, s["oT1"], b - 1)
                finished(pe, s["tri" if causal else "exp"], b * NH + h)
                for t in range(NT):
                    lo = t * P if causal else 0
                    at = N if t else 0
                    last = pe.matmul(OB[lane:lane + RW, gg, lo:N], lhsT=va[:, u, t, h, :],
                                     rhs=prob[:, h % RING, at:at + N - lo], start=(t == 0), stop=(t == NT - 1),
                                     skip_group_check=causal)
                last.then_inc(s["pv"], 1)

            def complete_ot(b):
                finished(pe, s["oT1"], b)
                if isinstance(b, int) and b == B - 1:
                    finished(pe, s["x"], b - 1)
                elif isinstance(b, int) and b == B - 2:
                    if keep_max:
                        finished(pe, s["mT0"], b + 1)
                        finished(pe, s["mT1"], b + 1)
                    else:
                        finished(pe, s["x"], b - 1)
                else:
                    lanes_taken(b + 2)
                    finished(pe, s["mT1" if keep_max else "kT"], b + 1 if keep_max else b + 2)
                for h in range(NT):
                    for gg in range(G):
                        last = turn(nc, (M0, M1)[h][:, gg * P:(gg + 1) * P], oT[:, gg, h * P:(h + 1) * P], ident[:, :])
                last.then_inc(s["ot"], 1)

            def complete_yt(b):
                finished(pe, s["yd" if deflate else "y"], b)
                if not isinstance(b, int) or b + 3 < B:
                    finished(pe, s["raw"], b + 3)
                for h in range(NT):
                    last = turn(nc, M0[:, h * P:(h + 1) * P], y[:, h, :], ident[:, :])
                last.then_inc(s["yt"], 1)

            def complete_proj(b):
                finished(pe, s["yT"], b)
                for h in range(NT):
                    last = pe.matmul(M1[:, h * C:(h + 1) * C], lhsT=yT[:, h * P:(h + 1) * P], rhs=wo[:, :],
                                     start=True, stop=True)
                last.then_inc(s["proj"], 1)

            def step(b, u):
                for h in range(NH):
                    scores(b, u, h)
                    if h >= LAG:
                        products(b, u, h - LAG)
                    elif behind(b):
                        products(b - 1, 1 - u, NH + h - LAG)
                    if keep_max and h < TLAG:
                        prepare_top(b, u, NH - TLAG + h)
                    if keep_max and h >= TLAG and next1(b):
                        prepare_top(b + 1, 1 - u, h - TLAG)
                    if h == AT["turns"] and next1(b):
                        prepare_turns(b + 1)
                    if keep_max and h == AT["mt1"]:
                        prepare_mt(b, 1)
                    if h == AT["rt"] and next2(b):
                        prepare_rt(b + 2)
                    if h == AT["qkv"] and next2(b):
                        prepare_qkv(b + 2)
                    if behind(b):
                        if h == AT["ot"]:
                            complete_ot(b - 1)
                        if h == AT["yt"]:
                            complete_yt(b - 1)
                        if h == AT["proj"]:
                            complete_proj(b - 1)
                    if keep_max and h == AT["mt0"] and next1(b):
                        prepare_mt(b + 1, 0)

            prepare_rt(0)
            prepare_qkv(0)
            prepare_turns(0)
            if keep_max:
                for h in range(NH - TLAG):
                    prepare_top(0, 0, h)
                prepare_mt(0, 0)
            prepare_rt(1)
            prepare_qkv(1)
            every_step(pe, step)
            for h in range(NH - LAG, NH):
                products(B - 1, 1, h)
            complete_ot(B - 1)
            complete_yt(B - 1)
            complete_proj(B - 1)

        @block.scalar
        def _(act):
            act.preload_act_table_set("natural_log_exp_and_others")

            def prepare_rT(b):
                finished(act, s["rt"], b)
                act.activation(rT[:, :], M0[:, 0:N], ACT.Copy).then_inc(s["rT"], 1)

            def prepare_root(b):
                if norm_eps is not None:
                    finished(act, s["sse"], b)
                    act.activation(ln[:, :, :], ss[:, :, :], ACT.Ln).then_inc(s["ln"], 1)
                    finished(act, s["ln"], b)
                    act.activation(rn[:, :, :], ln[:, :, :], ACT.Exp, scale=-0.5).then_inc(s["root"], 1)

            def take_k(b, u):
                finished(act, s["kt"], b)
                act.activation(kT[:, u].rearrange("p g n -> p (g n)"), M1.bitcast(BF16), ACT.Copy).then_inc(s["kT"], 1)

            def take_max(b, half):
                finished(act, s[("mt0", "mt1")[half]], b)
                act.activation(mT[:, half, :], (M0, M1)[half].bitcast(BF16)[0:2 * HN, 0:N], ACT.Copy)\
                   .then_inc(s[("mT0", "mT1")[half]], 1)

            def take_lane(b, u, lane):
                if lane == 0:
                    act.wait_ge(s["zeroq"], 1)
                    finished(act, s["qt"], b)
                rows = slice(RW * lane, RW * (lane + 1))
                act.activation(qm[rows, u, :, lane, :], M0[rows, :].bitcast(BF16).rearrange("p (g n) -> p g n", n=N),
                               ACT.Copy).then_inc(s["qm"], 1)

            def exps(b, h):
                finished(act, s["sc"], b * NH + h)
                if not (isinstance(b, int) and b * NH + h < RING):
                    finished(act, s["pv"], b * NH + h - RING)
                act.activation(prob[:, h % RING, 0:n_prob], SB[h % NSB][:, 0:n_prob], ACT.Exp,
                               scale=scale).then_inc(s["exp"], 1)

            def complete_oT(b, half):
                if half == 0:
                    finished(act, s["ot"], b - 1)
                finished(act, s["pv"], b * NH + (half + 1) * NH // 2 - 1)
                part = slice(half * G // 2, (half + 1) * G // 2)
                act.activation(oT[:, part, :], OB[:, part, :], ACT.Copy).then_inc(s[("oT0", "oT1")[half]], 1)

            def complete_yT(b):
                finished(act, s["yt"], b)
                act.activation(yT[:, :], M0[:, 0:N], ACT.Copy).then_inc(s["yT"], 1)

            def step(b, u):
                for h in range(NH):
                    exps(b, h)
                    if h == AT["oT1"] and behind(b):
                        complete_oT(b - 1, 1)
                    if h == AT["turns"] and next1(b):
                        take_k(b + 1, 1 - u)
                    if keep_max and h == AT["mt1"]:
                        take_max(b, 1)
                    if AT["lanes"] <= h < AT["lanes"] + SA and next1(b):
                        take_lane(b + 1, 1 - u, h - AT["lanes"])
                    if h == AT["oT0"]:
                        complete_oT(b, 0)
                    if h == AT["rt"] and next2(b):
                        prepare_rT(b + 2)
                    if h == AT["root"] and next2(b):
                        prepare_root(b + 2)
                    if h == AT["yt"] and behind(b):
                        complete_yT(b - 1)
                    if keep_max and h == AT["mt0"] and next1(b):
                        take_max(b + 1, 0)

            prepare_rT(0)
            prepare_root(0)
            take_k(0, 0)
            for lane in range(SA):
                take_lane(0, 0, lane)
            if keep_max:
                take_max(0, 0)
            prepare_rT(1)
            prepare_root(1)
            every_step(act, step)
            complete_oT(B - 1, 1)
            complete_yT(B - 1)


def moe1_phase(nc, g, name):
    T4 = 4
    TG = T4 * P
    NG = B * N // TG
    with ExitStack() as ctx:
        s = semaphores(nc, ctx, name, "zero tick ptick rb1 cps cs tps vconst stats mv vareps rstd r nstats nmv nvareps nrstd n xr "
                                      "nt nT lg lgb mx d ex sum rsum p eq rank best hot1 q2 mx2 eq2 rank2 best2 hot2 "
                                      "both ws w1 rest w2 w3 wt wst wT init acc0 bc bcs up relu down t acc at x")

        def sb(nm, shape, dt=F32):
            return ctx.enter_context(nc.sbuf_tensor(name + nm, shape, dt))

        half = sb("half", [P, T4])
        eps = sb("eps", [P, T4])
        ones = sb("ones", [E, E])
        identb = sb("identb", [P, P], BF16)
        rowb = sb("rowb", [3 * E, E, P], BF16)
        rb1 = sb("rb1", [P, E, FJ, E])
        vconst = sb("vconst", [E, C])
        cs = sb("cs", [E, C])
        st = sb("st", [P, T4, 6])
        mv = sb("mv", [P, T4, 2])
        ve = sb("ve", [P, T4])
        rstd = sb("rstd", [P, T4])
        r = sb("r", [P, T4, C])
        n = sb("n", [P, T4, C])
        nT = sb("nT", [P, 2, TG])
        lg = sb("lg", [P, T4, E])
        pr = sb("pr", [P, T4, E])
        h1 = sb("h1", [P, T4, E])
        h2 = sb("h2", [P, T4, E])
        mx = sb("mx", [P, T4])
        ws = sb("ws", [P, T4, E])
        w3 = sb("w3", [P, T4, 3, E], BF16)
        wT = sb("wT", [E, TG])
        w3T = sb("w3T", [3 * E, 2, TG], BF16)
        hid = sb("hid", [P, 2, FJ, TG])
        bc = sb("bc", [P, 2, TG])
        tt = sb("tt", [P, 2, TG])
        acc = sb("acc", [P, 2, TG])
        X, ident, PS = g["X"], g["ident"], g["PS"]
        xg = X[:, :, :, :].rearrange("p (i s) h c -> p i (s h) c", s=T4 // NT)
        UP = [PS[:, j, :] for j in range(FJ)]
        DN = PS[:, 4, :]
        BC = PS[:, 5, :]
        M, M2 = PS[:, 6, :], PS[:, 7, :]
        first = g["first"][:, :].unsqueeze(1).broadcast_to([P, T4, E])
        block = ctx.enter_context(nc.Block())

        def rounds(prepare, step, eng):
            prepare(0, 0)
            with eng.Fori(0, NG // 2 - 1) as k:
                step(2 * k, 0, True)
                step(2 * k + 1, 1, True)
            step(NG - 2, 0, True)
            step(NG - 1, 1, False)

        @block.gpsimd
        def _(pool):
            pool.memset(half[:, :], -0.5).then_inc(s["zero"], 1)
            pool.memset(eps[:, :], LN_EPS).then_inc(s["zero"], 1)
            pool.memset(ones[:, :], 1.0).then_inc(s["zero"], 1)
            pool.memset(rb1[:, :, :, :], 0.0).then_inc(s["zero"], 1)
            pool.wait_ge(s["zero"], 4)
            pool.sem_inc(s["acc"], 2)

            def root(i, a, b, c):
                finished(pool, s[a], i)
                pool.tensor_tensor(ve[:, :], mv[:, :, 1], eps[:, :], ALU.add).then_inc(s[b], 1)
                finished(pool, s[b], i)
                pool.tensor_tensor(rstd[:, :], ve[:, :], half[:, :], ALU.pow).then_inc(s[c], 1)

            def prepare(i, u):
                root(i, "mv", "vareps", "rstd")
                root(i, "nmv", "nvareps", "nrstd")
                pool.tensor_tensor(xg[:, i], xg[:, i], r[:, :, :], ALU.add).then_inc(s["xr"], 1)

            def step(i, u, ahead):
                for e in range(E):
                    finished(pool, s["t"], i * E + e + 2)
                    if e:
                        finished(pool, s["acc"], i * E + e + 1)
                    else:
                        finished(pool, s["acc0"], i)
                    pool.tensor_tensor(acc[:, u, :], acc[:, u, :], tt[:, e % 2, :], ALU.add).then_inc(s["acc"], 1)
                    if e == 0 and ahead:
                        prepare(i + 1, 1 - u)

            rounds(prepare, step, pool)

        @block.vector
        def _(v):
            v.sem_inc(s["t"], 2)
            v.wait_ge(s["zero"], 4)
            v.tensor_copy(identb[:, :], ident[:, :]).then_inc(s["zero"], 1)
            v.tensor_copy(rowb[:, :, :], g["row3"][:, :, :]).then_inc(s["zero"], 1)
            for e in range(E):
                last = v.tensor_scalar(rb1[:, e, :, e], g["b1e"][:, e, :], 0.0, None, ALU.max)
            last.then_inc(s["rb1"], 1)
            finished(v, s["cps"], 0)
            v.tensor_tensor(cs[:, :], M[0:E, 0:C], g["b2e"][:, :], ALU.add).then_inc(s["cs"], 1)
            finished(v, s["cs"], 0)
            v.tensor_tensor(vconst[:, :], g["b2e"][:, :], cs[:, :], ALU.subtract).then_inc(s["cs"], 1)
            finished(v, s["cs"], 1)
            finished(v, s["tps"], 0)
            v.tensor_tensor(vconst[:, :], vconst[:, :], M2[0:E, 0:C], ALU.add).then_inc(s["vconst"], 1)

            def norm(i, src, dst, a, b, c, d):
                for t in range(T4):
                    last = v.bn_stats(st[:, t, :], src[:, t, :])
                last.then_inc(s[a], 1)
                held(v, s[a], i, s["tick"])
                for t in range(T4):
                    last = v.bn_aggr(mv[:, t, :], st[:, t, :])
                last.then_inc(s[b], 1)
                finished(v, s[c], i)
                for t in range(T4):
                    last = v.tensor_scalar(dst[:, t, :], src[:, t, :], mv[:, t, 0:1], rstd[:, t:t + 1],
                                           ALU.subtract, ALU.mult)
                last.then_inc(s[d], 1)

            def prepare_norm(i):
                norm(i, xg[:, i], r, "stats", "mv", "rstd", "r")
                finished(v, s["r"], i)
                norm(i, r, n, "nstats", "nmv", "nrstd", "n")

            def prepare_choice(i):
                def then(before, after, op):
                    finished(v, s[before], i)
                    op().then_inc(s[after], 1)

                bias = g["rb1"][:, :].unsqueeze(1).broadcast_to([P, T4, E])
                then("lg", "lgb", lambda: v.tensor_tensor(
                    lg[:, :, :], M2[:, 0:T4 * E].rearrange("p (t e) -> p t e", e=E), bias, ALU.add))
                then("lgb", "mx", lambda: v.tensor_reduce(mx[:, :], lg[:, :, :], AX.X, ALU.max))
                then("mx", "d", lambda: v.tensor_tensor(lg[:, :, :], lg[:, :, :], spread(mx[:, :], E), ALU.subtract))
                then("ex", "sum", lambda: v.tensor_reduce(mx[:, :], pr[:, :, :], AX.X, ALU.add))
                then("sum", "rsum", lambda: v.reciprocal(mx[:, :], mx[:, :]))
                then("rsum", "p", lambda: v.tensor_tensor(pr[:, :, :], pr[:, :, :], spread(mx[:, :], E), ALU.mult))
                then("p", "q2", lambda: v.tensor_reduce(mx[:, :], pr[:, :, :], AX.X, ALU.max))
                then("q2", "eq", lambda: v.tensor_tensor(h1[:, :, :], pr[:, :, :], spread(mx[:, :], E), ALU.is_equal))
                then("eq", "rank", lambda: v.tensor_tensor(h1[:, :, :], h1[:, :, :], first, ALU.mult))
                then("rank", "best", lambda: v.tensor_reduce(mx[:, :], h1[:, :, :], AX.X, ALU.max))
                then("best", "hot1", lambda: v.tensor_tensor(h1[:, :, :], h1[:, :, :], spread(mx[:, :], E),
                                                             ALU.is_equal))
                then("hot1", "rest", lambda: v.scalar_tensor_tensor(
                    out=ws[:, :, :], in0=h1[:, :, :], scalar=-2.0, in1=pr[:, :, :], op0=ALU.mult, op1=ALU.add))
                then("rest", "mx2", lambda: v.tensor_reduce(mx[:, :], ws[:, :, :], AX.X, ALU.max))
                then("mx2", "eq2", lambda: v.tensor_tensor(h2[:, :, :], ws[:, :, :], spread(mx[:, :], E),
                                                           ALU.is_equal))
                then("eq2", "rank2", lambda: v.tensor_tensor(h2[:, :, :], h2[:, :, :], first, ALU.mult))
                then("rank2", "best2", lambda: v.tensor_reduce(mx[:, :], h2[:, :, :], AX.X, ALU.max))
                then("best2", "hot2", lambda: v.tensor_tensor(h2[:, :, :], h2[:, :, :], spread(mx[:, :], E),
                                                              ALU.is_equal))
                then("hot2", "both", lambda: v.tensor_tensor(h1[:, :, :], h1[:, :, :], h2[:, :, :], ALU.add))
                then("both", "ws", lambda: v.tensor_tensor(ws[:, :, :], h1[:, :, :], pr[:, :, :], ALU.mult))
                then("ws", "w1", lambda: v.tensor_copy(w3[:, :, 0, :], ws[:, :, :]))
                then("w1", "w2", lambda: v.tensor_tensor(pr[:, :, :], ws[:, :, :], w3[:, :, 0, :], ALU.subtract))
                then("w2", "w3", lambda: v.tensor_copy(w3[:, :, 1, :], pr[:, :, :]))
                then("w3", "wt", lambda: v.tensor_tensor(w3[:, :, 2, :], pr[:, :, :], w3[:, :, 1, :], ALU.subtract))

            def weigh(i, u, e):
                finished(v, s["down"], i * E + e)
                v.wait_ge(s["acc"], i * E + e + 1)
                finished(v, s["bcs"], i * E + e + 1)
                v.tensor_tensor(tt[:, e % 2, :], DN, bc[:, e % 2, :], ALU.mult).then_inc(s["t"], 1)

            def complete(i):
                finished(v, s["at"], i)
                finished(v, s["xr"], i)
                v.tensor_tensor(xg[:, i], xg[:, i], M.rearrange("p (t c) -> p t c", c=C), ALU.add).then_inc(s["x"], 1)

            def prepare(i, u):
                prepare_norm(i)
                prepare_choice(i)

            def step(i, u, ahead):
                for e in range(E):
                    weigh(i, u, e)
                    if e == 0 and ahead:
                        prepare_norm(i + 1)
                    if e == 2 and ahead:
                        prepare_choice(i + 1)
                complete(i)

            rounds(prepare, step, v)

        @block.tensor
        def _(pe):
            pe.wait_ge(s["zero"], 6)
            finished(pe, s["rb1"], 0)
            for e in range(E):
                for j in range(FJ):
                    last = pe.matmul(M[0:E, 0:C], lhsT=rb1[:, e, j, :], rhs=g["W2e"][:, e, j, :],
                                     start=(e == 0 and j == 0), stop=(e == E - 1 and j == FJ - 1))
            last.then_inc(s["cps"], 1)
            finished(pe, s["cs"], 0)
            pe.matmul(M2[0:E, 0:C], lhsT=ones[:, :], rhs=cs[:, :], start=True, stop=True).then_inc(s["tps"], 1)
            finished(pe, s["vconst"], 0)

            def prepare_turn(i, u):
                finished(pe, s["n"], i)
                for t in range(T4):
                    last = turn(nc, M[:, t * P:(t + 1) * P], n[:, t, :], ident[:, :])
                last.then_inc(s["nt"], 1)

            def prepare_logits(i, u):
                finished(pe, s["nT"], i)
                for t in range(T4):
                    last = pe.matmul(M2[:, t * E:(t + 1) * E], lhsT=nT[:, u, t * P:(t + 1) * P], rhs=g["rw1"][:, :],
                                     start=True, stop=True)
                last.then_inc(s["lg"], 1)

            def prepare_weights(i, u):
                finished(pe, s["wt"], i)
                for t in range(T4):
                    last = turn(nc, M[0:E, t * P:(t + 1) * P], ws[:, t, :], ident[:, :])
                for t in range(T4):
                    last = turn(nc, M2.bitcast(BF16)[0:3 * E, t * P:(t + 1) * P], w3[:, t, :, :], identb[:, :])
                last.then_inc(s["wst"], 1)
                finished(pe, s["wT"], i)
                pe.matmul(M, lhsT=vconst[:, :], rhs=wT[:, :], start=True, stop=True).then_inc(s["init"], 1)

            def expert(i, u, e):
                if e == 0:
                    finished(pe, s["acc0"], i)
                for j in range(FJ):
                    pe.wait_ge(s["relu"], i * E * FJ + e * FJ + j + 1)
                    pe.matmul(UP[j], lhsT=g["W1e"][:, e, j * P:(j + 1) * P], rhs=nT[:, u, :],
                              start=True, stop=True).then_inc(s["up"], 1)
                pe.wait_ge(s["bcs"], i * E + e + 1)
                pe.matmul(BC, lhsT=rowb[:, e, :], rhs=w3T[:, u, :], start=True, stop=True).then_inc(s["bc"], 1)

            def expert_out(i, u, e):
                pe.wait_ge(s["t"], i * E + e + 2)
                for j in range(FJ):
                    pe.wait_ge(s["relu"], i * E * FJ + e * FJ + j + 1 + FJ)
                    last = pe.matmul(DN, lhsT=g["W2e"][:, e, j, :], rhs=hid[:, e % 2, j, :],
                                     start=(j == 0), stop=(j == FJ - 1))
                last.then_inc(s["down"], 1)

            def complete(i, u):
                finished(pe, s["acc"], i * E + E + 1)
                for t in range(T4):
                    last = turn(nc, M[:, t * P:(t + 1) * P], acc[:, u, t * P:(t + 1) * P], ident[:, :])
                last.then_inc(s["at"], 1)

            def prepare(i, u):
                prepare_turn(i, u)
                prepare_logits(i, u)
                prepare_weights(i, u)

            def step(i, u, ahead):
                expert(i, u, 0)
                for e in range(E):
                    if e < E - 1:
                        expert(i, u, e + 1)
                    expert_out(i, u, e)
                    if ahead and e == 1:
                        prepare_turn(i + 1, 1 - u)
                    if ahead and e == 2:
                        prepare_logits(i + 1, 1 - u)
                    if ahead and e == 5:
                        prepare_weights(i + 1, 1 - u)
                if ahead:
                    finished(pe, s["acc0"], i + 1)
                complete(i, u)

            rounds(prepare, step, pe)

        @block.scalar
        def _(act):
            act.sem_inc(s["relu"], FJ)
            act.sem_inc(s["bcs"], 1)

            def prepare_nT(i, u):
                finished(act, s["nt"], i)
                act.activation(nT[:, u, :], M, ACT.Identity, bias=g["beta"][:, 0:1],
                               scale=g["gamma"][:, 0:1]).then_inc(s["nT"], 1)

            def prepare_exp(i, u):
                finished(act, s["d"], i)
                act.activation(pr[:, :, :], lg[:, :, :], ACT.Exp).then_inc(s["ex"], 1)

            def prepare_wT(i, u):
                finished(act, s["wst"], i)
                act.activation(wT[:, :], M[0:E, :], ACT.Copy)
                act.activation(w3T[:, u, :], M2.bitcast(BF16)[0:3 * E, 0:TG], ACT.Copy).then_inc(s["wT"], 1)
                finished(act, s["init"], i)
                act.activation(acc[:, u, :], M, ACT.Copy).then_inc(s["acc0"], 1)

            def expert(i, u, e):
                for j in range(FJ):
                    finished(act, s["up"], i * E * FJ + e * FJ + j)
                    act.activation(hid[:, e % 2, j, :], UP[j], ACT.Relu, bias=g["b1e"][:, e, j:j + 1])\
                       .then_inc(s["relu"], 1)
                finished(act, s["bc"], i * E + e)
                act.wait_ge(s["t"], i * E + e + 1)
                act.activation(bc[:, e % 2, :], BC, ACT.Copy).then_inc(s["bcs"], 1)

            def prepare(i, u):
                prepare_nT(i, u)
                prepare_exp(i, u)
                prepare_wT(i, u)

            def step(i, u, ahead):
                for e in range(E):
                    expert(i, u, e)
                    if ahead and e == 2:
                        prepare_nT(i + 1, 1 - u)
                    if ahead and e == 3:
                        prepare_exp(i + 1, 1 - u)
                    if ahead and e == 6:
                        prepare_wT(i + 1, 1 - u)

            rounds(prepare, step, act)


def build(nc, d, out):
    with ExitStack() as ctx:
        def sb(name, shape, dt=F32):
            return ctx.enter_context(nc.sbuf_tensor(name, shape, dt))

        g = {"x_dram": d["x"]}
        g["X"] = sb("X", [P, B, NT, C])
        g["HT"] = sb("HT", [P, B, N])
        g["PS"] = ctx.enter_context(nc.psum_tensor("PS", [P, 8, 512], F32))
        g["first_loads"], g["loads"] = [], []

        def const(name, shape, first=False):
            g[name] = sb("k_" + name, shape)
            full = g[name][tuple(slice(None) for _ in shape)]
            g["first_loads" if first else "loads"].append((full, d[name]))

        const("ident", [P, P], True)
        const("conv1_w", [P, MULT * TAPS], True)
        const("conv1_b", [P, MULT], True)
        const("conv2_w", [P, MULT * TAPS], True)
        for n in ("conv2_b", "ln0_g", "ln0_b"):
            const(n, [P, 1], True)
        for n, shape in LATER.items():
            const(n, list(shape))
        if "conv" in PHASES:
            conv_phase(nc, g)
        if "lin" in PHASES:
            linear_phase(nc, g)
        if "ffn" in PHASES:
            ffn_phase(nc, g)
        if "moe0a" in PHASES:
            moe0_phase(nc, g, "m0a")
        if "at0" in PHASES:
            attention_phase(nc, g, "a0", norm_eps=1.1920928955078125e-07, scale=HD ** -0.5, deflate=True)
        if "moe0b" in PHASES:
            moe0_phase(nc, g, "m0b")
        if "at1" in PHASES:
            attention_phase(nc, g, "a1", scale=HD ** -0.5, bias=True, causal=True, keep_max=True)
        if "moe1a" in PHASES:
            moe1_phase(nc, g, "m1a")
        if "at2" in PHASES:
            attention_phase(nc, g, "a2", norm_eps=1e-6, weights=True, bias=True, keep_max=True)
        if "moe1b" in PHASES:
            moe1_phase(nc, g, "m1b")
        s_out = ctx.enter_context(nc.semaphore("stored"))
        block = ctx.enter_context(nc.Block())

        @block.sync
        def _(sp):
            sp.dma_start(out.rearrange("b (h p) c -> p b h c", p=P), g["X"][:, :, :, :]).then_inc(s_out, 16)
            sp.wait_ge(s_out, 16)


LATER = {
    "Wq": (P, L, C), "Wkv": (P, L, 2 * C), "bq": (P, L), "bkv": (P, L, 2 * C), "lnA_g": (P, L), "lnA_b": (P, L),
    "head_mask": (P, C), "pair_turn": (P, C), "cosT": (P, NT, C), "sinT": (P, NT, C), "cosF": (P, N), "sinF": (P, N),
    "W1": (P, FF), "b1": (P, FJ), "W2": (P, FJ, C), "b2": (P, 1), "ln2_g": (P, C), "ln2_b": (P, C),
    "rw0": (P, E), "rb0": (P, E), "ew0": (P, E, C), "eb0": (E, C), "first": (P, E),
    "a0_wqkv": (P, 3 * C), "a0_wo": (P, C),
    "a1_wqkv": (P, 3 * C), "a1_wo": (P, C), "a1_bqkv": (P, 3 * C), "a1_bo": (P, C), "tri": (P, NT, N),
    "a2_wqkv": (P, 3 * C), "a2_wo": (P, C), "a2_bqkv": (P, 3 * C), "a2_bo": (P, C), "a2_wn": (P, 2 * C),
    "gamma": (P, 1), "beta": (P, 1), "rw1": (P, E), "rb1": (P, E), "W1e": (P, E, FF), "b1e": (P, E, FJ),
    "W2e": (P, E, FJ, C), "b2e": (E, C), "row3": (3 * E, E, P),
}
PHASES = ("conv", "lin", "ffn", "moe0a", "at0", "moe0b", "at1", "moe1a", "at2", "moe1b")


def tables():
    t = {}
    t["ident"] = np.eye(P, dtype=np.float32)
    c = np.arange(C)
    t["head_mask"] = (c[:, None] // HD == c[None, :] // HD).astype(np.float32)
    m = np.zeros((C, C), np.float32)
    m[0::2, 1::2] = -np.eye(C // 2)
    m[1::2, 0::2] = np.eye(C // 2)
    t["pair_turn"] = m
    inv = np.float32(1.0) / np.float32(10000.0) ** (np.arange(0, C, 2, dtype=np.float32) / np.float32(C))
    freqs = np.repeat(np.arange(N, dtype=np.float32)[:, None] * inv[None, :].astype(np.float32), 2, axis=-1)
    cos, sin = np.cos(freqs).astype(np.float32), np.sin(freqs).astype(np.float32)
    t["cosF"], t["sinF"] = np.ascontiguousarray(cos.T), np.ascontiguousarray(sin.T)
    sign = np.where(c % 2 == 0, -1.0, 1.0).astype(np.float32)
    t["cosT"] = np.ascontiguousarray(cos.reshape(NT, P, C).transpose(1, 0, 2))
    t["sinT"] = np.ascontiguousarray((sin * sign).reshape(NT, P, C).transpose(1, 0, 2))
    t["first"] = np.tile(np.arange(E, 0, -1, dtype=np.float32), (P, 1))
    q = np.arange(N).reshape(NT, P).transpose(1, 0)
    t["tri"] = np.where(np.arange(N)[None, None, :] <= q[:, :, None], 0.0, -3e38).astype(np.float32)
    row = np.zeros((E, E, P), np.float32)
    row[np.arange(E), np.arange(E)] = 1.0
    t["row3"] = np.concatenate([row] * 3)
    return t


def laid_out(i):
    a = {}

    def every(v):
        return np.tile(np.asarray(v).reshape(1, -1), (P, 1))

    def column(v):
        return np.asarray(v).reshape(-1, P).T

    p = "L0_attn_a_"
    a["x"] = i[p + "x"]
    a["conv1_w"] = i[p + "conv1_w"].reshape(P, MULT * TAPS)
    a["conv1_b"] = i[p + "conv1_b"].reshape(P, MULT)
    a["conv2_w"] = i[p + "conv2_w"].reshape(P, MULT * TAPS)
    for n in ("conv2_b", "ln0_g", "ln0_b", "b2"):
        a[n] = column(i[p + n])
    a["Wq"] = i[p + "Wq"].transpose(1, 0, 2)
    a["Wkv"] = np.concatenate([i[p + "Wk"], i[p + "Wv"]], axis=2).transpose(1, 0, 2)
    a["bkv"] = np.tile(np.concatenate([i[p + "bk"], i[p + "bv"]], axis=1)[None], (P, 1, 1))
    for n in ("bq", "lnA_g", "lnA_b"):
        a[n] = i[p + n].T
    a["W1"], a["b1"] = i[p + "W1"], column(i[p + "b1"])
    a["W2"] = i[p + "W2"].reshape(FJ, P, C).transpose(1, 0, 2)
    a["ln2_g"], a["ln2_b"] = every(i[p + "ln2_g"]), every(i[p + "ln2_b"])
    p = "L0_ffn_"
    a["rw0"], a["rb0"] = i[p + "router_w"].T, every(i[p + "router_b"])
    a["ew0"], a["eb0"] = i[p + "expert_w"].transpose(2, 0, 1), i[p + "expert_b"]
    a["a0_wqkv"], a["a0_wo"] = i["L0_attn_b_w_qkv"].T, i["L0_attn_b_w_proj"].T
    p = "L1_attn_a_"
    a["a1_wqkv"], a["a1_wo"] = i[p + "Wqkv"], i[p + "Wo"]
    a["a1_bqkv"], a["a1_bo"] = every(i[p + "bqkv"]), every(i[p + "bo"])
    p = "L1_attn_b_"
    a["a2_wqkv"], a["a2_wo"] = i[p + "Wqkv"].T, i[p + "Wo"].T
    a["a2_bqkv"], a["a2_bo"] = every(i[p + "bqkv"]), every(i[p + "bo"])
    a["a2_wn"] = every(np.concatenate([np.tile(i[p + "wq"], NH), np.tile(i[p + "wk"], NH)]))
    p = "L1_ffn_"
    a["gamma"], a["beta"] = column(i[p + "gamma"]), column(i[p + "beta"])
    a["rw1"], a["rb1"] = i[p + "Wr"], every(i[p + "br"])
    a["W1e"] = i[p + "W1"].transpose(1, 0, 2)
    a["b1e"] = i[p + "b1"].reshape(E, FJ, P).transpose(2, 0, 1)
    a["W2e"] = i[p + "W2"].reshape(E, FJ, P, C).transpose(2, 0, 1, 3)
    a["b2e"] = i[p + "b2"]
    return a


def kernel(**inputs):
    from concourse import bacc
    from concourse.bass_utils import run_bass_kernel_spmd

    nc = bacc.Bacc("TRN2", target_bir_lowering=False, num_devices=1)
    arrays = {**laid_out({k: np.asarray(v) for k, v in inputs.items()}), **tables()}
    arrays = {k: np.ascontiguousarray(v) for k, v in arrays.items()}
    d = {k: nc.dram_tensor("in_" + k, v.shape, mybir.dt.from_np(v.dtype), kind="ExternalInput").ap()
         for k, v in arrays.items()}
    out = nc.dram_tensor("out_x", (B, N, C), F32, kind="ExternalOutput").ap()
    build(nc, d, out)
    r = run_bass_kernel_spmd(nc, [{"in_" + k: v for k, v in arrays.items()}], core_ids=[0])
    return r.results[0]["out_x"]
```

```python
from contextlib import ExitStack

import numpy as np

import concourse.bass as bass
from concourse import mybir

F32 = mybir.dt.float32
BF16 = mybir.dt.bfloat16
ALU = mybir.AluOpType
ACT = mybir.ActivationFunctionType
AX = mybir.AxisListType

P = 128
B = 16
N = 256
NT = N // P
C = 128
NH = 16
HD = C // NH
L = 4
TAPS = 5
PAD = TAPS // 2
MULT = 4
FF = 512
FJ = FF // P
E = 8
GELU_SHIFT = 0.21
LN_EPS = 1e-5
LN_EPS_A = 1e-12




def semaphores(nc, ctx, prefix, names):
    sems = {n: nc.alloc_semaphore(f"{prefix}_{n}") for n in names.split()}

    def clear():
        nc.clear_and_free_semaphores(list(sems.values()))
        nc.all_engine_barrier()

    ctx.callback(clear)
    return sems


def finished(eng, sem, n):
    if isinstance(n, int) and n < 0:
        return
    eng.wait_ge(sem, n + 1)


def held(eng, sem, n, tick):
    if isinstance(n, int) and n < 0:
        return
    finished(eng, sem, n)
    eng.sem_inc(tick, 1)


def turn(nc, out, in_, ident):
    return nc.tensor.matmul(out, lhsT=in_, rhs=ident, start=True, stop=True, is_transpose=True)


def spread(ap, n):
    return ap.unsqueeze(len(ap.shape)).broadcast_to([*ap.shape, n])


def column(t, l):
    return t[:, :].rearrange("p (l o) -> p l o", o=1)[:, l, :]


def conv_phase(nc, g):
    U = 2
    steps = B // U
    taps = MULT * TAPS
    VT = taps - TAPS
    with ExitStack() as ctx:
        s = semaphores(nc, ctx, "cv", "x_first x_rest w later tick diag1 zero stats mv vareps rstd r rt rT c1 gl tap ptick atick wg ptap yt "
                                      "stats2 mv2 vareps2 rstd2 un unt h")

        def sb(name, shape, dt=F32):
            return ctx.enter_context(nc.sbuf_tensor("cv_" + name, shape, dt))

        st = sb("st", [P, 2, U, NT, 6])
        mv = sb("mv", [P, 2, U, NT, 2])
        ve = sb("ve", [P, 2, U, NT])
        rstd = sb("rstd", [P, 2, U, NT])
        r = sb("r", [P, 2, U, NT, C])
        rT = sb("rT", [P, 2, U, N + 2 * PAD])
        gl = sb("gl", [P, 2, U, MULT, N + 2 * PAD])
        y = sb("y", [P, U, N])
        z = sb("z", [P, U, N])
        wg = sb("wg", [P, U, TAPS, N])
        diag = sb("diag", [P, taps, C])
        half = sb("half", [P, NT])
        eps = sb("eps", [P, 2, NT])
        X, HT, ident, PS = g["X"], g["HT"], g["ident"], g["PS"]
        block = ctx.enter_context(nc.Block())
        bank_r = [PS[:, 3 * u, :] for u in range(U)]
        bank_c = [PS[:, 3 * u + 1:3 * u + 3, :].rearrange("p b (j n) -> p (b j) n", n=N) for u in range(U)]
        bank_y = [PS[:, 6 + u, :] for u in range(U)]

        def rounds(eng, step):
            step(0, 0, True, True)
            with eng.Fori(0, steps // 2 - 2) as k:
                step(2 * k + 1, 1, True, True)
                step(2 * k + 2, 0, True, True)
            step(steps - 3, 1, True, True)
            step(steps - 2, 0, True, False)
            step(steps - 1, 1, False, False)

        @block.sync
        def _(sp):
            for dst, src in g["first_loads"]:
                sp.dma_start(dst, src).then_inc(s["w"], 16)
            xd = g["x_dram"].rearrange("b (h p) c -> p b h c", p=P)
            sp.dma_start(X[:, 0:2 * U], xd[:, 0:2 * U]).then_inc(s["x_first"], 16)
            for q in range(1, 4):
                sp.dma_start(X[:, 4 * q:4 * q + 4], xd[:, 4 * q:4 * q + 4]).then_inc(s["x_rest"], 16)
            for dst, src in g["loads"]:
                sp.dma_start(dst, src).then_inc(s["later"], 16)
            sp.wait_ge(s["later"], 16 * len(g["loads"]))

        @block.gpsimd
        def _(pool):
            pool.memset(half[:, :], -0.5).then_inc(s["zero"], 1)
            pool.memset(eps[:, 0, :], LN_EPS).then_inc(s["zero"], 1)
            pool.memset(eps[:, 1, :], LN_EPS_A).then_inc(s["zero"], 1)
            pool.memset(rT[:, :, :, :], 0.0).then_inc(s["zero"], 1)
            pool.memset(gl[:, :, :, :, :], 0.0).then_inc(s["zero"], 1)
            pool.wait_ge(s["zero"], 5)

            def root(i, m):
                a, b, c = (("mv", "vareps", "rstd"), ("mv2", "vareps2", "rstd2"))[m]
                for u in range(U):
                    pool.wait_ge(s[a], i * U + u + 1)
                    pool.tensor_tensor(ve[:, m, u, :], mv[:, m, u, :, 1], eps[:, m, :], ALU.add).then_inc(s[b], 1)
                for u in range(U):
                    pool.wait_ge(s[b], i * U + u + 1)
                    pool.tensor_tensor(rstd[:, m, u, :], ve[:, m, u, :], half[:, :], ALU.pow).then_inc(s[c], 1)

            def conv2_last(i, par):
                held(pool, s["tap"], i * (U * (VT + 1)) - 1, s["ptick"])
                for t in range(VT, taps):
                    for u in range(U):
                        if t == VT:
                            held(pool, s["wg"], i * U + u, s["ptick"])
                        else:
                            pool.wait_ge(s["ptap"], (i * TAPS + t - VT - 1) * U + u + 1)
                        pool.tensor_tensor(z[:, u, :], rT[:, par, u, PAD:PAD + N] if t == VT else z[:, u, :],
                                           wg[:, u, t - VT, :], ALU.add).then_inc(s["ptap"], 1)

            def step(i, par, next1, next2):
                if next2:
                    root(i + 2, 0)
                conv2_last(i, par)
                root(i, 1)

            root(0, 0)
            root(1, 0)
            rounds(pool, step)

        @block.vector
        def _(v):
            v.wait_ge(s["w"], 16 * len(g["first_loads"]))
            for t in range(MULT * TAPS):
                d = v.tensor_scalar(diag[:, t, :], ident[:, :], g["conv1_w"][:, t:t + 1], None, ALU.mult)
            d.then_inc(s["diag1"], 1)
            v.wait_ge(s["x_first"], 16)
            v.wait_ge(s["zero"], 5)

            def norm_stats(i, m, src):
                stats, mvs = (("stats", "mv"), ("stats2", "mv2"))[m]
                for u in range(U):
                    for h in range(NT):
                        last = v.bn_stats(st[:, m, u, h, :], src(u, h))
                    last.then_inc(s[stats], 1)
                for u in range(U):
                    held(v, s[stats], i * U + u, s["tick"])
                    for h in range(NT):
                        last = v.bn_aggr(mv[:, m, u, h, :], st[:, m, u, h, :])
                    last.then_inc(s[mvs], 1)

            def norm_apply(i, m, src):
                rs, done = (("rstd", "r"), ("rstd2", "un"))[m]
                for u in range(U):
                    finished(v, s[("rt", "unt")[m]], (i - 1) * U + u)
                    v.wait_ge(s[rs], i * U + u + 1)
                    for h in range(NT):
                        last = v.tensor_scalar(r[:, m, u, h, :], src(u, h), mv[:, m, u, h, 0:1],
                                               rstd[:, m, u, h:h + 1], ALU.subtract, ALU.mult)
                    last.then_inc(s[done], 1)

            xv = X[:, :, :, :].rearrange("p (i u) h c -> p i u h c", u=U)

            def x_of(i):
                return lambda u, h: xv[:, i, u, h, :]

            def y_of(u, h):
                return bank_y[u][:, h * C:(h + 1) * C]

            def conv2(i, par, next2):
                for t in range(VT + 1):
                    if t == VT // 2 and next2:
                        norm_apply(i + 2, 0, x_of(i + 2))
                    for u in range(U):
                        if t:
                            v.wait_ge(s["tap"], i * (U * (VT + 1)) + (t - 1) * U + u + 1)
                        else:
                            v.wait_ge(s["gl"], i * U + u + 1)
                        if t < VT:
                            src = gl[:, par, u, t // TAPS, t % TAPS:t % TAPS + N]
                            w = g["conv2_w"][:, t:t + 1]
                        if t == 0:
                            op = v.tensor_scalar(y[:, u, :], src, w, g["conv2_b"][:, 0:1], ALU.mult, ALU.add)
                        elif t < VT:
                            op = v.scalar_tensor_tensor(out=y[:, u, :], in0=src, scalar=w, in1=y[:, u, :],
                                                        op0=ALU.mult, op1=ALU.add)
                        else:
                            v.wait_ge(s["ptap"], (i * TAPS + TAPS - 1) * U + u + 1)
                            op = v.tensor_tensor(y[:, u, :], y[:, u, :], z[:, u, :], ALU.add)
                        op.then_inc(s["tap"], 1)

            def step(i, par, next1, next2):
                if next2:
                    norm_stats(i + 2, 0, x_of(i + 2))
                conv2(i, par, next2)
                for u in range(U):
                    v.wait_ge(s["yt"], i * U + u + 1)
                norm_stats(i, 1, y_of)
                norm_apply(i, 1, y_of)

            for i in range(2):
                norm_stats(i, 0, x_of(i))
                norm_apply(i, 0, x_of(i))
            v.wait_ge(s["x_rest"], 48)
            rounds(v, step)

        @block.tensor
        def _(pe):
            pe.wait_ge(s["w"], 16 * len(g["first_loads"]))
            pe.wait_ge(s["diag1"], 1)

            def turn_r(i):
                for u in range(U):
                    pe.wait_ge(s["r"], i * U + u + 1)
                    finished(pe, s["rT"], (i - 1) * U + u)
                    for h in range(NT):
                        last = turn(nc, bank_r[u][:, h * P:(h + 1) * P], r[:, 0, u, h, :], ident[:, :])
                    last.then_inc(s["rt"], 1)

            def conv1(i, par, u):
                pe.wait_ge(s["rT"], i * U + u + 1)
                finished(pe, s["gl"], (i - 1) * U + u)
                for j in range(MULT):
                    for k in range(TAPS):
                        last = pe.matmul(bank_c[u][:, j, :], lhsT=diag[:, j * TAPS + k, :],
                                         rhs=rT[:, par, u, k:k + N], start=(k == 0), stop=(k == TAPS - 1))
                last.then_inc(s["c1"], 1)

            def turn_y(i):
                for u in range(U):
                    pe.wait_ge(s["tap"], i * (U * (VT + 1)) + VT * U + u + 1)
                    finished(pe, s["h"], (i - 1) * U + u)
                    for h in range(NT):
                        last = turn(nc, bank_y[u][:, h * P:(h + 1) * P], y[:, u, h * P:(h + 1) * P], ident[:, :])
                    last.then_inc(s["yt"], 1)

            def turn_back(i):
                for u in range(U):
                    pe.wait_ge(s["un"], i * U + u + 1)
                    for h in range(NT):
                        last = turn(nc, bank_y[u][:, h * P:(h + 1) * P], r[:, 1, u, h, :], ident[:, :])
                    last.then_inc(s["unt"], 1)

            def step(i, par, next1, next2):
                if next1:
                    conv1(i + 1, 1 - par, 0)
                if not isinstance(i, int) or i > 0:
                    turn_back(i - 1)
                if next1:
                    conv1(i + 1, 1 - par, 1)
                if next2:
                    turn_r(i + 2)
                turn_y(i)

            turn_r(0)
            for u in range(U):
                conv1(0, 0, u)
            turn_r(1)
            rounds(pe, step)
            turn_back(steps - 1)

        @block.scalar
        def _(act):
            act.preload_act_table_set("gelu_and_others")
            act.wait_ge(s["w"], 16 * len(g["first_loads"]))
            act.wait_ge(s["zero"], 5)
            hv = HT[:, :, :].rearrange("p (i u) n -> p i u n", u=U)

            def take_r(i, par):
                held(act, s["ptap"], (i - 1) * (TAPS * U) - 1, s["atick"])
                for u in range(U):
                    act.wait_ge(s["rt"], i * U + u + 1)
                    act.activation(rT[:, par, u, PAD:PAD + N], bank_r[u][:, 0:N], ACT.Copy).then_inc(s["rT"], 1)

            def hidden(i, par, u):
                finished(act, s["tap"], (i - 1) * (U * (VT + 1)) - 1)
                act.wait_ge(s["c1"], i * U + u + 1)
                for j in range(MULT):
                    last = act.activation(gl[:, par, u, j, PAD:PAD + N], bank_c[u][:, j, :], ACT.Gelu,
                                          bias=g["conv1_b"][:, j:j + 1])
                last.then_inc(s["gl"], 1)

            def weigh_last(i, par, u):
                act.wait_ge(s["gl"], i * U + u + 1)
                finished(act, s["ptap"], (i * TAPS - 1) * U + u)
                for t in range(TAPS):
                    last = act.activation(wg[:, u, t, :], gl[:, par, u, MULT - 1, t:t + N], ACT.Identity,
                                          scale=g["conv2_w"][:, VT + t:VT + t + 1])
                last.then_inc(s["wg"], 1)

            def save(i):
                for u in range(U):
                    held(act, s["unt"], i * U + u, s["atick"])
                    act.activation(hv[:, i, u, :], bank_y[u][:, 0:N], ACT.Identity, bias=g["ln0_b"][:, 0:1],
                                   scale=g["ln0_g"][:, 0:1]).then_inc(s["h"], 1)

            def step(i, par, next1, next2):
                if next1:
                    hidden(i + 1, 1 - par, 0)
                if not isinstance(i, int) or i > 0:
                    save(i - 1)
                if next1:
                    hidden(i + 1, 1 - par, 1)
                if next2:
                    take_r(i + 2, par)
                if next1:
                    for u in range(U):
                        weigh_last(i + 1, 1 - par, u)

            take_r(0, 0)
            for u in range(U):
                hidden(0, 0, u)
                weigh_last(0, 0, u)
            take_r(1, 1)
            rounds(act, step)
            save(steps - 1)


def linear_phase(nc, g):
    U = 4
    steps = B // U
    with ExitStack() as ctx:
        stages = ("h proj kv q qs k kc ks ksum kvm kmean km kvbd den kv2 kv2s dens z qc qsn out yz y stats mv vareps "
                  "rstd un unt").split()
        s = semaphores(nc, ctx, "la", "zero tick atick ptick load0 load1 save0 save1 " +
                       " ".join(f"{n}{p}" for n in stages for p in range(2)))

        def sb(name, shape, dt=F32):
            return ctx.enter_context(nc.sbuf_tensor("la_" + name, shape, dt))

        half = sb("half", [P, 2, NT])
        eps = sb("eps", [P, 2, NT])
        ones = sb("ones", [P, 1])
        h = sb("h", [P, U, N])
        q = sb("q", [P, U, N])
        kv = sb("kv", [P, U, NT, 2 * C])
        k = sb("k", [P, U, NT, C])
        kc = sb("kc", [P, U, NT, C])
        ks = sb("ks", [P, U, NT, C])
        kmean = sb("kmean", [P, U, 1])
        km = sb("km", [P, U, NH])
        kvbd = sb("kvbd", [P, U, C])
        kv2 = sb("kv2", [P, U, C])
        z = sb("z", [P, U, NT * NH])
        y = sb("y", [P, U, NT, C])
        un = sb("un", [P, U, NT, C])
        qc = sb("qc", [P, U, N])
        qs = sb("qs", [P, U, N])
        st = sb("st", [P, U, NT, 6])
        mv = sb("mv", [P, U, NT, 2])
        ve = sb("ve", [P, U, NT])
        rstd = sb("rstd", [P, U, NT])
        HT, ident, PS = g["HT"], g["ident"], g["PS"]
        hv = HT[:, :, :].rearrange("p (i u) n -> p i u n", u=U)
        A = [PS[:, 2 * u, :] for u in range(U)]
        D = [PS[:, 2 * u + 1, :] for u in range(U)]
        block = ctx.enter_context(nc.Block())

        def pair(p):
            return (2 * p, 2 * p + 1)

        def done(eng, stage, n, u):
            finished(eng, s[f"{stage}{u // 2}"], n * 2 + u % 2)

        def done_held(eng, stage, n, u, tick):
            held(eng, s[f"{stage}{u // 2}"], n * 2 + u % 2, s[tick])

        def sem(stage, u):
            return s[f"{stage}{u // 2}"]

        def rounds(half_round, begin=None, end=None, eng=None):
            def group(i):
                for l in range(L):
                    n = i * L + l
                    if l == 0 and begin:
                        begin(i, 0)
                    first = isinstance(n, int) and n == 0
                    half_round((n, l, 0), None if first else (n - 1, (l - 1) % L, 1))
                    if l == 0 and end and not first:
                        end(i - 1, 1)
                    if l == 0 and begin:
                        begin(i, 1)
                    half_round((n, l, 1), (n, l, 0))
                    if l == L - 1 and end:
                        end(i, 0)

            group(0)
            with eng.Fori(1, steps) as i:
                group(i)
            half_round(None, (steps * L - 1, L - 1, 1))
            if end:
                end(steps - 1, 1)

        @block.gpsimd
        def _(pool):
            pool.memset(half[:, :, :], -0.5).then_inc(s["zero"], 1)
            pool.memset(eps[:, :, :], LN_EPS_A).then_inc(s["zero"], 1)
            pool.memset(ones[:, :], 1.0).then_inc(s["zero"], 1)
            pool.wait_ge(s["zero"], 3)

            def half_round(front, back):
                if front:
                    n, l, p = front
                    a, b = pair(p)
                    pool.wait_ge(sem("qs", b), n * 2 + b % 2 + 1)
                    pool.tensor_tensor(qc[:, a:b + 1, :], q[:, a:b + 1, :],
                                       g["cosF"][:, :].unsqueeze(1).broadcast_to([P, 2, N]),
                                       ALU.mult).then_inc(sem("qc", a), 2)
                if back:
                    m, l, p = back
                    a, b = pair(p)
                    pool.wait_ge(sem("mv", b), m * 2 + b % 2 + 1)
                    pool.tensor_tensor(ve[:, a:b + 1, :], mv[:, a:b + 1, :, 1], eps[:, :, :], ALU.add)\
                        .then_inc(sem("vareps", a), 2)
                    pool.wait_ge(sem("vareps", b), m * 2 + b % 2 + 1)
                    pool.tensor_tensor(rstd[:, a:b + 1, :], ve[:, a:b + 1, :], half[:, :, :], ALU.pow)\
                        .then_inc(sem("rstd", a), 2)
                if front:
                    n, l, p = front
                    a, b = pair(p)
                    pool.tensor_tensor(qs[:, a:b + 1, :], q[:, a:b + 1, :],
                                       g["sinF"][:, :].unsqueeze(1).broadcast_to([P, 2, N]),
                                       ALU.mult).then_inc(sem("qsn", a), 2)

            rounds(half_round, eng=pool)

        @block.vector
        def _(v):
            v.wait_ge(s["zero"], 3)

            def half_round(front, back):
                if back:
                    n, l, p = back
                    for u in pair(p):
                        v.wait_ge(sem("dens", u), n * 2 + u % 2 + 1)
                        v.reciprocal(z[:, u, :], z[:, u, :]).then_inc(sem("z", u), 1)
                if front:
                    n, l, p = front
                    bias = g["bkv"][:, l, :].unsqueeze(1).broadcast_to([P, NT, 2 * C])
                    for u in pair(p):
                        v.wait_ge(sem("proj", u), n * 2 + u % 2 + 1)
                        v.tensor_tensor(kv[:, u], A[u].rearrange("p (h c) -> p h c", h=NT), bias,
                                        ALU.add).then_inc(sem("kv", u), 1)
                if back:
                    n, l, p = back
                    for u in pair(p):
                        v.wait_ge(sem("out", u), n * 2 + u % 2 + 1)
                        v.wait_ge(sem("z", u), n * 2 + u % 2 + 1)
                        v.tensor_tensor(y[:, u].rearrange("p h (n d) -> p (h n) d", d=HD),
                                        A[u][:, 0:N].rearrange("p (n d) -> p n d", d=HD),
                                        spread(z[:, u, :], HD), ALU.mult).then_inc(sem("yz", u), 1)
                    for u in pair(p):
                        v.wait_ge(sem("yz", u), n * 2 + u % 2 + 1)
                        yu = y[:, u].rearrange("p h c -> p (h c)")
                        v.tensor_tensor(yu, D[u][:, 0:N], yu, ALU.add).then_inc(sem("y", u), 1)
                if front:
                    n, l, p = front
                    for u in pair(p):
                        v.wait_ge(sem("k", u), n * 2 + u % 2 + 1)
                        v.scalar_tensor_tensor(out=kc[:, u], in0=k[:, u], scalar=GELU_SHIFT, in1=g["cosT"][:, :, :],
                                               op0=ALU.add, op1=ALU.mult)
                        for par in range(2):
                            a = [t.rearrange("p h (c t) -> p h c t", t=2) for t in (ks[:, u], k[:, u], g["sinT"][:, :, :])]
                            last = v.scalar_tensor_tensor(out=a[0][:, :, :, par], in0=a[1][:, :, :, 1 - par],
                                                          scalar=GELU_SHIFT, in1=a[2][:, :, :, par],
                                                          op0=ALU.add, op1=ALU.mult)
                        last.then_inc(sem("ks", u), 1)
                if back:
                    n, l, p = back
                    for u in pair(p):
                        v.wait_ge(sem("y", u), n * 2 + u % 2 + 1)
                        for t in range(NT):
                            last = v.bn_stats(st[:, u, t, :], y[:, u, t, :])
                        last.then_inc(sem("stats", u), 1)
                    for u in pair(p):
                        done_held(v, "stats", n, u, "tick")
                        for t in range(NT):
                            last = v.bn_aggr(mv[:, u, t, :], st[:, u, t, :])
                        last.then_inc(sem("mv", u), 1)
                if front:
                    n, l, p = front
                    for u in pair(p):
                        v.wait_ge(sem("ksum", u), n * 2 + u % 2 + 1)
                        v.tensor_scalar(kmean[:, u, :], D[u][:, N:N + 1], 1.0 / N, GELU_SHIFT, ALU.mult,
                                        ALU.add).then_inc(sem("kmean", u), 1)
                    for u in pair(p):
                        v.wait_ge(sem("kmean", u), n * 2 + u % 2 + 1)
                        v.tensor_scalar(km[:, u, :], g["head_mask"][:, 0:C:HD], kmean[:, u, :], None,
                                        ALU.mult).then_inc(sem("km", u), 1)
                    for u in pair(p):
                        v.wait_ge(sem("kvm", u), n * 2 + u % 2 + 1)
                        v.scalar_tensor_tensor(out=kvbd[:, u, :], in0=A[u][:, 0:C], scalar=1.0 / N, in1=g["head_mask"][:, :],
                                               op0=ALU.mult, op1=ALU.mult).then_inc(sem("kvbd", u), 1)
                if back:
                    n, l, p = back
                    for u in pair(p):
                        v.wait_ge(sem("rstd", u), n * 2 + u % 2 + 1)
                        for t in range(NT):
                            last = v.tensor_scalar(un[:, u, t, :], y[:, u, t, :], mv[:, u, t, 0:1],
                                                   rstd[:, u, t:t + 1], ALU.subtract, ALU.mult)
                        last.then_inc(sem("un", u), 1)

            rounds(half_round, eng=v)

        @block.tensor
        def _(pe):
            pe.wait_ge(s["zero"], 3)

            def half_round(front, back):
                if back:
                    n, l, p = back
                    for u in pair(p):
                        pe.wait_ge(sem("kvbd", u), n * 2 + u % 2 + 1)
                        pe.matmul(A[u][:, C:2 * C], lhsT=g["pair_turn"][:, :], rhs=kvbd[:, u, :], start=True, stop=True)\
                          .then_inc(sem("kv2", u), 1)
                if front:
                    n, l, p = front
                    for u in pair(p):
                        if l == 0:
                            finished(pe, s[f"load{p}"], (n // L if isinstance(n, int) else group_of[0]) * 2 + u % 2)
                        done(pe, "h", n - 1, u)
                        pe.matmul(D[u][:, 0:N], lhsT=g["Wq"][:, l, :], rhs=h[:, u, :], start=True, stop=True)
                        for t in range(NT):
                            last = pe.matmul(A[u][:, t * 2 * C:(t + 1) * 2 * C], lhsT=h[:, u, t * P:(t + 1) * P],
                                             rhs=g["Wkv"][:, l, :], start=True, stop=True)
                        last.then_inc(sem("proj", u), 1)
                if back:
                    n, l, p = back
                    for u in pair(p):
                        pe.wait_ge(sem("qc", u), n * 2 + u % 2 + 1)
                        pe.wait_ge(sem("qsn", u), n * 2 + u % 2 + 1)
                        pe.wait_ge(sem("kv2s", u), n * 2 + u % 2 + 1)
                        for t in range(NT):
                            part, tok = A[u][:, t * C:(t + 1) * C], slice(t * P, (t + 1) * P)
                            pe.matmul(part, lhsT=qc[:, u, tok], rhs=kvbd[:, u, :], start=True, stop=False)
                            last = pe.matmul(part, lhsT=qs[:, u, tok], rhs=kv2[:, u, :], start=False, stop=True)
                        last.then_inc(sem("out", u), 1)
                if front:
                    n, l, p = front
                    for u in pair(p):
                        pe.wait_ge(sem("k", u), n * 2 + u % 2 + 1)
                        pe.wait_ge(sem("q", u), n * 2 + u % 2 + 1)
                        for t in range(NT):
                            pe.matmul(D[u][:, N:N + 1], lhsT=k[:, u, t, :], rhs=ones[:, :],
                                      start=(t == 0), stop=(t == NT - 1))
                        for t in range(NT):
                            last = turn(nc, D[u][:, t * P:(t + 1) * P], h[:, u, t * P:(t + 1) * P], ident[:, :])
                        last.then_inc(sem("ksum", u), 1)
                    for u in pair(p):
                        pe.wait_ge(sem("ks", u), n * 2 + u % 2 + 1)
                        for j, part in enumerate((kc, ks)):
                            for t in range(NT):
                                last = pe.matmul(A[u][:, 0:C], lhsT=part[:, u, t, :], rhs=kv[:, u, t, C:2 * C],
                                                 start=(j == 0 and t == 0), stop=(j == 1 and t == NT - 1))
                        last.then_inc(sem("kvm", u), 1)
                    for u in pair(p):
                        pe.wait_ge(sem("km", u), n * 2 + u % 2 + 1)
                        pe.wait_ge(sem("qs", u), n * 2 + u % 2 + 1)
                        for t in range(NT):
                            last = pe.matmul(D[u][:, N + 1 + t * NH:N + 1 + (t + 1) * NH], lhsT=q[:, u, t * P:(t + 1) * P],
                                             rhs=km[:, u, :], start=True, stop=True)
                        last.then_inc(sem("den", u), 1)
                if back:
                    n, l, p = back
                    for u in pair(p):
                        pe.wait_ge(sem("un", u), n * 2 + u % 2 + 1)
                        for t in range(NT):
                            last = turn(nc, A[u][:, t * P:(t + 1) * P], un[:, u, t, :], ident[:, :])
                        last.then_inc(sem("unt", u), 1)

            group_of = [0]

            def begin(i, p):
                group_of[0] = i

            rounds(half_round, begin, eng=pe)

        @block.scalar
        def _(act):
            act.preload_act_table_set("gelu_and_others")

            def begin(i, p):
                for u in pair(p):
                    held(act, s[f"save{p}"], (i - 1) * 2 + u % 2, s["atick"])
                    act.activation(h[:, u, :], hv[:, i, u, :], ACT.Copy).then_inc(s[f"load{p}"], 1)

            def half_round(front, back):
                if back:
                    n, l, p = back
                    for u in pair(p):
                        act.wait_ge(sem("kv2", u), n * 2 + u % 2 + 1)
                        act.activation(kv2[:, u, :], A[u][:, C:2 * C], ACT.Copy).then_inc(sem("kv2s", u), 1)
                if front:
                    n, l, p = front
                    for u in pair(p):
                        act.wait_ge(sem("proj", u), n * 2 + u % 2 + 1)
                        act.activation(q[:, u, :], D[u][:, 0:N], ACT.Gelu, bias=g["bq"][:, l:l + 1])\
                           .then_inc(sem("q", u), 1)
                    for u in pair(p):
                        act.wait_ge(sem("kv", u), n * 2 + u % 2 + 1)
                        act.activation(k[:, u], kv[:, u, :, 0:C], ACT.Gelu).then_inc(sem("k", u), 1)
                    for u in pair(p):
                        act.wait_ge(sem("q", u), n * 2 + u % 2 + 1)
                        act.activation(q[:, u, :], q[:, u, :], ACT.Copy, bias=GELU_SHIFT).then_inc(sem("qs", u), 1)
                    for u in pair(p):
                        act.wait_ge(sem("den", u), n * 2 + u % 2 + 1)
                        act.activation(z[:, u, :], D[u][:, N + 1:N + 1 + NT * NH], ACT.Copy, bias=1e-6)\
                           .then_inc(sem("dens", u), 1)
                if back:
                    n, l, p = back
                    for u in pair(p):
                        act.wait_ge(sem("unt", u), n * 2 + u % 2 + 1)
                        act.activation(h[:, u, :], A[u][:, 0:N], ACT.Identity, bias=g["lnA_b"][:, l:l + 1],
                                       scale=g["lnA_g"][:, l:l + 1]).then_inc(sem("h", u), 1)

            def end(i, p):
                for u in pair(p):
                    held(act, s[f"h{p}"], (i + 1) * (L * 2) - 2 + u % 2, s["atick"])
                    act.activation(hv[:, i, u, :], h[:, u, :], ACT.Copy).then_inc(s[f"save{p}"], 1)

            rounds(half_round, begin, end, act)


def ffn_phase(nc, g):
    U = 2
    steps = B // U
    with ExitStack() as ctx:
        s = semaphores(nc, ctx, "ff", "zero tick atick h0 up gl down y yt stats mv vareps rstd un ug ub x")

        def sb(name, shape, dt=F32):
            return ctx.enter_context(nc.sbuf_tensor("ff_" + name, shape, dt))

        half = sb("half", [P, U, NT])
        eps = sb("eps", [P, U, NT])
        h = sb("h", [P, 2, U, N])
        gl = sb("gl", [P, 2, U, FJ, N])
        y = sb("y", [P, U, N])
        un = sb("un", [P, U, NT, C])
        st = sb("st", [P, U, NT, 6])
        mv = sb("mv", [P, U, NT, 2])
        ve = sb("ve", [P, U, NT])
        rstd = sb("rstd", [P, U, NT])
        X, HT, ident, PS = g["X"], g["HT"], g["ident"], g["PS"]
        hv = HT[:, :, :].rearrange("p (i u) n -> p i u n", u=U)
        xv = X[:, :, :, :].rearrange("p (i u) h c -> p i u h c", u=U)
        up = [PS[:, 4 * u:4 * u + 2, :].rearrange("p b (j n) -> p (b j) n", n=N) for u in range(U)]
        D = [PS[:, 4 * u + 2, :] for u in range(U)]
        T = [PS[:, 4 * u + 3, :] for u in range(U)]
        gain = g["ln2_g"][:, :].unsqueeze(1).broadcast_to([P, U * NT, C])
        shift = g["ln2_b"][:, :].unsqueeze(1).broadcast_to([P, U * NT, C])
        block = ctx.enter_context(nc.Block())

        def rounds(eng, step):
            step(0, 0, True, True)
            with eng.Fori(0, steps // 2 - 2) as k:
                step(2 * k + 1, 1, True, True)
                step(2 * k + 2, 0, True, True)
            step(steps - 3, 1, True, True)
            step(steps - 2, 0, True, False)
            step(steps - 1, 1, False, False)

        @block.gpsimd
        def _(pool):
            pool.memset(half[:, :, :], -0.5).then_inc(s["zero"], 1)
            pool.memset(eps[:, :, :], LN_EPS_A).then_inc(s["zero"], 1)
            pool.wait_ge(s["zero"], 2)

            def step(i, par, next1, next2):
                pool.wait_ge(s["mv"], i + 1)
                pool.tensor_tensor(ve[:, :, :], mv[:, :, :, 1], eps[:, :, :], ALU.add).then_inc(s["vareps"], 1)
                pool.wait_ge(s["vareps"], i + 1)
                pool.tensor_tensor(rstd[:, :, :], ve[:, :, :], half[:, :, :], ALU.pow).then_inc(s["rstd"], 1)
                all_un = un[:, :, :, :].rearrange("p u h c -> p (u h) c")
                pool.wait_ge(s["un"], i + 1)
                pool.tensor_tensor(all_un, all_un, gain, ALU.mult).then_inc(s["ug"], 1)

            rounds(pool, step)

        @block.vector
        def _(v):
            def step(i, par, next1, next2):
                for u in range(U):
                    v.wait_ge(s["down"], i * U + u + 1)
                    v.scalar_tensor_tensor(out=y[:, u, :], in0=D[u][:, 0:N], scalar=g["b2"][:, 0:1],
                                           in1=h[:, par, u, :], op0=ALU.add, op1=ALU.add).then_inc(s["y"], 1)
                for u in range(U):
                    v.wait_ge(s["yt"], i * U + u + 1)
                    for t in range(NT):
                        last = v.bn_stats(st[:, u, t, :], T[u][:, t * C:(t + 1) * C])
                last.then_inc(s["stats"], 1)
                held(v, s["stats"], i, s["tick"])
                for u in range(U):
                    for t in range(NT):
                        last = v.bn_aggr(mv[:, u, t, :], st[:, u, t, :])
                last.then_inc(s["mv"], 1)
                xi = xv[:, i].rearrange("p u h c -> p (u h) c")
                v.tensor_tensor(xi, xi, shift, ALU.add).then_inc(s["ub"], 1)
                v.wait_ge(s["rstd"], i + 1)
                for u in range(U):
                    for t in range(NT):
                        last = v.tensor_scalar(un[:, u, t, :], T[u][:, t * C:(t + 1) * C], mv[:, u, t, 0:1],
                                               rstd[:, u, t:t + 1], ALU.subtract, ALU.mult)
                last.then_inc(s["un"], 1)
                v.wait_ge(s["ug"], i + 1)
                v.wait_ge(s["ub"], i + 1)
                v.tensor_tensor(xi, xi, un[:, :, :, :].rearrange("p u h c -> p (u h) c"), ALU.add).then_inc(s["x"], 1)

            rounds(v, step)

        @block.tensor
        def _(pe):
            def first(i, par, u):
                pe.wait_ge(s["h0"], i * U + u + 1)
                finished(pe, s["gl"], (i - 1) * U + u)
                for j in range(FJ):
                    last = pe.matmul(up[u][:, j, :], lhsT=g["W1"][:, j * P:(j + 1) * P], rhs=h[:, par, u, :],
                                     start=True, stop=True)
                last.then_inc(s["up"], 1)

            def second(i, par, u):
                pe.wait_ge(s["gl"], i * U + u + 1)
                for j in range(FJ):
                    last = pe.matmul(D[u][:, 0:N], lhsT=g["W2"][:, j, :], rhs=gl[:, par, u, j, :],
                                     start=(j == 0), stop=(j == FJ - 1))
                last.then_inc(s["down"], 1)

            def step(i, par, next1, next2):
                for u in range(U):
                    if next1:
                        first(i + 1, 1 - par, u)
                    second(i, par, u)
                finished(pe, s["un"], i - 1)
                for u in range(U):
                    pe.wait_ge(s["y"], i * U + u + 1)
                    for t in range(NT):
                        last = turn(nc, T[u][:, t * P:(t + 1) * P], y[:, u, t * P:(t + 1) * P], ident[:, :])
                    last.then_inc(s["yt"], 1)

            for u in range(U):
                first(0, 0, u)
            rounds(pe, step)

        @block.scalar
        def _(act):
            act.preload_act_table_set("gelu_and_others")

            def load(i, par):
                held(act, s["y"], (i - 1) * U - 1, s["atick"])
                for u in range(U):
                    act.activation(h[:, par, u, :], hv[:, i, u, :], ACT.Copy).then_inc(s["h0"], 1)

            def hidden(i, par):
                for u in range(U):
                    act.wait_ge(s["up"], i * U + u + 1)
                    for j in range(FJ):
                        last = act.activation(gl[:, par, u, j, :], up[u][:, j, :], ACT.Gelu, bias=g["b1"][:, j:j + 1])
                    last.then_inc(s["gl"], 1)

            def step(i, par, next1, next2):
                if next1:
                    hidden(i + 1, 1 - par)
                if next2:
                    load(i + 2, par)

            load(0, 0)
            load(1, 1)
            hidden(0, 0)
            rounds(act, step)


def moe0_phase(nc, g, name):
    U = 2
    steps = B // U
    EB = E // 2
    SLICES = NT * EB
    BIAS_AT = 4
    SLOT = (0, 1, 2, 4, 5, 6, 8, 10)
    with ExitStack() as ctx:
        s = semaphores(nc, ctx, name, "zero tick stats mv vareps rstd r rt rT lg lgb mx d eq rank best hot sum ex w ws wst "
                                      "wsT bias bx acc all side ptick part added")

        def sb(nm, shape, dt=F32):
            return ctx.enter_context(nc.sbuf_tensor(name + nm, shape, dt))

        half = sb("half", [P, U, NT])
        eps = sb("eps", [P, U, NT])
        st = sb("st", [P, U, NT, 6])
        mv = sb("mv", [P, U, NT, 2])
        ve = sb("ve", [P, U, NT])
        rstd = sb("rstd", [P, U, NT])
        r = sb("r", [P, U, NT, C])
        rT = sb("rT", [P, 2, U, N])
        lg = sb("lg", [P, U, NT, E])
        mx = sb("mx", [P, U, NT])
        dd = sb("dd", [P, U, NT, E])
        hot = sb("hot", [P, 2, U, NT, E])
        w = sb("w", [P, U, NT])
        wsT = sb("wsT", [E, U, N])
        side = sb("side", [P, 2, EB, U, NT, C])
        X, ident, PS = g["X"], g["ident"], g["PS"]
        xv = X[:, :, :, :].rearrange("p (i u) h c -> p i u h c", u=U)
        T = [PS[:, 4 * u, :] for u in range(U)]
        R = [PS[:, 4 * u + 1, :] for u in range(U)]
        Y = [PS[:, 4 * u + 2:4 * u + 4, :] for u in range(U)]
        first = g["first"][:, :].unsqueeze(1).broadcast_to([P, U * NT, E])
        block = ctx.enter_context(nc.Block())

        def rounds(eng, prepare, step):
            prepare(0, 0)
            step(0, 0, True)
            with eng.Fori(0, steps // 2 - 1) as k:
                step(2 * k + 1, 1, True)
                step(2 * k + 2, 0, True)
            step(steps - 1, 1, False)

        def tiles(t):
            return t.rearrange("p u h e -> p (u h) e") if len(t.shape) == 4 else t.rearrange("p u h -> p (u h)")

        @block.gpsimd
        def _(pool):
            pool.memset(half[:, :, :], -0.5).then_inc(s["zero"], 1)
            pool.memset(eps[:, :, :], LN_EPS).then_inc(s["zero"], 1)
            pool.wait_ge(s["zero"], 2)

            def prepare(i, par):
                pool.wait_ge(s["mv"], i + 1)
                pool.tensor_tensor(ve[:, :, :], mv[:, :, :, 1], eps[:, :, :], ALU.add).then_inc(s["vareps"], 1)
                pool.wait_ge(s["vareps"], i + 1)
                pool.tensor_tensor(rstd[:, :, :], ve[:, :, :], half[:, :, :], ALU.pow).then_inc(s["rstd"], 1)

            def complete(i, par):
                pool.wait_ge(s["acc"], (i + 1) * SLICES * U)
                pool.wait_ge(s["side"], (i + 1) * NT * U * EB)
                for m in range(EB):
                    if m:
                        pool.wait_ge(s["part"], i * (EB - 1) + m)
                    pool.sem_inc(s["ptick"], 1)
                    last = pool.tensor_tensor(xv[:, i], xv[:, i], side[:, par, m], ALU.add)
                    last.then_inc(s["part" if m < EB - 1 else "added"], 1)

            def step(i, par, ahead):
                if ahead:
                    prepare(i + 1, 1 - par)
                if not isinstance(i, int) or i > 0:
                    complete(i - 1, 1 - par)

            rounds(pool, prepare, step)
            complete(steps - 1, 1)

        @block.vector
        def _(v):
            def prepare(i, par, add_last_bias=lambda: None, beside=lambda k: None):
                def each(op):
                    for u in range(U):
                        for h in range(NT):
                            last = op(u, h)
                    return last

                ht = tiles(hot[:, par])
                lt, dt, mt, wt = tiles(lg[:, :, :, :]), tiles(dd[:, :, :, :]), tiles(mx[:, :, :]), tiles(w[:, :, :])
                each(lambda u, h: v.bn_stats(st[:, u, h, :], xv[:, i, u, h, :])).then_inc(s["stats"], 1)
                held(v, s["stats"], i, s["tick"])
                each(lambda u, h: v.bn_aggr(mv[:, u, h, :], st[:, u, h, :])).then_inc(s["mv"], 1)
                beside(0)
                beside(1)
                beside(2)
                beside(3)
                finished(v, s["rt"], i - 1)
                v.wait_ge(s["rstd"], i + 1)
                each(lambda u, h: v.tensor_scalar(r[:, u, h, :], xv[:, i, u, h, :], mv[:, u, h, 0:1], rstd[:, u, h:h + 1],
                                                 ALU.subtract, ALU.mult)).then_inc(s["r"], 1)
                beside(4)
                add_last_bias()
                beside(5)
                beside(6)
                beside(7)
                beside(8)
                bias = g["rb0"][:, :].unsqueeze(1).broadcast_to([P, NT, E])
                v.wait_ge(s["lg"], i + 1)
                for u in range(U):
                    last = v.tensor_tensor(lg[:, u], R[u][:, 0:NT * E].rearrange("p (h e) -> p h e", e=E), bias, ALU.add)
                last.then_inc(s["lgb"], 1)
                v.wait_ge(s["lgb"], i + 1)
                v.tensor_reduce(mt, lt, AX.X, ALU.max).then_inc(s["mx"], 1)
                v.wait_ge(s["mx"], i + 1)
                v.tensor_tensor(dt, lt, spread(mt, E), ALU.subtract).then_inc(s["d"], 1)
                finished(v, s["side"], (i - 1) * NT * U * EB - 1)
                v.wait_ge(s["d"], i + 1)
                v.tensor_tensor(ht, lt, spread(mt, E), ALU.is_equal).then_inc(s["eq"], 1)
                beside(9)
                v.wait_ge(s["eq"], i + 1)
                v.tensor_tensor(ht, ht, first, ALU.mult).then_inc(s["rank"], 1)
                beside(10)
                v.wait_ge(s["rank"], i + 1)
                v.tensor_reduce(mt, ht, AX.X, ALU.max).then_inc(s["best"], 1)
                v.wait_ge(s["ex"], i + 1)
                v.tensor_reduce(wt, dt, AX.X, ALU.add).then_inc(s["sum"], 1)
                beside(11)
                v.wait_ge(s["best"], i + 1)
                v.tensor_tensor(ht, ht, spread(mt, E), ALU.is_equal).then_inc(s["hot"], 1)
                v.wait_ge(s["sum"], i + 1)
                v.reciprocal(wt, wt).then_inc(s["w"], 1)
                beside(12)
                v.wait_ge(s["hot"], i + 1)
                v.wait_ge(s["w"], i + 1)
                v.tensor_tensor(ht, ht, spread(wt, E), ALU.mult).then_inc(s["ws"], 1)
                beside(13)
                beside(14)
                beside(15)

            def add_bias(i):
                v.wait_ge(s["bias"], i + 1)
                v.wait_ge(s["acc"], (i * SLICES + BIAS_AT) * U)
                for u in range(U):
                    last = v.tensor_tensor(xv[:, i, u], xv[:, i, u],
                                           R[u][:, 256:512].rearrange("p (h c) -> p h c", h=NT), ALU.add)
                last.then_inc(s["bx"], 1)

            def add(i, par, k):
                h, e = divmod(k, EB)
                if k == 0:
                    v.wait_ge(s["ws"], i + 1)
                for u in range(U):
                    if e == 0:
                        v.wait_ge(s["all"], (i * NT + h) * 2 * U + u + 1)
                    if k == BIAS_AT:
                        v.wait_ge(s["bx"], i + 1)
                    if e > 0:
                        finished(v, s["acc"], (i * SLICES + k - 1) * U + u)
                    v.scalar_tensor_tensor(
                        out=xv[:, i, u, h, :], in0=Y[u][:, 0, e * C:(e + 1) * C],
                        scalar=hot[:, par, u, h, e:e + 1], in1=xv[:, i, u, h, :], op0=ALU.mult,
                        op1=ALU.add).then_inc(s["acc"], 1)

            def slot(i, par, k):
                for j in range(SLICES):
                    if SLOT[j] == k:
                        add(i, par, j)

            def step(i, par, ahead):
                if ahead:
                    prepare(i + 1, 1 - par, lambda: add_bias(i), lambda k: slot(i, par, k))
                else:
                    for k in range(SLICES):
                        if k == BIAS_AT:
                            add_bias(i)
                        add(i, par, k)

            rounds(v, prepare, step)

        @block.tensor
        def _(pe):
            def turn_r(i, par):
                pe.wait_ge(s["r"], i + 1)
                finished(pe, s["wsT"], i - 1)
                for u in range(U):
                    for h in range(NT):
                        last = turn(nc, T[u][:, h * P:(h + 1) * P], r[:, u, h, :], ident[:, :])
                last.then_inc(s["rt"], 1)

            def prepare_logits(i, par):
                pe.wait_ge(s["rT"], i + 1)
                finished(pe, s["bx"], i - 1)
                for u in range(U):
                    for h in range(NT):
                        last = pe.matmul(R[u][:, h * E:(h + 1) * E], lhsT=rT[:, par, u, h * P:(h + 1) * P],
                                         rhs=g["rw0"][:, :], start=True, stop=True)
                last.then_inc(s["lg"], 1)

            def turn_hot(i, par):
                pe.wait_ge(s["ws"], i + 1)
                for u in range(U):
                    for t in range(NT):
                        last = turn(nc, T[u][0:E, t * P:(t + 1) * P], hot[:, par, u, t, :], ident[:, :])
                last.then_inc(s["wst"], 1)

            def prepare_bias(i):
                pe.wait_ge(s["wsT"], i + 1)
                for u in range(U):
                    for t in range(NT):
                        last = pe.matmul(R[u][:, 256 + t * C:256 + (t + 1) * C], lhsT=wsT[:, u, t * P:(t + 1) * P],
                                         rhs=g["eb0"][:, :], start=True, stop=True)
                last.then_inc(s["bias"], 1)

            def products(i, par, h, b):
                for u in range(U):
                    if b == 0:
                        finished(pe, s["acc"], ((i * NT + h) * EB - 1) * U + u)
                    else:
                        finished(pe, s["side"], ((i * NT + h - 1) * U + u + 1) * EB - 1)
                    pe.matmul(Y[u][:, b, :], lhsT=rT[:, par, u, h * P:(h + 1) * P],
                              rhs=g["ew0"][:, EB * b:EB * (b + 1), :], start=True, stop=True).then_inc(s["all"], 1)

            def prepare(i, par):
                turn_r(i, par)
                prepare_logits(i, par)
                products(i, par, 0, 0)
                turn_hot(i, par)
                products(i, par, 0, 1)

            def step(i, par, ahead):
                prepare_bias(i)
                if ahead:
                    turn_r(i + 1, 1 - par)
                products(i, par, 1, 0)
                if ahead:
                    prepare_logits(i + 1, 1 - par)
                products(i, par, 1, 1)
                if ahead:
                    products(i + 1, 1 - par, 0, 0)
                    turn_hot(i + 1, 1 - par)
                    products(i + 1, 1 - par, 0, 1)

            rounds(pe, prepare, step)

        @block.scalar
        def _(act):
            def prepare_rT(i, par):
                act.wait_ge(s["rt"], i + 1)
                for u in range(U):
                    last = act.activation(rT[:, par, u, :], T[u][:, 0:N], ACT.Copy)
                last.then_inc(s["rT"], 1)

            def prepare_exp(i):
                act.wait_ge(s["d"], i + 1)
                act.activation(dd[:, :, :, :], dd[:, :, :, :], ACT.Exp).then_inc(s["ex"], 1)

            def prepare_wsT(i):
                act.wait_ge(s["wst"], i + 1)
                finished(act, s["bias"], i - 1)
                for u in range(U):
                    last = act.activation(wsT[:, u, :], T[u][0:E, 0:N], ACT.Copy)
                last.then_inc(s["wsT"], 1)

            def prepare(i, par):
                prepare_rT(i, par)
                prepare_exp(i)
                prepare_wsT(i)

            def weigh(i, par, h):
                for u in range(U):
                    act.wait_ge(s["all"], ((i * NT + h) * 2 + 1) * U + u + 1)
                    for e in range(EB):
                        act.activation(side[:, par, e, u, h, :], Y[u][:, 1, e * C:(e + 1) * C], ACT.Copy,
                                       scale=hot[:, par, u, h, EB + e:EB + e + 1]).then_inc(s["side"], 1)

            def step(i, par, ahead):
                act.wait_ge(s["ws"], i + 1)
                finished(act, s["added"], i - 2)
                weigh(i, par, 0)
                if ahead:
                    prepare_rT(i + 1, 1 - par)
                    prepare_exp(i + 1)
                weigh(i, par, 1)
                if ahead:
                    prepare_wsT(i + 1)

            rounds(act, prepare, step)


def attention_phase(nc, g, name, scale=1.0, norm_eps=None, weights=False, bias=False, causal=False, keep_max=False,
                    deflate=False):
    G = 4
    S = NH // G
    RW = 32
    RING = 8
    NEG = -3e38
    if not keep_max:
        AT = {"unit": 1, "hi": 1, "lo": 2, "oT1": 3, "stats": 4, "aggr": 4, "lanes": 4, "r": 4, "turns": 5, "ot": 8,
              "y": 9, "dot": 10, "rt": 10, "qkv": 11, "oT0": 11, "yd": 12, "va": 12, "raw": 12, "yt": 13, "sq": 14,
              "ss": 14, "root": 14, "proj": 15, "x": 15}
        LAG, SA = 4, 1
    elif causal:
        AT = {"hi": 1, "lo": 2, "oT1": 3, "stats": 3, "aggr": 3, "turns": 4, "lanes": 4, "minus1": 5, "r": 5,
              "mt1": 6, "xb": 6, "ot": 8, "y": 8, "va": 8, "rt": 9, "qkv": 11, "oT0": 11, "raw": 11, "yt": 13,
              "minus0": 13, "proj": 14, "mt0": 14, "x": 15}
        LAG, SA = 4, 2
    else:
        AT = {"unit": 0, "wn": 1, "hi": 2, "lo": 2, "oT1": 3, "stats": 3, "aggr": 3, "turns": 4, "lanes": 4,
              "minus1": 5, "mt1": 6, "r": 6, "xb": 7, "y": 9, "ot": 10, "va": 11, "rt": 11, "oT0": 11, "qkv": 12,
              "raw": 12, "sq": 12, "yt": 13, "minus0": 13, "ss": 13, "proj": 14, "root": 15, "x": 15, "mt0": 15}
        LAG, SA = 3, 2
    TLAG = 6
    HN = NH // 2

    n_prob = NT * N - (P if causal else 0)
    with ExitStack() as ctx:
        s = semaphores(nc, ctx, name, "zero zeroq tick ptick stats mv vareps rstd r rt rT qkv0 qkv1 raw sq ss sse ln root nw rn unit wn hi lo "
                                      " qt kt kT qm qmv mt0 mt1 mT0 mT1 nwa nwb nwc top mx nhi0 nhi1 nlo0 nlo1 sc exp tri pv oT0 oT1 ot den y va t1 t2 t3 yd yt yT "
                                      "proj xb x")

        def sb(nm, shape, dt=F32):
            return ctx.enter_context(nc.sbuf_tensor(name + nm, shape, dt))

        half = sb("half", [P, NT])
        eps = sb("eps", [P, NT])
        st = sb("st", [P, NT, 6])
        mv = sb("mv", [P, NT, 2])
        ve = sb("ve", [P, NT])
        rstd = sb("rstd", [P, NT])
        r = sb("r", [P, NT, C])
        rT = sb("rT", [P, N])
        identb = sb("identb", [P, P], BF16)
        qk = sb("qk", [P, NT, 2 * C])
        sq = sb("sq", [P, NT, 2 * C])
        ss = sb("ss", [P, NT, 2 * NH])
        rn = sb("rn", [P, NT, 2 * NH])
        ln = sb("ln", [P, NT, 2 * NH])
        nw = sb("nw", [P, NT, 2 * NH])
        parts = sb("parts", [P, NT, 2, NH, RW], BF16)
        qm = sb("qm", [P, 2, G, S, N], BF16)
        kT = sb("kT", [P, 2, G, N], BF16)
        va = sb("va", [P, 2, NT, NH, RW])
        mx = sb("mx", [P, NT, NH])
        minus = sb("minus", [P, NT, NH, 2], BF16)
        mT = sb("mT", [2 * HN, 2, N], BF16)
        sel = sb("sel", [2 * HN, HN, P], BF16)
        prob = sb("prob", [P, RING, NT * N])
        oT = sb("oT", [P, G, N])
        den = sb("den", [P, NT, NH])
        y = sb("y", [P, NT, C])
        t = sb("t", [P, NT, C])
        dot = sb("dot", [P, NT, NH])
        vv = sb("vv", [P, NT, NH])
        yT = sb("yT", [P, N])
        vs = sb("vs", [P, 2, NT, C])
        junk = sb("junk", [P, 2 * NT, N])
        X, ident, PS = g["X"], g["ident"], g["PS"]
        wqkv, wo = g[name + "_wqkv"], g[name + "_wo"]
        SB = [PS[:, i, :] for i in range(2 if keep_max else 4)]
        NSB = len(SB)
        MB = [PS[:, 2, :], PS[:, 3, :]]
        OB = PS[:, 4:6, :].rearrange("p b (g n) -> p (b g) n", n=N)
        M0, M1 = PS[:, 6, :], PS[:, 7, :]
        block = ctx.enter_context(nc.Block())

        def heads(ap):
            return ap.rearrange("p t (n d) -> p t n d", d=HD)

        def next1(b):
            return not isinstance(b, int) or b + 1 < B

        def next2(b):
            return not isinstance(b, int) or b + 2 < B

        def every_step(eng, step):
            step(0, 0)
            with eng.Fori(0, B // 2 - 2) as i:
                step(2 * i + 1, 1)
                step(2 * i + 2, 0)
            for b in range(B - 3, B):
                step(b, b % 2)

        def behind(b):
            return not isinstance(b, int) or b > 0

        @block.gpsimd
        def _(pool):
            pool.memset(half[:, :], -0.5).then_inc(s["zero"], 1)
            pool.memset(eps[:, :], LN_EPS).then_inc(s["zero"], 1)
            pool.memset(parts[:, :, :, :, :], 0.0).then_inc(s["zero"], 1)
            pool.memset(va[:, :, :, :, :], 0.0).then_inc(s["zero"], 1)
            pool.wait_ge(s["zero"], 4)
            pool.memset(va[:, :, :, :, HD:HD + 1], 1.0).then_inc(s["zero"], 1)
            pool.wait_ge(s["zero"], 5)

            def prepare_rstd(b):
                pool.wait_ge(s["mv"], b + 1)
                pool.tensor_tensor(ve[:, :], mv[:, :, 1], eps[:, :], ALU.add).then_inc(s["vareps"], 1)
                pool.wait_ge(s["vareps"], b + 1)
                pool.tensor_tensor(rstd[:, :], ve[:, :], half[:, :], ALU.pow).then_inc(s["rstd"], 1)

            def place_v(b, u):
                held(pool, s["raw"], b, s["ptick"])
                held(pool, s["pv"], (b - 1) * NH - 1, s["ptick"])
                if deflate:
                    held(pool, s["yd"], b - 2, s["ptick"])
                pool.tensor_copy(va[:, u, :, :, 0:HD], heads(vs[:, u])).then_inc(s["va"], 1)

            def select(b, h):
                held(pool, s["exp"], b * NH + h, s["ptick"])
                a = prob[:, h % RING, :]
                for at in (0, N):
                    part = a[:, at:at + P]
                    last = pool.affine_select(out=part, in_=part, compare_op=ALU.is_ge, fill=0.0, base=0,
                                              pattern=[[1, P]], channel_multiplier=-1)
                last.then_inc(s["tri"], 1)

            def step(b, u):
                for h in range(NH):
                    if causal:
                        select(b, h)
                    if h == AT.get("aggr") and next2(b):
                        prepare_rstd(b + 2)
                    if h == AT.get("xb") and bias:
                        pool.wait_ge(s["r"], b + 1)
                        nx = X[:, b]
                        pool.tensor_tensor(nx, nx, g[name + "_bo"][:, :].unsqueeze(1).broadcast_to([P, NT, C]),
                                           ALU.add).then_inc(s["xb"], 1)
                    if h == AT.get("va") and next1(b):
                        place_v(b + 1, 1 - u)

            prepare_rstd(0)
            prepare_rstd(1)
            place_v(0, 0)
            every_step(pool, step)

        @block.vector
        def _(v):
            v.memset(qm[:, :, :, :, :], 0.0).then_inc(s["zeroq"], 1)
            v.wait_ge(s["zero"], 5)
            v.tensor_copy(identb[:, :], ident[:, :]).then_inc(s["zero"], 1)
            if keep_max:
                pairs = ident[0:2 * HN, 0:2 * HN].rearrange("p (n k) -> p n k", k=2)
                v.tensor_tensor(sel[:, :, :], pairs[:, :, 0:1].broadcast_to([2 * HN, HN, P]),
                                pairs[:, :, 1:2].broadcast_to([2 * HN, HN, P]), ALU.add).then_inc(s["zero"], 1)

            def take_lane(b, u, lane):
                if lane == SA:
                    v.wait_ge(s["zeroq"], 1)
                    v.wait_ge(s["qt"], b + 1)
                    finished(v, s["qm"], b * SA + SA - 1)
                rows = slice(RW * lane, RW * (lane + 1))
                v.tensor_copy(qm[rows, u, :, lane, :], M0[rows, :].bitcast(BF16).rearrange("p (g n) -> p g n", n=N))\
                 .then_inc(s["qmv"], 1)

            def prepare_stats(b):
                for h in range(NT):
                    last = v.bn_stats(st[:, h, :], X[:, b, h, :])
                last.then_inc(s["stats"], 1)

            def prepare_aggr(b):
                held(v, s["stats"], b, s["tick"])
                for h in range(NT):
                    last = v.bn_aggr(mv[:, h, :], st[:, h, :])
                last.then_inc(s["mv"], 1)

            def prepare_r(b):
                held(v, s["rstd"], b, s["tick"])
                for h in range(NT):
                    last = v.tensor_scalar(r[:, h, :], X[:, b, h, :], mv[:, h, 0:1], rstd[:, h:h + 1],
                                           ALU.subtract, ALU.mult)
                last.then_inc(s["r"], 1)

            def prepare_raw(b, u):
                finished(v, s["va"], b - 2)
                for h in range(NT):
                    src = (M1, M0)[h][:, 0:3 * C]
                    v.wait_ge(s["qkv0" if h == 0 else "qkv1"], b + 1)
                    outs = ((qk[:, h, :].rearrange("p (n d) -> p n d", d=HD), 0, 2 * C),
                            (vs[:, u, h, :].rearrange("p (n d) -> p n d", d=HD), 2 * C, 3 * C))
                    for dst, lo, hi in outs:
                        part = src[:, lo:hi].rearrange("p (n d) -> p n d", d=HD)
                        if bias:
                            last = v.tensor_tensor(dst, part, g[name + "_bqkv"][:, lo:hi].rearrange(
                                "p (n d) -> p n d", d=HD), ALU.add)
                        else:
                            last = v.tensor_copy(dst, part)
                    last.then_inc(s["raw"], 1) if h else None

            def prepare_sq(b):
                v.wait_ge(s["raw"], b + 1)
                v.tensor_tensor(sq[:, :, :], qk[:, :, :], qk[:, :, :], ALU.mult).then_inc(s["sq"], 1)

            def prepare_ss(b):
                v.wait_ge(s["sq"], b + 1)
                v.tensor_reduce(ss[:, :, :], heads(sq[:, :, :]), AX.X, ALU.add).then_inc(s["ss"], 1)
                v.wait_ge(s["ss"], b + 1)
                v.tensor_scalar(ss[:, :, :], ss[:, :, :], 1.0 / HD, norm_eps, ALU.mult, ALU.add).then_inc(s["sse"], 1)

            def prepare_unit(b):
                v.wait_ge(s["root"], b + 1)
                v.tensor_tensor(nw[:, :, :], rn[:, :, :], rn[:, :, :], ALU.mult).then_inc(s["nwa"], 1)
                v.wait_ge(s["nwa"], b + 1)
                v.tensor_tensor(nw[:, :, :], nw[:, :, :], ss[:, :, :], ALU.mult).then_inc(s["nwb"], 1)
                v.wait_ge(s["nwb"], b + 1)
                v.tensor_scalar(nw[:, :, :], nw[:, :, :], -0.5, 1.5, ALU.mult, ALU.add).then_inc(s["nwc"], 1)
                v.wait_ge(s["nwc"], b + 1)
                v.tensor_tensor(rn[:, :, :], rn[:, :, :], nw[:, :, :], ALU.mult).then_inc(s["rn"], 1)
                v.wait_ge(s["rn"], b + 1)
                v.tensor_tensor(heads(qk[:, :, :]), heads(qk[:, :, :]), spread(rn[:, :, :], HD),
                                ALU.mult).then_inc(s["unit"], 1)

            def prepare_wn(b):
                v.wait_ge(s["unit"], b + 1)
                v.tensor_tensor(qk[:, :, :], qk[:, :, :], g[name + "_wn"][:, :].unsqueeze(1).broadcast_to(
                    [P, NT, 2 * C]), ALU.mult).then_inc(s["wn"], 1)

            def halves(w):
                return heads(qk[:, :, w * C:(w + 1) * C])

            def prepare_hi(b):
                v.wait_ge(s["wn" if weights else "unit" if norm_eps is not None else "raw"], b + 1)
                finished(v, s["qt"], b - 1)
                for w in range(2):
                    rows = parts[:, :, w, :, :].rearrange("p t n (k d) -> p t n k d", d=HD)
                    for t in range(NT):
                        last = v.tensor_copy(rows[:, t, :, 0:2 + w:1 + w],
                                             halves(w)[:, t].unsqueeze(2).broadcast_to([P, NH, 2, HD]))
                last.then_inc(s["hi"], 1)

            def prepare_lo(b):
                v.wait_ge(s["hi"], b + 1)
                for w, at in ((0, 2 * HD), (1, HD)):
                    last = v.tensor_tensor(parts[:, :, w, :, at:at + HD], halves(w), parts[:, :, w, :, 0:HD],
                                           ALU.subtract)
                last.then_inc(s["lo"], 1)

            def prepare_max(b, h):
                if not causal:
                    v.wait_ge(s["top"], b * NH + h + 1)
                if causal:
                    held(v, s["top"], b * NH + h, s["tick"])
                    for t in range(NT):
                        last = v.tensor_tensor_reduce(
                            out=junk[:, h % 2 * NT + t, 0:(t + 1) * P], in0=MB[h % 2][:, t * N:t * N + (t + 1) * P],
                            in1=g["tri"][:, t, 0:(t + 1) * P], scale=1.0, scalar=NEG, op0=ALU.add, op1=ALU.max,
                            accum_out=mx[:, t, h:h + 1])
                else:
                    last = v.tensor_reduce(mx[:, :, h], MB[h % 2].rearrange("p (t n) -> p t n", n=N), AX.X, ALU.max)
                last.then_inc(s["mx"], 1)

            def prepare_minus(b, half):
                part = slice(half * HN, (half + 1) * HN)
                finished(v, s["mx"], b * NH + half * HN + HN - 1)
                finished(v, s[("mt0", "mt1")[half]], b - 1)
                v.tensor_scalar(minus[:, :, part, 0], mx[:, :, part], -1.0, None, ALU.mult)\
                 .then_inc(s[("nhi0", "nhi1")[half]], 1)
                v.wait_ge(s[("nhi0", "nhi1")[half]], b + 1)
                v.scalar_tensor_tensor(out=minus[:, :, part, 1], in0=mx[:, :, part], scalar=-1.0,
                                       in1=minus[:, :, part, 0], op0=ALU.mult, op1=ALU.subtract)\
                 .then_inc(s[("nlo0", "nlo1")[half]], 1)

            def complete_y(b):
                v.wait_ge(s["ot"], b + 1)
                cols = [(M0, M1)[h][:, :].rearrange("p (n r) -> p n r", r=RW) for h in range(NT)]
                for h in range(NT):
                    last = v.reciprocal(den[:, h, :], cols[h][:, :, HD])
                last.then_inc(s["den"], 1)
                v.wait_ge(s["den"], b + 1)
                for h in range(NT):
                    last = v.tensor_tensor(y[:, h, :].rearrange("p (n d) -> p n d", d=HD), cols[h][:, :, 0:HD],
                                           spread(den[:, h, :], HD), ALU.mult)
                last.then_inc(s["y"], 1)

            def complete_dot(b, u):
                vh = va[:, u, :, :, 0:HD]
                yh, th = heads(y[:, :, :]), heads(t[:, :, :])
                v.tensor_tensor(th, vh, vh, ALU.mult).then_inc(s["t1"], 1)
                v.wait_ge(s["t1"], b * 4 + 1)
                v.tensor_reduce(vv[:, :, :], th, AX.X, ALU.add).then_inc(s["t1"], 1)
                v.wait_ge(s["t1"], b * 4 + 2)
                v.wait_ge(s["y"], b + 1)
                v.tensor_tensor(th, yh, vh, ALU.mult).then_inc(s["t2"], 1)
                v.tensor_scalar(vv[:, :, :], vv[:, :, :], 1e-24, None, ALU.max).then_inc(s["t1"], 1)
                v.wait_ge(s["t1"], b * 4 + 3)
                v.reciprocal(vv[:, :, :], vv[:, :, :]).then_inc(s["t1"], 1)
                v.wait_ge(s["t2"], b + 1)
                v.tensor_reduce(dot[:, :, :], th, AX.X, ALU.add).then_inc(s["t3"], 1)
                v.wait_ge(s["t1"], b * 4 + 4)
                v.wait_ge(s["t3"], b * 3 + 1)
                v.tensor_tensor(dot[:, :, :], dot[:, :, :], vv[:, :, :], ALU.mult).then_inc(s["t3"], 1)

            def complete_yd(b, u):
                vh = va[:, u, :, :, 0:HD]
                yh, th = heads(y[:, :, :]), heads(t[:, :, :])
                v.wait_ge(s["t3"], b * 3 + 2)
                v.tensor_tensor(th, vh, spread(dot[:, :, :], HD), ALU.mult).then_inc(s["t3"], 1)
                v.wait_ge(s["t3"], b * 3 + 3)
                v.tensor_tensor(yh, yh, th, ALU.subtract).then_inc(s["yd"], 1)

            def complete_x(b):
                v.wait_ge(s["proj"], b + 1)
                if bias:
                    v.wait_ge(s["xb"], b + 1)
                v.tensor_tensor(X[:, b], X[:, b], M1[:, 0:N].rearrange("p (t c) -> p t c", t=NT),
                                ALU.add).then_inc(s["x"], 1)

            def step(b, u):
                for h in range(NH):
                    if keep_max and h < TLAG:
                        prepare_max(b, NH - TLAG + h)
                    if keep_max and h >= TLAG and next1(b):
                        prepare_max(b + 1, h - TLAG)
                    if next1(b):
                        if h == AT.get("unit") and norm_eps is not None:
                            prepare_unit(b + 1)
                        if h == AT.get("wn") and weights:
                            prepare_wn(b + 1)
                        if h == AT.get("hi"):
                            prepare_hi(b + 1)
                        if h == AT.get("lo"):
                            prepare_lo(b + 1)
                        if AT["lanes"] + SA <= h < AT["lanes"] + S:
                            take_lane(b + 1, 1 - u, h - AT["lanes"])
                    if next2(b):
                        if h == AT.get("stats"):
                            prepare_stats(b + 2)
                        if h == AT.get("aggr"):
                            prepare_aggr(b + 2)
                        if h == AT.get("r"):
                            prepare_r(b + 2)
                        if h == AT.get("raw"):
                            prepare_raw(b + 2, u)
                        if h == AT.get("sq") and norm_eps is not None:
                            prepare_sq(b + 2)
                        if h == AT.get("ss") and norm_eps is not None:
                            prepare_ss(b + 2)
                    if keep_max and h == AT.get("minus1"):
                        prepare_minus(b, 1)
                    if keep_max and h == AT.get("minus0") and next1(b):
                        prepare_minus(b + 1, 0)
                    if behind(b):
                        if h == AT.get("y"):
                            complete_y(b - 1)
                        if h == AT.get("dot") and deflate:
                            complete_dot(b - 1, 1 - u)
                        if h == AT.get("yd") and deflate:
                            complete_yd(b - 1, 1 - u)
                        if h == AT.get("x"):
                            complete_x(b - 1)

            for b in range(2):
                prepare_stats(b)
                prepare_aggr(b)
                prepare_r(b)
                prepare_raw(b, b)
                if norm_eps is not None:
                    prepare_sq(b)
                    prepare_ss(b)
                if b == 0:
                    if norm_eps is not None:
                        prepare_unit(0)
                    if weights:
                        prepare_wn(0)
                    prepare_hi(0)
                    prepare_lo(0)
                    for lane in range(SA, S):
                        take_lane(0, 0, lane)
                    if keep_max:
                        for h in range(NH - TLAG):
                            prepare_max(0, h)
                        prepare_minus(0, 0)
            every_step(v, step)
            complete_y(B - 1)
            if deflate:
                complete_dot(B - 1, 1)
                complete_yd(B - 1, 1)
            complete_x(B - 1)

        @block.tensor
        def _(pe):
            pe.wait_ge(s["zero"], 7 if keep_max else 6)

            def turned(dst, what):
                for gg in range(G):
                    for h in range(NT):
                        last = turn(nc, dst.bitcast(BF16)[:, gg * N + h * P:gg * N + (h + 1) * P],
                                    parts[:, h, what, S * gg:S * gg + S, :], identb[:, :])
                return last

            def lanes_taken(b):
                finished(pe, s["qm"], b * SA + SA - 1)
                if SA < S:
                    finished(pe, s["qmv"], (b + 1) * (S - SA) - 1)

            def prepare_rt(b):
                pe.wait_ge(s["r"], b + 1)
                if isinstance(b, int) and b <= 2:
                    lanes_taken(b - 1)
                    finished(pe, s["kT"], b - 1)
                    if keep_max:
                        finished(pe, s["mT0"], min(b - 1, 0))
                        finished(pe, s["mT1"], b - 2)
                else:
                    finished(pe, s["y"], b - 3)
                for h in range(NT):
                    last = turn(nc, M0[:, h * P:(h + 1) * P], r[:, h, :], ident[:, :])
                last.then_inc(s["rt"], 1)

            def prepare_qkv(b):
                pe.wait_ge(s["rT"], b + 1)
                for h in range(NT):
                    pe.matmul((M1, M0)[h][:, 0:3 * C], lhsT=rT[:, h * P:(h + 1) * P], rhs=wqkv[:, :],
                              start=True, stop=True).then_inc(s["qkv0" if h == 0 else "qkv1"], 1)

            def prepare_turns(b):
                pe.wait_ge(s["lo"], b + 1)
                finished(pe, s["x"], b - 3)
                if keep_max:
                    finished(pe, s["mT0"], b - 1)
                turned(M1, 1).then_inc(s["kt"], 1)
                turned(M0, 0).then_inc(s["qt"], 1)

            def prepare_top(b, u, h):
                gg = h // S
                if h == 0:
                    pe.wait_ge(s["kT"], b + 1)
                if h < SA:
                    pe.wait_ge(s["qm"], b * SA + h + 1)
                elif h < S:
                    finished(pe, s["qmv"], b * (S - SA) + h - SA)
                if not (isinstance(b, int) and b == 0 and h < 2):
                    finished(pe, s["mx"], b * NH + h - 2)
                for t in range(NT):
                    keys = (t + 1) * P if causal else N
                    last = pe.matmul(MB[h % 2][:, t * N:t * N + keys],
                                     lhsT=qm[:, u, gg, h % S, t * P:(t + 1) * P],
                                     rhs=kT[:, u, gg, 0:keys], start=True, stop=True)
                last.then_inc(s["top"], 1)

            def prepare_mt(b, half):
                pe.wait_ge(s[("nlo0", "nlo1")[half]], b + 1)
                if half == 1:
                    finished(pe, s["kT"], b + 1 if next1(b) else b)
                    if not next1(b):
                        finished(pe, s["x"], b - 2)
                elif isinstance(b, int) and b <= 1:
                    lanes_taken(0)
                    if b == 1:
                        pe.wait_ge(s["raw"], 3)
                for t in range(NT):
                    last = turn(nc, (M0, M1)[half].bitcast(BF16)[0:2 * HN, t * P:(t + 1) * P],
                                minus[:, t, half * HN:(half + 1) * HN, :], identb[:, :])
                last.then_inc(s[("mt0", "mt1")[half]], 1)

            def scores(b, u, h):
                gg = h // S
                if h == 0:
                    pe.wait_ge(s["zeroq"], 1)
                    pe.wait_ge(s["kT"], b + 1)
                if h < SA:
                    pe.wait_ge(s["qm"], b * SA + h + 1)
                elif h < S:
                    finished(pe, s["qmv"], b * (S - SA) + h - SA)
                if not (isinstance(b, int) and b == 0 and h < NSB):
                    finished(pe, s["exp"], b * NH + h - NSB)
                if keep_max and h % HN == 0:
                    pe.wait_ge(s[("mT0", "mT1")[h // HN]], b + 1)
                for t in range(NT):
                    lo = t * P if causal else 0
                    at = N if t else 0
                    last = pe.matmul(SB[h % NSB][:, at:at + N - lo], lhsT=kT[:, u, gg, t * P:(t + 1) * P],
                                     rhs=qm[:, u, gg, h % S, lo:N], start=True, stop=not keep_max)
                    if keep_max:
                        last = pe.matmul(SB[h % NSB][:, at:at + N - lo], lhsT=sel[:, h % HN, :],
                                         rhs=mT[:, h // HN, lo:N], start=False, stop=True)
                last.then_inc(s["sc"], 1)

            def products(b, u, h):
                gg, lane = h // S, RW * (h % S)
                if h == 0:
                    finished(pe, s["oT0"], b - 1)
                    pe.wait_ge(s["va"], b + 1)
                if h == NH // 2:
                    finished(pe, s["oT1"], b - 1)
                pe.wait_ge(s["tri" if causal else "exp"], b * NH + h + 1)
                for t in range(NT):
                    lo = t * P if causal else 0
                    at = N if t else 0
                    last = pe.matmul(OB[lane:lane + RW, gg, lo:N], lhsT=va[:, u, t, h, :],
                                     rhs=prob[:, h % RING, at:at + N - lo], start=(t == 0), stop=(t == NT - 1),
                                     skip_group_check=causal)
                last.then_inc(s["pv"], 1)

            def complete_ot(b):
                pe.wait_ge(s["oT1"], b + 1)
                if isinstance(b, int) and b == B - 1:
                    finished(pe, s["x"], b - 1)
                elif isinstance(b, int) and b == B - 2:
                    if keep_max:
                        pe.wait_ge(s["mT0"], b + 2)
                        pe.wait_ge(s["mT1"], b + 2)
                    else:
                        finished(pe, s["x"], b - 1)
                else:
                    lanes_taken(b + 2)
                    pe.wait_ge(s["mT1" if keep_max else "kT"], b + 1 if keep_max else b + 3)
                for h in range(NT):
                    for gg in range(G):
                        last = turn(nc, (M0, M1)[h][:, gg * P:(gg + 1) * P], oT[:, gg, h * P:(h + 1) * P], ident[:, :])
                last.then_inc(s["ot"], 1)

            def complete_yt(b):
                pe.wait_ge(s["yd" if deflate else "y"], b + 1)
                if not isinstance(b, int) or b + 3 < B:
                    pe.wait_ge(s["raw"], b + 4)
                for h in range(NT):
                    last = turn(nc, M0[:, h * P:(h + 1) * P], y[:, h, :], ident[:, :])
                last.then_inc(s["yt"], 1)

            def complete_proj(b):
                pe.wait_ge(s["yT"], b + 1)
                for h in range(NT):
                    last = pe.matmul(M1[:, h * C:(h + 1) * C], lhsT=yT[:, h * P:(h + 1) * P], rhs=wo[:, :],
                                     start=True, stop=True)
                last.then_inc(s["proj"], 1)

            def step(b, u):
                for h in range(NH):
                    scores(b, u, h)
                    if h >= LAG:
                        products(b, u, h - LAG)
                    elif behind(b):
                        products(b - 1, 1 - u, NH + h - LAG)
                    if keep_max and h < TLAG:
                        prepare_top(b, u, NH - TLAG + h)
                    if keep_max and h >= TLAG and next1(b):
                        prepare_top(b + 1, 1 - u, h - TLAG)
                    if h == AT.get("turns") and next1(b):
                        prepare_turns(b + 1)
                    if keep_max and h == AT.get("mt1"):
                        prepare_mt(b, 1)
                    if h == AT.get("rt") and next2(b):
                        prepare_rt(b + 2)
                    if h == AT.get("qkv") and next2(b):
                        prepare_qkv(b + 2)
                    if behind(b):
                        if h == AT.get("ot"):
                            complete_ot(b - 1)
                        if h == AT.get("yt"):
                            complete_yt(b - 1)
                        if h == AT.get("proj"):
                            complete_proj(b - 1)
                    if keep_max and h == AT.get("mt0") and next1(b):
                        prepare_mt(b + 1, 0)

            prepare_rt(0)
            prepare_qkv(0)
            prepare_turns(0)
            if keep_max:
                for h in range(NH - TLAG):
                    prepare_top(0, 0, h)
                prepare_mt(0, 0)
            prepare_rt(1)
            prepare_qkv(1)
            every_step(pe, step)
            for h in range(NH - LAG, NH):
                products(B - 1, 1, h)
            complete_ot(B - 1)
            complete_yt(B - 1)
            complete_proj(B - 1)

        @block.scalar
        def _(act):
            act.preload_act_table_set("natural_log_exp_and_others")

            def prepare_rT(b):
                act.wait_ge(s["rt"], b + 1)
                act.activation(rT[:, :], M0[:, 0:N], ACT.Copy).then_inc(s["rT"], 1)

            def prepare_root(b):
                if norm_eps is not None:
                    act.wait_ge(s["sse"], b + 1)
                    act.activation(ln[:, :, :], ss[:, :, :], ACT.Ln).then_inc(s["ln"], 1)
                    act.wait_ge(s["ln"], b + 1)
                    act.activation(rn[:, :, :], ln[:, :, :], ACT.Exp, scale=-0.5).then_inc(s["root"], 1)

            def take_k(b, u):
                act.wait_ge(s["kt"], b + 1)
                act.activation(kT[:, u].rearrange("p g n -> p (g n)"), M1.bitcast(BF16), ACT.Copy).then_inc(s["kT"], 1)

            def take_max(b, half):
                act.wait_ge(s[("mt0", "mt1")[half]], b + 1)
                act.activation(mT[:, half, :], (M0, M1)[half].bitcast(BF16)[0:2 * HN, 0:N], ACT.Copy)\
                   .then_inc(s[("mT0", "mT1")[half]], 1)

            def take_lane(b, u, lane):
                if lane == 0:
                    act.wait_ge(s["zeroq"], 1)
                    act.wait_ge(s["qt"], b + 1)
                rows = slice(RW * lane, RW * (lane + 1))
                act.activation(qm[rows, u, :, lane, :], M0[rows, :].bitcast(BF16).rearrange("p (g n) -> p g n", n=N),
                               ACT.Copy).then_inc(s["qm"], 1)

            def exps(b, h):
                act.wait_ge(s["sc"], b * NH + h + 1)
                if not (isinstance(b, int) and b * NH + h < RING):
                    finished(act, s["pv"], b * NH + h - RING)
                act.activation(prob[:, h % RING, 0:n_prob], SB[h % NSB][:, 0:n_prob], ACT.Exp,
                               scale=scale).then_inc(s["exp"], 1)

            def complete_oT(b, half):
                if half == 0:
                    finished(act, s["ot"], b - 1)
                finished(act, s["pv"], b * NH + (half + 1) * NH // 2 - 1)
                part = slice(half * G // 2, (half + 1) * G // 2)
                act.activation(oT[:, part, :], OB[:, part, :], ACT.Copy).then_inc(s[("oT0", "oT1")[half]], 1)

            def complete_yT(b):
                act.wait_ge(s["yt"], b + 1)
                act.activation(yT[:, :], M0[:, 0:N], ACT.Copy).then_inc(s["yT"], 1)

            def step(b, u):
                for h in range(NH):
                    exps(b, h)
                    if h == AT.get("oT1") and behind(b):
                        complete_oT(b - 1, 1)
                    if h == AT.get("turns") and next1(b):
                        take_k(b + 1, 1 - u)
                    if keep_max and h == AT.get("mt1"):
                        take_max(b, 1)
                    if AT["lanes"] <= h < AT["lanes"] + SA and next1(b):
                        take_lane(b + 1, 1 - u, h - AT["lanes"])
                    if h == AT.get("oT0"):
                        complete_oT(b, 0)
                    if h == AT.get("rt") and next2(b):
                        prepare_rT(b + 2)
                    if h == AT.get("root") and next2(b):
                        prepare_root(b + 2)
                    if h == AT.get("yt") and behind(b):
                        complete_yT(b - 1)
                    if keep_max and h == AT.get("mt0") and next1(b):
                        take_max(b + 1, 0)

            prepare_rT(0)
            prepare_root(0)
            take_k(0, 0)
            for lane in range(SA):
                take_lane(0, 0, lane)
            if keep_max:
                take_max(0, 0)
            prepare_rT(1)
            prepare_root(1)
            every_step(act, step)
            complete_oT(B - 1, 1)
            complete_yT(B - 1)


def moe1_phase(nc, g, name, out=None):
    T4 = 4
    TG = T4 * P
    NG = B * N // TG
    with ExitStack() as ctx:
        s = semaphores(nc, ctx, name, "zero tick ptick rb1 cps cs tps vconst stats mv vareps rstd r nstats nmv nvareps nrstd n xr "
                                      "nt nT lg lgb mx d ex sum rsum p eq rank best hot1 q2 mx2 eq2 rank2 best2 hot2 "
                                      "both ws w1 rest w2 w3 wt wst wT init acc0 bc bcs up relu down t acc at x stored")

        def sb(nm, shape, dt=F32):
            return ctx.enter_context(nc.sbuf_tensor(name + nm, shape, dt))

        half = sb("half", [P, T4])
        eps = sb("eps", [P, T4])
        ones = sb("ones", [E, E])
        identb = sb("identb", [P, P], BF16)
        rowb = sb("rowb", [3 * E, E, P], BF16)
        rb1 = sb("rb1", [P, E, FJ, E])
        vconst = sb("vconst", [E, C])
        cs = sb("cs", [E, C])
        st = sb("st", [P, T4, 6])
        mv = sb("mv", [P, T4, 2])
        ve = sb("ve", [P, T4])
        rstd = sb("rstd", [P, T4])
        r = sb("r", [P, T4, C])
        n = sb("n", [P, T4, C])
        nT = sb("nT", [P, 2, TG])
        lg = sb("lg", [P, T4, E])
        pr = sb("pr", [P, T4, E])
        h1 = sb("h1", [P, T4, E])
        h2 = sb("h2", [P, T4, E])
        mx = sb("mx", [P, T4])
        ws = sb("ws", [P, T4, E])
        w3 = sb("w3", [P, T4, 3, E], BF16)
        wT = sb("wT", [E, TG])
        w3T = sb("w3T", [3 * E, 2, TG], BF16)
        hid = sb("hid", [P, 2, FJ, TG])
        bc = sb("bc", [P, 2, TG])
        tt = sb("tt", [P, 2, TG])
        acc = sb("acc", [P, 2, TG])
        X, ident, PS = g["X"], g["ident"], g["PS"]
        xg = X[:, :, :, :].rearrange("p (i s) h c -> p i (s h) c", s=T4 // NT)
        UP = [PS[:, j, :] for j in range(FJ)]
        DN = PS[:, 4, :]
        BC = PS[:, 5, :]
        M, M2 = PS[:, 6, :], PS[:, 7, :]
        first = g["first"][:, :].unsqueeze(1).broadcast_to([P, T4, E])
        block = ctx.enter_context(nc.Block())

        def rounds(start, step, end, eng):
            start()
            step(0, 0, True, False)
            with eng.Fori(0, NG // 2 - 1) as k:
                step(2 * k + 1, 1, True, True)
                step(2 * k + 2, 0, True, True)
            step(NG - 1, 1, False, True)
            end()

        if out is not None:
            og = out.rearrange("(i s) (h p) c -> i p s h c", s=T4 // NT, p=P)

            @block.sync
            def _(sp):
                for i in range(NG):
                    sp.wait_ge(s["x"], i + 1)
                    sp.dma_start(og[i], X[:, i * T4 // NT:(i + 1) * T4 // NT]).then_inc(s["stored"], 16)
                sp.wait_ge(s["stored"], NG * 16)

        @block.gpsimd
        def _(pool):
            pool.memset(half[:, :], -0.5).then_inc(s["zero"], 1)
            pool.memset(eps[:, :], LN_EPS).then_inc(s["zero"], 1)
            pool.memset(ones[:, :], 1.0).then_inc(s["zero"], 1)
            pool.memset(rb1[:, :, :, :], 0.0).then_inc(s["zero"], 1)
            pool.wait_ge(s["zero"], 4)
            pool.sem_inc(s["acc"], 2)

            def root(i, a, b, c):
                pool.wait_ge(s[a], i + 1)
                pool.tensor_tensor(ve[:, :], mv[:, :, 1], eps[:, :], ALU.add).then_inc(s[b], 1)
                pool.wait_ge(s[b], i + 1)
                pool.tensor_tensor(rstd[:, :], ve[:, :], half[:, :], ALU.pow).then_inc(s[c], 1)

            def prepare(i, u):
                root(i, "mv", "vareps", "rstd")
                root(i, "nmv", "nvareps", "nrstd")
                pool.tensor_tensor(xg[:, i], xg[:, i], r[:, :, :], ALU.add).then_inc(s["xr"], 1)

            def step(i, u, ahead, behind):
                for e in range(E):
                    pool.wait_ge(s["t"], i * E + e + 3)
                    if e:
                        pool.wait_ge(s["acc"], i * E + e + 2)
                    else:
                        pool.wait_ge(s["acc0"], i + 1)
                    pool.tensor_tensor(acc[:, u, :], acc[:, u, :], tt[:, e % 2, :], ALU.add).then_inc(s["acc"], 1)
                    if e == 0 and ahead:
                        prepare(i + 1, 1 - u)

            rounds(lambda: prepare(0, 0), step, lambda: None, pool)

        @block.vector
        def _(v):
            v.sem_inc(s["t"], 2)
            v.wait_ge(s["zero"], 4)
            v.tensor_copy(identb[:, :], ident[:, :]).then_inc(s["zero"], 1)
            v.tensor_copy(rowb[:, :, :], g["row3"][:, :, :]).then_inc(s["zero"], 1)
            for e in range(E):
                last = v.tensor_scalar(rb1[:, e, :, e], g["b1e"][:, e, :], 0.0, None, ALU.max)
            last.then_inc(s["rb1"], 1)

            def norm(i, src, dst, a, b, c, d):
                for t in range(T4):
                    last = v.bn_stats(st[:, t, :], src[:, t, :])
                last.then_inc(s[a], 1)
                held(v, s[a], i, s["tick"])
                for t in range(T4):
                    last = v.bn_aggr(mv[:, t, :], st[:, t, :])
                last.then_inc(s[b], 1)
                v.wait_ge(s[c], i + 1)
                for t in range(T4):
                    last = v.tensor_scalar(dst[:, t, :], src[:, t, :], mv[:, t, 0:1], rstd[:, t:t + 1],
                                           ALU.subtract, ALU.mult)
                last.then_inc(s[d], 1)

            def prepare_norm(i):
                norm(i, xg[:, i], r, "stats", "mv", "rstd", "r")
                v.wait_ge(s["r"], i + 1)
                norm(i, r, n, "nstats", "nmv", "nrstd", "n")

            def prepare_choice(i):
                bias = g["rb1"][:, :].unsqueeze(1).broadcast_to([P, T4, E])
                v.wait_ge(s["lg"], i + 1)
                v.tensor_tensor(lg[:, :, :], M2[:, 0:T4 * E].rearrange("p (t e) -> p t e", e=E), bias,
                                ALU.add).then_inc(s["lgb"], 1)
                v.wait_ge(s["lgb"], i + 1)
                v.tensor_reduce(mx[:, :], lg[:, :, :], AX.X, ALU.max).then_inc(s["mx"], 1)
                v.wait_ge(s["mx"], i + 1)
                v.tensor_tensor(lg[:, :, :], lg[:, :, :], spread(mx[:, :], E), ALU.subtract).then_inc(s["d"], 1)
                v.wait_ge(s["ex"], i + 1)
                v.tensor_reduce(mx[:, :], pr[:, :, :], AX.X, ALU.add).then_inc(s["sum"], 1)
                v.wait_ge(s["sum"], i + 1)
                v.reciprocal(mx[:, :], mx[:, :]).then_inc(s["rsum"], 1)
                v.wait_ge(s["rsum"], i + 1)
                v.tensor_tensor(pr[:, :, :], pr[:, :, :], spread(mx[:, :], E), ALU.mult).then_inc(s["p"], 1)
                v.wait_ge(s["p"], i + 1)
                v.tensor_reduce(mx[:, :], pr[:, :, :], AX.X, ALU.max).then_inc(s["q2"], 1)
                v.wait_ge(s["q2"], i + 1)
                v.tensor_tensor(h1[:, :, :], pr[:, :, :], spread(mx[:, :], E), ALU.is_equal).then_inc(s["eq"], 1)
                v.wait_ge(s["eq"], i + 1)
                v.tensor_tensor(h1[:, :, :], h1[:, :, :], first, ALU.mult).then_inc(s["rank"], 1)
                v.wait_ge(s["rank"], i + 1)
                v.tensor_reduce(mx[:, :], h1[:, :, :], AX.X, ALU.max).then_inc(s["best"], 1)
                v.wait_ge(s["best"], i + 1)
                v.tensor_tensor(h1[:, :, :], h1[:, :, :], spread(mx[:, :], E),
                    ALU.is_equal).then_inc(s["hot1"], 1)
                v.wait_ge(s["hot1"], i + 1)
                v.scalar_tensor_tensor(out=ws[:, :, :], in0=h1[:, :, :], scalar=-2.0, in1=pr[:, :, :],
                                       op0=ALU.mult, op1=ALU.add).then_inc(s["rest"], 1)
                v.wait_ge(s["rest"], i + 1)
                v.tensor_reduce(mx[:, :], ws[:, :, :], AX.X, ALU.max).then_inc(s["mx2"], 1)
                v.wait_ge(s["mx2"], i + 1)
                v.tensor_tensor(h2[:, :, :], ws[:, :, :], spread(mx[:, :], E),
                    ALU.is_equal).then_inc(s["eq2"], 1)
                v.wait_ge(s["eq2"], i + 1)
                v.tensor_tensor(h2[:, :, :], h2[:, :, :], first, ALU.mult).then_inc(s["rank2"], 1)
                v.wait_ge(s["rank2"], i + 1)
                v.tensor_reduce(mx[:, :], h2[:, :, :], AX.X, ALU.max).then_inc(s["best2"], 1)
                v.wait_ge(s["best2"], i + 1)
                v.tensor_tensor(h2[:, :, :], h2[:, :, :], spread(mx[:, :], E),
                    ALU.is_equal).then_inc(s["hot2"], 1)
                v.wait_ge(s["hot2"], i + 1)
                v.tensor_tensor(h1[:, :, :], h1[:, :, :], h2[:, :, :], ALU.add).then_inc(s["both"], 1)
                v.wait_ge(s["both"], i + 1)
                v.tensor_tensor(ws[:, :, :], h1[:, :, :], pr[:, :, :], ALU.mult).then_inc(s["ws"], 1)
                v.wait_ge(s["ws"], i + 1)
                v.tensor_copy(w3[:, :, 0, :], ws[:, :, :]).then_inc(s["w1"], 1)
                v.wait_ge(s["w1"], i + 1)
                v.tensor_tensor(pr[:, :, :], ws[:, :, :], w3[:, :, 0, :], ALU.subtract).then_inc(s["w2"], 1)
                v.wait_ge(s["w2"], i + 1)
                v.tensor_copy(w3[:, :, 1, :], pr[:, :, :]).then_inc(s["w3"], 1)
                v.wait_ge(s["w3"], i + 1)
                v.tensor_tensor(w3[:, :, 2, :], pr[:, :, :], w3[:, :, 1, :], ALU.subtract).then_inc(s["wt"], 1)

            def weigh(i, u, e):
                v.wait_ge(s["down"], i * E + e + 1)
                v.wait_ge(s["acc"], i * E + e + 1)
                v.wait_ge(s["bcs"], i * E + e + 2)
                v.tensor_tensor(tt[:, e % 2, :], DN, bc[:, e % 2, :], ALU.mult).then_inc(s["t"], 1)

            def complete(i):
                v.wait_ge(s["at"], i + 1)
                v.wait_ge(s["xr"], i + 1)
                v.tensor_tensor(xg[:, i], xg[:, i], M.rearrange("p (t c) -> p t c", c=C), ALU.add).then_inc(s["x"], 1)

            def start():
                prepare_norm(0)
                prepare_choice(0)
                v.wait_ge(s["cps"], 1)
                v.tensor_tensor(cs[:, :], M[0:E, 0:C], g["b2e"][:, :], ALU.add).then_inc(s["cs"], 1)
                v.wait_ge(s["cs"], 1)
                v.tensor_tensor(vconst[:, :], g["b2e"][:, :], cs[:, :], ALU.subtract).then_inc(s["cs"], 1)
                v.wait_ge(s["cs"], 2)
                v.wait_ge(s["tps"], 1)
                v.tensor_tensor(vconst[:, :], vconst[:, :], M2[0:E, 0:C], ALU.add).then_inc(s["vconst"], 1)

            def step(i, u, ahead, behind):
                for e in range(E):
                    weigh(i, u, e)
                    if e == 0 and ahead:
                        prepare_norm(i + 1)
                    if e == 1 and behind:
                        complete(i - 1)
                    if e == 3 and ahead:
                        prepare_choice(i + 1)

            rounds(start, step, lambda: complete(NG - 1), v)

        @block.tensor
        def _(pe):
            pe.wait_ge(s["zero"], 6)
            pe.wait_ge(s["rb1"], 1)

            def prepare_turn(i, u):
                pe.wait_ge(s["n"], i + 1)
                finished(pe, s["x"], i - 2)
                for t in range(T4):
                    last = turn(nc, M[:, t * P:(t + 1) * P], n[:, t, :], ident[:, :])
                last.then_inc(s["nt"], 1)

            def prepare_logits(i, u):
                pe.wait_ge(s["nT"], i + 1)
                for t in range(T4):
                    last = pe.matmul(M2[:, t * E:(t + 1) * E], lhsT=nT[:, u, t * P:(t + 1) * P], rhs=g["rw1"][:, :],
                                     start=True, stop=True)
                last.then_inc(s["lg"], 1)

            def prepare_weights(i, u):
                pe.wait_ge(s["wt"], i + 1)
                for t in range(T4):
                    last = turn(nc, M[0:E, t * P:(t + 1) * P], ws[:, t, :], ident[:, :])
                for t in range(T4):
                    last = turn(nc, M2.bitcast(BF16)[0:3 * E, t * P:(t + 1) * P], w3[:, t, :, :], identb[:, :])
                last.then_inc(s["wst"], 1)

            def prepare_init(i, u):
                pe.wait_ge(s["wT"], i + 1)
                pe.matmul(M, lhsT=vconst[:, :], rhs=wT[:, :], start=True, stop=True).then_inc(s["init"], 1)

            def expert_up(i, u, e):
                for j in range(FJ):
                    pe.wait_ge(s["relu"], i * E * FJ + e * FJ + j + 1)
                    pe.matmul(UP[j], lhsT=g["W1e"][:, e, j * P:(j + 1) * P], rhs=nT[:, u, :],
                              start=True, stop=True).then_inc(s["up"], 1)

            def expert_weight(i, u, e):
                pe.wait_ge(s["bcs"], i * E + e + 1)
                pe.matmul(BC, lhsT=rowb[:, e, :], rhs=w3T[:, u, :], start=True, stop=True).then_inc(s["bc"], 1)

            def expert(i, u, e):
                expert_up(i, u, e)
                expert_weight(i, u, e)

            def expert_out(i, u, e):
                pe.wait_ge(s["t"], i * E + e + 2)
                for j in range(FJ):
                    pe.wait_ge(s["relu"], i * E * FJ + e * FJ + j + 1 + FJ)
                    last = pe.matmul(DN, lhsT=g["W2e"][:, e, j, :], rhs=hid[:, e % 2, j, :],
                                     start=(j == 0), stop=(j == FJ - 1))
                last.then_inc(s["down"], 1)

            def complete(i, u):
                if isinstance(i, int) and i == NG - 1:
                    finished(pe, s["x"], i - 1)
                else:
                    pe.wait_ge(s["acc0"], i + 2)
                pe.wait_ge(s["acc"], i * E + E + 2)
                for t in range(T4):
                    last = turn(nc, M[:, t * P:(t + 1) * P], acc[:, u, t * P:(t + 1) * P], ident[:, :])
                last.then_inc(s["at"], 1)

            def start():
                prepare_turn(0, 0)
                prepare_logits(0, 0)
                pe.wait_ge(s["rb1"], 1)
                for e in range(E):
                    for j in range(FJ):
                        last = pe.matmul(M[0:E, 0:C], lhsT=rb1[:, e, j, :], rhs=g["W2e"][:, e, j, :],
                                         start=(e == 0 and j == 0), stop=(e == E - 1 and j == FJ - 1))
                last.then_inc(s["cps"], 1)
                expert_up(0, 0, 0)
                pe.wait_ge(s["cs"], 1)
                pe.matmul(M2[0:E, 0:C], lhsT=ones[:, :], rhs=cs[:, :], start=True, stop=True).then_inc(s["tps"], 1)
                pe.wait_ge(s["vconst"], 1)
                prepare_weights(0, 0)
                prepare_init(0, 0)
                expert_weight(0, 0, 0)

            def step(i, u, ahead, behind):
                for e in range(E):
                    if e < E - 1:
                        expert(i, u, e + 1)
                    elif ahead:
                        expert(i + 1, 1 - u, 0)
                    expert_out(i, u, e)
                    if behind and e == 0:
                        complete(i - 1, 1 - u)
                    if ahead and e == 2:
                        prepare_turn(i + 1, 1 - u)
                    if ahead and e == 3:
                        prepare_logits(i + 1, 1 - u)
                    if ahead and e == 5:
                        prepare_weights(i + 1, 1 - u)
                    if ahead and e == 6:
                        prepare_init(i + 1, 1 - u)

            rounds(start, step, lambda: complete(NG - 1, 1), pe)

        @block.scalar
        def _(act):
            act.sem_inc(s["relu"], FJ)
            act.sem_inc(s["bcs"], 1)

            def prepare_nT(i, u):
                act.wait_ge(s["nt"], i + 1)
                act.activation(nT[:, u, :], M, ACT.Identity, bias=g["beta"][:, 0:1],
                               scale=g["gamma"][:, 0:1]).then_inc(s["nT"], 1)

            def prepare_exp(i, u):
                act.wait_ge(s["d"], i + 1)
                act.activation(pr[:, :, :], lg[:, :, :], ACT.Exp).then_inc(s["ex"], 1)

            def prepare_wT(i, u):
                act.wait_ge(s["wst"], i + 1)
                act.activation(wT[:, :], M[0:E, :], ACT.Copy)
                act.activation(w3T[:, u, :], M2.bitcast(BF16)[0:3 * E, 0:TG], ACT.Copy).then_inc(s["wT"], 1)

            def prepare_acc(i, u):
                act.wait_ge(s["init"], i + 1)
                act.activation(acc[:, u, :], M, ACT.Copy).then_inc(s["acc0"], 1)

            def expert_relu(i, u, e):
                for j in range(FJ):
                    act.wait_ge(s["up"], i * E * FJ + e * FJ + j + 1)
                    act.activation(hid[:, e % 2, j, :], UP[j], ACT.Relu, bias=g["b1e"][:, e, j:j + 1])\
                       .then_inc(s["relu"], 1)

            def expert_weight(i, u, e):
                act.wait_ge(s["bc"], i * E + e + 1)
                act.wait_ge(s["t"], i * E + e + 1)
                act.activation(bc[:, e % 2, :], BC, ACT.Copy).then_inc(s["bcs"], 1)

            def expert(i, u, e):
                expert_relu(i, u, e)
                expert_weight(i, u, e)

            def start():
                prepare_nT(0, 0)
                prepare_exp(0, 0)
                expert_relu(0, 0, 0)
                prepare_wT(0, 0)
                prepare_acc(0, 0)
                expert_weight(0, 0, 0)

            def step(i, u, ahead, behind):
                for e in range(E):
                    if e < E - 1:
                        expert(i, u, e + 1)
                    elif ahead:
                        expert(i + 1, 1 - u, 0)
                    if ahead and e == 2:
                        prepare_nT(i + 1, 1 - u)
                    if ahead and e == 4:
                        prepare_exp(i + 1, 1 - u)
                    if ahead and e == 5:
                        prepare_wT(i + 1, 1 - u)
                    if ahead and e == 6:
                        prepare_acc(i + 1, 1 - u)

            rounds(start, step, lambda: None, act)


def build(nc, d, out):
    with ExitStack() as ctx:
        def sb(name, shape, dt=F32):
            return ctx.enter_context(nc.sbuf_tensor(name, shape, dt))

        g = {"x_dram": d["x"]}
        g["X"] = sb("X", [P, B, NT, C])
        g["HT"] = sb("HT", [P, B, N])
        g["PS"] = ctx.enter_context(nc.psum_tensor("PS", [P, 8, 512], F32))
        g["first_loads"], g["loads"] = [], []

        def const(name, shape, first=False):
            g[name] = sb("k_" + name, shape)
            full = g[name][tuple(slice(None) for _ in shape)]
            g["first_loads" if first else "loads"].append((full, d[name]))

        const("ident", [P, P], True)
        const("conv1_w", [P, MULT * TAPS], True)
        const("conv1_b", [P, MULT], True)
        const("conv2_w", [P, MULT * TAPS], True)
        for n in ("conv2_b", "ln0_g", "ln0_b"):
            const(n, [P, 1], True)
        for n, shape in LATER.items():
            const(n, list(shape))
        conv_phase(nc, g)
        linear_phase(nc, g)
        ffn_phase(nc, g)
        moe0_phase(nc, g, "m0a")
        attention_phase(nc, g, "a0", norm_eps=1.1920928955078125e-07, scale=HD ** -0.5, deflate=True)
        moe0_phase(nc, g, "m0b")
        attention_phase(nc, g, "a1", scale=HD ** -0.5, bias=True, causal=True, keep_max=True)
        moe1_phase(nc, g, "m1a")
        attention_phase(nc, g, "a2", norm_eps=1e-6, weights=True, bias=True, keep_max=True)
        moe1_phase(nc, g, "m1b", out)


LATER = {
    "Wq": (P, L, C), "Wkv": (P, L, 2 * C), "bq": (P, L), "bkv": (P, L, 2 * C), "lnA_g": (P, L), "lnA_b": (P, L),
    "head_mask": (P, C), "pair_turn": (P, C), "cosT": (P, NT, C), "sinT": (P, NT, C), "cosF": (P, N), "sinF": (P, N),
    "W1": (P, FF), "b1": (P, FJ), "W2": (P, FJ, C), "b2": (P, 1), "ln2_g": (P, C), "ln2_b": (P, C),
    "rw0": (P, E), "rb0": (P, E), "ew0": (P, E, C), "eb0": (E, C), "first": (P, E),
    "a0_wqkv": (P, 3 * C), "a0_wo": (P, C),
    "a1_wqkv": (P, 3 * C), "a1_wo": (P, C), "a1_bqkv": (P, 3 * C), "a1_bo": (P, C), "tri": (P, NT, N),
    "a2_wqkv": (P, 3 * C), "a2_wo": (P, C), "a2_bqkv": (P, 3 * C), "a2_bo": (P, C), "a2_wn": (P, 2 * C),
    "gamma": (P, 1), "beta": (P, 1), "rw1": (P, E), "rb1": (P, E), "W1e": (P, E, FF), "b1e": (P, E, FJ),
    "W2e": (P, E, FJ, C), "b2e": (E, C), "row3": (3 * E, E, P),
}


def tables():
    t = {}
    t["ident"] = np.eye(P, dtype=np.float32)
    c = np.arange(C)
    t["head_mask"] = (c[:, None] // HD == c[None, :] // HD).astype(np.float32)
    m = np.zeros((C, C), np.float32)
    m[0::2, 1::2] = -np.eye(C // 2)
    m[1::2, 0::2] = np.eye(C // 2)
    t["pair_turn"] = m
    inv = np.float32(1.0) / np.float32(10000.0) ** (np.arange(0, C, 2, dtype=np.float32) / np.float32(C))
    freqs = np.repeat(np.arange(N, dtype=np.float32)[:, None] * inv[None, :].astype(np.float32), 2, axis=-1)
    cos, sin = np.cos(freqs).astype(np.float32), np.sin(freqs).astype(np.float32)
    t["cosF"], t["sinF"] = np.ascontiguousarray(cos.T), np.ascontiguousarray(sin.T)
    sign = np.where(c % 2 == 0, -1.0, 1.0).astype(np.float32)
    t["cosT"] = np.ascontiguousarray(cos.reshape(NT, P, C).transpose(1, 0, 2))
    t["sinT"] = np.ascontiguousarray((sin * sign).reshape(NT, P, C).transpose(1, 0, 2))
    t["first"] = np.tile(np.arange(E, 0, -1, dtype=np.float32), (P, 1))
    q = np.arange(N).reshape(NT, P).transpose(1, 0)
    t["tri"] = np.where(np.arange(N)[None, None, :] <= q[:, :, None], 0.0, -3e38).astype(np.float32)
    row = np.zeros((E, E, P), np.float32)
    row[np.arange(E), np.arange(E)] = 1.0
    t["row3"] = np.concatenate([row] * 3)
    return t


def laid_out(i):
    a = {}

    def every(v):
        return np.tile(np.asarray(v).reshape(1, -1), (P, 1))

    def column(v):
        return np.asarray(v).reshape(-1, P).T

    p = "L0_attn_a_"
    a["x"] = i[p + "x"]
    a["conv1_w"] = i[p + "conv1_w"].reshape(P, MULT * TAPS)
    a["conv1_b"] = i[p + "conv1_b"].reshape(P, MULT)
    a["conv2_w"] = i[p + "conv2_w"].reshape(P, MULT * TAPS)
    for n in ("conv2_b", "ln0_g", "ln0_b", "b2"):
        a[n] = column(i[p + n])
    a["Wq"] = i[p + "Wq"].transpose(1, 0, 2)
    a["Wkv"] = np.concatenate([i[p + "Wk"], i[p + "Wv"]], axis=2).transpose(1, 0, 2)
    a["bkv"] = np.tile(np.concatenate([i[p + "bk"], i[p + "bv"]], axis=1)[None], (P, 1, 1))
    for n in ("bq", "lnA_g", "lnA_b"):
        a[n] = i[p + n].T
    a["W1"], a["b1"] = i[p + "W1"], column(i[p + "b1"])
    a["W2"] = i[p + "W2"].reshape(FJ, P, C).transpose(1, 0, 2)
    a["ln2_g"], a["ln2_b"] = every(i[p + "ln2_g"]), every(i[p + "ln2_b"])
    p = "L0_ffn_"
    a["rw0"], a["rb0"] = i[p + "router_w"].T, every(i[p + "router_b"])
    a["ew0"], a["eb0"] = i[p + "expert_w"].transpose(2, 0, 1), i[p + "expert_b"]
    a["a0_wqkv"], a["a0_wo"] = i["L0_attn_b_w_qkv"].T, i["L0_attn_b_w_proj"].T
    p = "L1_attn_a_"
    a["a1_wqkv"], a["a1_wo"] = i[p + "Wqkv"], i[p + "Wo"]
    a["a1_bqkv"], a["a1_bo"] = every(i[p + "bqkv"]), every(i[p + "bo"])
    p = "L1_attn_b_"
    a["a2_wqkv"], a["a2_wo"] = i[p + "Wqkv"].T, i[p + "Wo"].T
    a["a2_bqkv"], a["a2_bo"] = every(i[p + "bqkv"]), every(i[p + "bo"])
    a["a2_wn"] = every(np.concatenate([np.tile(i[p + "wq"], NH), np.tile(i[p + "wk"], NH)]))
    p = "L1_ffn_"
    a["gamma"], a["beta"] = column(i[p + "gamma"]), column(i[p + "beta"])
    a["rw1"], a["rb1"] = i[p + "Wr"], every(i[p + "br"])
    a["W1e"] = i[p + "W1"].transpose(1, 0, 2)
    a["b1e"] = i[p + "b1"].reshape(E, FJ, P).transpose(2, 0, 1)
    a["W2e"] = i[p + "W2"].reshape(E, FJ, P, C).transpose(2, 0, 1, 3)
    a["b2e"] = i[p + "b2"]
    return a


def kernel(**inputs):
    from concourse import bacc
    from concourse.bass_utils import run_bass_kernel_spmd

    nc = bacc.Bacc("TRN2", target_bir_lowering=False, num_devices=1)
    arrays = {**laid_out({k: np.asarray(v) for k, v in inputs.items()}), **tables()}
    arrays = {k: np.ascontiguousarray(v) for k, v in arrays.items()}
    d = {k: nc.dram_tensor("in_" + k, v.shape, mybir.dt.from_np(v.dtype), kind="ExternalInput").ap()
         for k, v in arrays.items()}
    out = nc.dram_tensor("out_x", (B, N, C), F32, kind="ExternalOutput").ap()
    build(nc, d, out)
    r = run_bass_kernel_spmd(nc, [{"in_" + k: v for k, v in arrays.items()}], core_ids=[0])
    return r.results[0]["out_x"]
```
